# Optimizing a Trainium2 kernel written in Bass

```python
import numpy as np
import jax
import jax.numpy as jnp

def _softmax(x, axis=-1):
    return jax.nn.softmax(x, axis=axis)

def _gelu(x):
    return jax.nn.gelu(x, approximate=True)

def _silu(x):
    return jax.nn.silu(x)

def _sigmoid(x):
    return jax.nn.sigmoid(x)

def _layernorm(x, axis=-1, eps=1e-05):
    m = jnp.mean(x, axis=axis, keepdims=True)
    v = jnp.var(x, axis=axis, keepdims=True)
    return (x - m) / jnp.sqrt(v + eps)

def _scatter_add(tgt, idx, src, axis=0):
    return tgt.at[idx].add(src)

def _segment_sum(src, seg, n):
    return jax.ops.segment_sum(src, seg, n)
kernel_name = 'mk_early_fusion_d1_tok_img256_r4_36b31c'

def setup_inputs(seed: int=0):
    np.random.seed(seed)
    _w = jnp.asarray

    def _rec_inputs():
        import jax
        import jax.numpy as jnp
        _rk = jax.random.key(seed)
        x = -0.000125008 + 0.999885 * jax.random.normal(jax.random.fold_in(_rk, 1), (64, 64, 64, 64), jnp.float32)
        txt = -0.000570488 + 0.251296 * jax.random.normal(jax.random.fold_in(_rk, 2), (64, 128, 64), jnp.float32)
        return (x, txt)
    x, txt = _rec_inputs()

    def _L0_tok_setup():
        import jax, jax.numpy as jnp
        import numpy as np
        B, C, H, W = (32, 64, 64, 64)
        STRIDE, HEADS = (4, 8)

        def _ln(x, w, b):
            mu = x.mean(-1, keepdims=True)
            var = ((x - mu) ** 2).mean(-1, keepdims=True)
            return (x - mu) * jax.lax.rsqrt(var + 1e-05) * w + b
        key = jax.random.key(seed)
        ks = jax.random.split(key, 4)
        return {'features': jax.random.normal(ks[0], (B, C, H, W), dtype=jnp.float32), 'ln_q_w': jnp.ones((C,), jnp.float32), 'ln_q_b': jnp.zeros((C,), jnp.float32), 'Wq': jax.random.normal(ks[1], (C, C), dtype=jnp.float32) * 0.02, 'ln_kv_w': jnp.ones((C,), jnp.float32), 'ln_kv_b': jnp.zeros((C,), jnp.float32), 'Wkv': jax.random.normal(ks[2], (2 * C, C), dtype=jnp.float32) * 0.02, 'proj_w': jax.random.normal(ks[3], (C, C), dtype=jnp.float32) * 0.02, 'proj_b': jnp.zeros((C,), jnp.float32), 'conv_stride': STRIDE, 'num_heads': HEADS}
    _L0_tok_all = _L0_tok_setup()
    _L0_tok_in = {k: v for k, v in _L0_tok_all.items() if k in ('ln_q_w', 'ln_q_b', 'Wq', 'ln_kv_w', 'ln_kv_b', 'Wkv', 'proj_w', 'proj_b')}
    del _L0_tok_all

    def _L0_attn_setup():
        import jax, jax.numpy as jnp
        import numpy as np
        import math
        N_SEQ, L_RES, D_MODEL = (128, 96, 64)
        N_HEAD, C_HEAD = (8, 32)
        EPS = 1e-05
        key = jax.random.key(seed)
        ks = jax.random.split(key, 8)
        s = 1.0 / math.sqrt(D_MODEL)
        return {'m': jax.random.normal(ks[0], (N_SEQ, L_RES, D_MODEL), jnp.float32), 'gamma': jnp.ones((D_MODEL,), jnp.float32), 'beta': jnp.zeros((D_MODEL,), jnp.float32), 'Wq': jax.random.normal(ks[1], (D_MODEL, N_HEAD * C_HEAD), jnp.float32) * s, 'Wk': jax.random.normal(ks[2], (D_MODEL, N_HEAD * C_HEAD), jnp.float32) * s, 'Wv': jax.random.normal(ks[3], (D_MODEL, N_HEAD * C_HEAD), jnp.float32) * s, 'Wg': jax.random.normal(ks[4], (D_MODEL, N_HEAD * C_HEAD), jnp.float32) * s, 'bg': jnp.zeros((N_HEAD * C_HEAD,), jnp.float32), 'Wo': jax.random.normal(ks[5], (N_HEAD * C_HEAD, D_MODEL), jnp.float32) * s, 'bo': jnp.zeros((D_MODEL,), jnp.float32)}
    _L0_attn_all = _L0_attn_setup()
    _L0_attn_in = {k: v for k, v in _L0_attn_all.items() if k in ('gamma', 'beta', 'Wq', 'Wk', 'Wv', 'Wg', 'bg', 'Wo', 'bo')}
    del _L0_attn_all

    def _L0_ffn_setup():
        import jax, jax.numpy as jnp
        import numpy as np
        B, T, IN_DIM = (64, 64, 64)
        HID, OUT_DIM = (128, 64)
        N_LAYERS, N_EXPERTS, N_SHARED = (2, 16, 1)
        key = jax.random.key(seed)
        ks = jax.random.split(key, 10)
        s = 0.02
        x = jax.random.normal(ks[0], (B, T, IN_DIM), dtype=jnp.float32)
        route_id = jax.random.randint(ks[1], (B,), 0, N_EXPERTS)
        Wi = jax.random.normal(ks[2], (HID, IN_DIM), dtype=jnp.float32) * s
        bi = jnp.zeros((HID,), dtype=jnp.float32)
        Wr = jax.random.normal(ks[3], (N_LAYERS, N_EXPERTS, HID, HID), dtype=jnp.float32) * s
        br = jax.random.normal(ks[4], (N_LAYERS, N_EXPERTS, HID), dtype=jnp.float32) * s
        Ws = jax.random.normal(ks[5], (N_LAYERS, N_SHARED, HID, HID), dtype=jnp.float32) * s
        bs = jax.random.normal(ks[6], (N_LAYERS, N_SHARED, HID), dtype=jnp.float32) * s
        Wo = jax.random.normal(ks[7], (OUT_DIM, HID), dtype=jnp.float32) * s
        bo = jnp.zeros((OUT_DIM,), dtype=jnp.float32)
        return {'x': x, 'route_id': route_id, 'Wi': Wi, 'bi': bi, 'Wr': Wr, 'br': br, 'Ws': Ws, 'bs': bs, 'Wo': Wo, 'bo': bo}
    _L0_ffn_all = _L0_ffn_setup()
    _L0_ffn_in = {k: v for k, v in _L0_ffn_all.items() if k in ('route_id', 'Wi', 'bi', 'Wr', 'br', 'Ws', 'bs', 'Wo', 'bo')}
    del _L0_ffn_all
    return {'x': x, 'txt': txt, 'L0_tok_ln_q_w': _L0_tok_in['ln_q_w'], 'L0_tok_ln_q_b': _L0_tok_in['ln_q_b'], 'L0_tok_Wq': _L0_tok_in['Wq'], 'L0_tok_ln_kv_w': _L0_tok_in['ln_kv_w'], 'L0_tok_ln_kv_b': _L0_tok_in['ln_kv_b'], 'L0_tok_Wkv': _L0_tok_in['Wkv'], 'L0_tok_proj_w': _L0_tok_in['proj_w'], 'L0_tok_proj_b': _L0_tok_in['proj_b'], 'L0_attn_gamma': _L0_attn_in['gamma'], 'L0_attn_beta': _L0_attn_in['beta'], 'L0_attn_Wq': _L0_attn_in['Wq'], 'L0_attn_Wk': _L0_attn_in['Wk'], 'L0_attn_Wv': _L0_attn_in['Wv'], 'L0_attn_Wg': _L0_attn_in['Wg'], 'L0_attn_bg': _L0_attn_in['bg'], 'L0_attn_Wo': _L0_attn_in['Wo'], 'L0_attn_bo': _L0_attn_in['bo'], 'L0_ffn_route_id': _L0_ffn_in['route_id'], 'L0_ffn_Wi': _L0_ffn_in['Wi'], 'L0_ffn_bi': _L0_ffn_in['bi'], 'L0_ffn_Wr': _L0_ffn_in['Wr'], 'L0_ffn_br': _L0_ffn_in['br'], 'L0_ffn_Ws': _L0_ffn_in['Ws'], 'L0_ffn_bs': _L0_ffn_in['bs'], 'L0_ffn_Wo': _L0_ffn_in['Wo'], 'L0_ffn_bo': _L0_ffn_in['bo']}

def reference(x, txt, L0_tok_ln_q_w, L0_tok_ln_q_b, L0_tok_Wq, L0_tok_ln_kv_w, L0_tok_ln_kv_b, L0_tok_Wkv, L0_tok_proj_w, L0_tok_proj_b, L0_attn_gamma, L0_attn_beta, L0_attn_Wq, L0_attn_Wk, L0_attn_Wv, L0_attn_Wg, L0_attn_bg, L0_attn_Wo, L0_attn_bo, L0_ffn_route_id, L0_ffn_Wi, L0_ffn_bi, L0_ffn_Wr, L0_ffn_br, L0_ffn_Ws, L0_ffn_bs, L0_ffn_Wo, L0_ffn_bo):
    import jax
    import jax.numpy as jnp

    def _L0_tok_ref(features, ln_q_w, ln_q_b, Wq, ln_kv_w, ln_kv_b, Wkv, proj_w, proj_b, conv_stride, num_heads):
        import jax, jax.numpy as jnp
        import numpy as np
        B, C, H, W = (32, 64, 64, 64)
        STRIDE, HEADS = (4, 8)

        def _ln(x, w, b):
            mu = x.mean(-1, keepdims=True)
            var = ((x - mu) ** 2).mean(-1, keepdims=True)
            return (x - mu) * jax.lax.rsqrt(var + 1e-05) * w + b
        s = conv_stride
        b, c, hh, ww = features.shape
        h, w = (hh // s, ww // s)
        hw, n, d = (h * w, s * s, c // num_heads)
        scale = c ** (-0.5)
        x = features.reshape(b, c, h, s, w, s)
        reduce_feats = x.mean((3, 5)).reshape(b, c, hw).transpose(0, 2, 1)
        unf = x.transpose(0, 1, 2, 4, 3, 5).reshape(b, c, hw, n).transpose(0, 2, 3, 1)
        q = _ln(reduce_feats, ln_q_w, ln_q_b) @ Wq.T
        q = q.reshape(b, hw, num_heads, d).transpose(0, 2, 1, 3)
        kv = _ln(unf, ln_kv_w, ln_kv_b) @ Wkv.T
        kv = kv.reshape(b, hw, n, 2, num_heads, d).transpose(3, 0, 4, 1, 2, 5)
        k, v = (kv[0], kv[1])
        attn = jax.nn.softmax(jnp.einsum('bhpd,bhpnd->bhpn', q * scale, k), axis=-1)
        aggre = jnp.einsum('bhpn,bhpnd->bhpd', attn, v)
        aggre = aggre.transpose(0, 2, 1, 3).reshape(b, hw, c)
        return reduce_feats + aggre @ proj_w.T + proj_b

    def _L0_attn_ref(m, gamma, beta, Wq, Wk, Wv, Wg, bg, Wo, bo):
        import jax, jax.numpy as jnp
        import numpy as np
        import math
        N_SEQ, L_RES, D_MODEL = (128, 96, 64)
        N_HEAD, C_HEAD = (8, 32)
        EPS = 1e-05
        N, L, D = m.shape
        H, C = (N_HEAD, C_HEAD)
        mu = jnp.mean(m, axis=-1, keepdims=True)
        var = jnp.mean(jnp.square(m - mu), axis=-1, keepdims=True)
        mn = (m - mu) * jax.lax.rsqrt(var + EPS) * gamma + beta
        q = (mn @ Wq).reshape(N, L, H, C)
        k = (mn @ Wk).reshape(N, L, H, C)
        v = (mn @ Wv).reshape(N, L, H, C)
        g = jax.nn.sigmoid(mn @ Wg + bg).reshape(N, L, H, C)
        scale = 1.0 / math.sqrt(C) / math.sqrt(L)
        att = jnp.einsum('slhc,tlhc->sth', q, k) * scale
        att = jax.nn.softmax(att, axis=1)
        o = jnp.einsum('sth,tlhc->slhc', att, v) * g
        return o.reshape(N, L, H * C) @ Wo + bo

    def _L0_ffn_ref(x, route_id, Wi, bi, Wr, br, Ws, bs, Wo, bo):
        import jax, jax.numpy as jnp
        import numpy as np
        B, T, IN_DIM = (64, 64, 64)
        HID, OUT_DIM = (128, 64)
        N_LAYERS, N_EXPERTS, N_SHARED = (2, 16, 1)
        flat = x.reshape(-1, x.shape[-1])
        n_tok = flat.shape[0]
        route = jnp.repeat(route_id, n_tok // route_id.shape[0])
        h = jax.nn.relu(flat @ Wi.T + bi)
        n_layers, n_experts = (Wr.shape[0], Wr.shape[1])
        for l in range(n_layers):
            shared = (jnp.einsum('nd,shd->snh', h, Ws[l]) + bs[l][:, None, :]).mean(axis=0)
            routed = jnp.zeros_like(h)
            for e in range(n_experts):
                ye = h @ Wr[l, e].T + br[l, e]
                routed = routed + jnp.where((route == e)[:, None], ye, 0.0)
            h = jax.nn.relu(shared + routed + h)
        out = h @ Wo.T + bo
        return out.reshape(*x.shape[:-1], out.shape[-1])
    h = _L0_tok_ref(x, L0_tok_ln_q_w, L0_tok_ln_q_b, L0_tok_Wq, L0_tok_ln_kv_w, L0_tok_ln_kv_b, L0_tok_Wkv, L0_tok_proj_w, L0_tok_proj_b, 4, 8)
    h = jnp.concatenate([h, txt], axis=1)
    h = h + _L0_attn_ref(_layernorm(h, axis=-1), L0_attn_gamma, L0_attn_beta, L0_attn_Wq, L0_attn_Wk, L0_attn_Wv, L0_attn_Wg, L0_attn_bg, L0_attn_Wo, L0_attn_bo)
    h = h + _L0_ffn_ref(_layernorm(h, axis=-1), L0_ffn_route_id, L0_ffn_Wi, L0_ffn_bi, L0_ffn_Wr, L0_ffn_br, L0_ffn_Ws, L0_ffn_bs, L0_ffn_Wo, L0_ffn_bo)
    return h

_drawn_inputs = setup_inputs


def setup_inputs(seed=0):
    import zlib

    import numpy as np

    out = dict(_drawn_inputs(seed))
    spreads = {'L0_tok_ln_q_w': (1.0, 0.6),
     'L0_tok_ln_q_b': (0.0, 2.0),
     'L0_tok_ln_kv_w': (1.0, 0.6),
     'L0_tok_ln_kv_b': (0.0, 0.365),
     'L0_tok_proj_b': (0.0, 0.1),
     'L0_attn_gamma': (1.0, 0.2),
     'L0_attn_beta': (0.0, 0.1),
     'L0_attn_bg': (0.0, 0.1),
     'L0_attn_bo': (0.0, 0.1),
     'L0_ffn_bi': (0.0, 0.1),
     'L0_ffn_bo': (0.0, 0.1)}
    factors = {'L0_tok_Wq': 56.409,
     'L0_ffn_Wr': 2.997,
     'L0_ffn_br': 5.31,
     'L0_ffn_Ws': 3.1,
     'L0_ffn_bs': 4.894}
    for name, (base, spread) in spreads.items():
        noise = np.random.default_rng([zlib.crc32(name.encode()), seed]).standard_normal(out[name].shape)
        drawn = base * np.exp(spread * noise) if base else spread * noise
        out[name] = jnp.asarray(drawn.astype(out[name].dtype))
    for name, factor in factors.items():
        out[name] = (out[name] * factor).astype(out[name].dtype)
    return out
```

```python
from contextlib import ExitStack

import numpy as np

import concourse.bass as bass
from concourse import mybir

ALU = mybir.AluOpType
ACT = mybir.ActivationFunctionType
AX = mybir.AxisListType.X
F32 = mybir.dt.float32
F16 = mybir.dt.float16
I32 = mybir.dt.int32

P = 128
EPS = 1e-5


def wait(eng, semaphore, value):
    if isinstance(value, int) and value <= 0:
        return
    eng.wait_ge(semaphore, value)


def spread(ap, axis, count):
    ap = ap.unsqueeze(axis)
    shape = list(ap.shape)
    shape[axis] = count
    return ap.to_broadcast(shape)


def minus_half(k, shape):
    ap = k.half[:]
    while len(ap.shape) < len(shape):
        ap = ap.unsqueeze(len(ap.shape))
    return ap.to_broadcast(shape)


class Memory:

    def __init__(self, nc, stack, prefix=""):
        self.nc, self.stack, self.prefix = nc, stack, prefix

    def sb(self, name, shape, dtype=F32):
        return self.stack.enter_context(self.nc.sbuf_tensor(self.prefix + name, shape, dtype))

    def ps(self, name, shape, dtype=F32):
        return self.stack.enter_context(self.nc.psum_tensor(self.prefix + name, shape, dtype))

    def sem(self, name):
        return self.stack.enter_context(self.nc.semaphore(self.prefix + name))


def setup_weights(nc, m, w, k):
    with ExitStack() as stack:
        t = Memory(nc, stack)
        C = 64
        wkv = t.sb("wkv", [P, C])
        wv = t.sb("wv", [C, C])
        wq2 = t.sb("wq2", [C, 2, C])
        proj2 = t.sb("proj2", [C, 2, C])
        kvw_row = t.sb("kvw_row", [P, C])
        kvb_row = t.sb("kvb_row", [C, C])
        wkv_sum = t.sb("wkv_sum", [P, 1])
        wkv2 = t.sb("wkv2", [P, 2, C])
        wvb = t.sb("wvb", [C, C])
        vbias = t.sb("vbias", [C, 1])
        ones = t.sb("ones", [C, P])
        vbias_cols = t.sb("vbias_cols", [C, P])
        projT = t.sb("projT", [C, C])
        projb_row = t.sb("projb_row", [P, C])
        qkvg = t.sb("qkvg", [P, 4, 256])
        qkvg_s = t.sb("qkvg_s", [P, 1024])
        wr = t.sb("wr", [P, 32, P])
        ws = t.sb("ws", [P, 2, P])
        brs = t.sb("brs", [32, P])
        bss = t.sb("bss", [32, P])
        wi = t.sb("wi", [P, 2, C])
        wi_s = t.sb("wi_s", [P, P])
        wo_nat = t.sb("wo_nat", [C, P])
        bank = [t.ps(f"sbank{i}", [P, 512]) for i in range(2)]
        loaded, zeroed, made = t.sem("loaded"), t.sem("zeroed"), t.sem("made")
        vec, product, moved = t.sem("vec"), t.sem("product"), t.sem("moved")
        n_loads = [0]

        with nc.Block() as block:
            @block.sync
            def _(sp):
                def load(dst, src):
                    sp.dma_start(dst, src).then_inc(loaded, 16)
                    n_loads[0] += 16
                load(wkv[:], w["tok_Wkv"])
                load(wv[:], w["tok_Wkv"][C:2 * C, :])
                for d in range(2):
                    load(wq2[:, d, :], w["tok_Wq"])
                    load(proj2[:, d, :], w["tok_proj_w"])
                    load(k.lnq_w[d * C:(d + 1) * C, :], w["tok_ln_q_w"].unsqueeze(1))
                    load(k.lnq_b[d * C:(d + 1) * C, :], w["tok_ln_q_b"].unsqueeze(1))
                    for n, name in enumerate(("attn_Wq", "attn_Wk", "attn_Wv", "attn_Wg")):
                        load(qkvg[d * C:(d + 1) * C, n, :], w[name])
                    load(wi[:, d, :], w["ffn_Wi"])
                load(kvw_row[:], w["tok_ln_kv_w"].partition_broadcast(P))
                load(kvb_row[:], w["tok_ln_kv_b"].partition_broadcast(C))
                load(projb_row[:], w["tok_proj_b"].partition_broadcast(P))
                load(k.gamma_row[:], w["attn_gamma"].partition_broadcast(P))
                load(k.beta_row[:], w["attn_beta"].partition_broadcast(P))
                load(k.bg_row[:], w["attn_bg"].partition_broadcast(P))
                load(k.attn_bo_row[:], w["attn_bo"].partition_broadcast(P))
                load(k.ffn_bo_row[:], w["ffn_bo"].partition_broadcast(P))
                load(k.attn_wo[:], w["attn_Wo"].rearrange("(k p) c -> p k c", k=2))
                load(wr[:], w["ffn_Wr"].rearrange("l e o i -> o (l e) i"))
                load(ws[:], w["ffn_Ws"].rearrange("l s o i -> o (l s) i"))
                load(brs[:], w["ffn_br"].rearrange("l e o -> (l e) o"))
                for n in range(2):
                    load(bss[16 * n:16 * n + 16, :], w["ffn_bs"][n, 0].partition_broadcast(16))
                load(wo_nat[:], w["ffn_Wo"])
                load(k.bi[:], w["ffn_bi"].unsqueeze(1))
                load(k.route[:], w["ffn_route_id"].unsqueeze(0))
                load(k.h_tok[:, :, 2, :], w["txt"].rearrange("b t c -> t b c"))

            @block.gpsimd
            def _(pool):
                clear = [(k.ident, 0.0), (k.parity, 0.0), (k.stat_sel, 0.0), (k.w_k, 0.0), (k.w_v, 0.0),
                         (k.w_q, 0.0), (k.w_proj, 0.0), (ones, 1.0), (k.half, -0.5)]
                for tile, value in clear:
                    pool.memset(tile[:], value).then_inc(zeroed, 1)
                pool.wait_ge(zeroed, len(clear))
                pool.affine_select(out=k.ident[:], in_=k.ident[:], compare_op=ALU.not_equal, fill=1.0,
                                   base=0, pattern=[[-1, P]], channel_multiplier=1).then_inc(made, 1)
                pool.wait_ge(made, 1)
                pool.tensor_copy(k.ident16[:], k.ident[:]).then_inc(made, 1)

            steps = [0]

            @block.vector
            def _(dve):
                def step(instruction):
                    steps[0] += 1
                    instruction.then_inc(vec, 1)
                    dve.wait_ge(vec, steps[0])
                dve.wait_ge(loaded, n_loads[0])
                dve.wait_ge(made, 2)
                for img in range(2):
                    step(dve.memset(k.stat_sel[64 * img:64 * img + 64, 30 + img:31 + img], 1.0 / C))
                step(dve.tensor_reduce(k.parity[:], k.ident[:].rearrange("p (t a) -> p a t", a=2), AX, ALU.add))
                step(dve.tensor_tensor(wkv[:], wkv[:], kvw_row[:], ALU.mult))
                step(dve.tensor_reduce(wkv_sum[:], wkv[:], AX, ALU.add))
                step(dve.tensor_scalar(wkv_sum[:], wkv_sum[:], -1.0 / C, None, ALU.mult))
                for d in range(2):
                    step(dve.tensor_scalar(wkv2[:, d, :], wkv[:], wkv_sum[:, 0:1], None, ALU.add))
                step(dve.tensor_tensor(wvb[:], wv[:], kvb_row[:], ALU.mult))
                step(dve.tensor_reduce(vbias[:], wvb[:], AX, ALU.add))
                step(dve.tensor_scalar(vbias_cols[:], ones[:], vbias[:, 0:1], None, ALU.mult))
                step(dve.tensor_scalar(qkvg_s[:], qkvg[:].rearrange("p a b -> p (a b)"), 64.0, None, ALU.mult))
                split = [(k.w_qk[:, 0].rearrange("p (g a h c) -> p a g h c", g=4, a=2, h=2)[:, n],
                          k.w_qk[:, 1].rearrange("p (g a h c) -> p a g h c", g=4, a=2, h=2)[:, n],
                          qkvg_s[:, 256 * n:256 * n + 256].rearrange("p (g h c) -> p g h c", g=4, h=2))
                         for n in range(2)]
                split.append((k.w_vg[:, 0], k.w_vg[:, 1], qkvg_s[:, 512:1024]))
                for hi, lo, whole in split:
                    step(dve.tensor_copy(hi, whole))
                    step(dve.tensor_tensor(lo, whole, hi, ALU.subtract))
                for n in range(2):
                    step(dve.tensor_tensor(ws[:, n, :], ws[:, n, :], k.ident[:], ALU.add))
                    for e in range(16):
                        step(dve.tensor_tensor(wr[:, 16 * n + e, :], wr[:, 16 * n + e, :], ws[:, n, :], ALU.add))
                step(dve.tensor_tensor(brs[:], brs[:], bss[:], ALU.add))

                def copy(n, dst, src, scale=1.0):
                    dve.wait_ge(product, n + 1)
                    dve.tensor_scalar(dst, src, scale, None, ALU.mult).then_inc(moved, 1)

                def halves(n, dst, src_of, scale=1.0):
                    dve.wait_ge(product, n + 1)
                    dve.tensor_scalar(dst[0:64, 0:64], src_of(0), scale, None, ALU.mult)
                    dve.tensor_scalar(dst[64:128, 64:128], src_of(1), scale, None, ALU.mult).then_inc(moved, 1)
                dve.wait_ge(product, 1)
                for j, dst in enumerate((k.w_k, k.w_v)):
                    dve.tensor_copy(dst[0:64, 0:64], bank[0][0:64, 64 * j:64 * j + 64])
                    last = dve.tensor_copy(dst[64:128, 64:128], bank[0][64:128, 64 * j:64 * j + 64])
                last.then_inc(moved, 1)
                halves(1, k.w_q, lambda i: bank[1][64 * i:64 * i + 64, 0:64], C ** -0.5)
                halves(2, k.w_proj, lambda i: bank[0][64 * i:64 * i + 64, 0:64])
                dve.wait_ge(product, 4)
                dve.tensor_copy(projT[:], bank[1][0:64, 0:64]).then_inc(moved, 1)
                dve.wait_ge(product, 5)
                for half in range(2):
                    last = dve.tensor_tensor(k.tok_const[:, 64 * half:64 * half + 64], bank[0][:, 0:64],
                                             projb_row[:], ALU.add)
                last.then_inc(moved, 1)
                dve.wait_ge(product, 6)
                dve.tensor_scalar(wi_s[:], bank[1][:, 0:128], 64.0, None, ALU.mult).then_inc(moved, 1)
                dve.wait_ge(moved, 6)
                step(dve.tensor_copy(k.wi_hi[:], wi_s[:]))
                step(dve.tensor_tensor(k.wi_lo[:], wi_s[:], k.wi_hi[:], ALU.subtract))
                copy(6, k.ffn_wo[:], bank[0][:, 0:64])
                copy(7, k.w_exp[:, :, P], bank[1][:, 0:32])
                for e in range(32):
                    copy(8 + e, k.w_exp[:, e, 0:P], bank[e % 2][:, 0:128])

            @block.tensor
            def _(pe):
                pe.wait_ge(made, 2)
                pe.wait_ge(vec, steps[0] - 2)
                n = [0]

                def start():
                    if n[0] >= 2:
                        pe.wait_ge(moved, n[0] - 1)
                    n[0] += 1
                    return bank[(n[0] - 1) % 2]
                pe.transpose(start()[:, 0:128], wkv2[:].rearrange("p a b -> p (a b)"), k.ident[:]).then_inc(product, 1)
                for src in (wq2, proj2, proj2):
                    pe.transpose(start()[:, 0:64], src[:].rearrange("p a b -> p (a b)"),
                                 k.ident[0:64, 0:64]).then_inc(product, 1)
                b = start()
                pe.wait_ge(moved, 4)
                pe.matmul(b[:, 0:64], vbias_cols[:], projT[:], start=True, stop=True).then_inc(product, 1)
                pe.transpose(start()[:, 0:128], wi[:].rearrange("p a b -> p (a b)"), k.ident[:]).then_inc(product, 1)
                pe.transpose(start()[:, 0:64], wo_nat[:], k.ident[0:64, 0:64]).then_inc(product, 1)
                pe.transpose(start()[:, 0:32], brs[:], k.ident[0:32, 0:32]).then_inc(product, 1)
                for e in range(32):
                    pe.transpose(start()[:, 0:128], wr[:, e, :], k.ident[:]).then_inc(product, 1)


def local_attention(nc, x, k):
    PAIRS, RING = 32, 4
    with ExitStack() as stack:
        t = Memory(nc, stack)
        x_pair = [t.sb(f"x_pair{i}", [P, 4, 1024]) for i in range(RING)]
        x_sq = t.sb("x_sq", [P, 4, 1024])
        f1, f2 = t.sb("f1", [P, 1024]), t.sb("f2", [P, 256, 2])
        feat_ch = [t.sb(f"feat_ch{i}", [P, 256]) for i in range(2)]
        stat_rows, stats = t.sb("stat_rows", [32, P, 4]), t.sb("stats", [P, 4, 32])
        mean_sq, var = t.sb("mean_sq", [P, 4, 16]), t.sb("var", [P, 4, 16])
        rstd = [t.sb(f"rstd{i}", [P, 2, 4, 4, 2]) for i in range(2)]
        feat = [t.sb(f"feat{i}", [P, 256]) for i in range(2)]
        feat_c = [t.sb(f"feat_c{i}", [P, 256]) for i in range(2)]
        q_sum, q_cent = t.sb("q_sum", [P, 4]), t.sb("q_cent", [P, 256])
        q_var, q_rstd = t.sb("q_var", [P, 4]), t.sb("q_rstd", [P, 4])
        q_hat, q_hatT = t.sb("q_hat", [P, 256]), t.sb("q_hatT", [P, 256])
        q = [t.sb(f"q{i}", [P, 2, P]) for i in range(2)]
        kq = t.sb("kq", [P, 16, P])
        q_sq = kq[:, 0:2].rearrange("p a b -> p (a b)")
        logit = [t.sb(f"logit{i}", [P, 256]) for i in range(2)]
        expo = [t.sb(f"expo{i}", [P, 256]) for i in range(2)]
        top = t.sb("top", [P, 16])
        weight = t.sb("weight", [P, 256])
        denom = t.sb("denom", [P, 16])
        inv = [t.sb(f"inv{i}", [P, 16]) for i in range(2)]
        wv = [t.sb(f"wv{i}", [P, 16, P]) for i in range(2)]
        agg = [t.sb(f"agg{i}", [P, P]) for i in range(2)]
        agg_n, aggT = t.sb("agg_n", [P, P]), t.sb("aggT", [P, P])
        k_bank = [t.ps(f"k_bank{i}", [P, 4, P]) for i in range(2)]
        v_bank = [t.ps(f"v_bank{i}", [P, 4, P]) for i in range(2)]
        s_bank, q_bank, a_bank = t.ps("s_bank", [P, 512]), t.ps("q_bank", [P, 512]), t.ps("a_bank", [P, 512])

        x_loaded = [t.sem(f"x_loaded{i}") for i in range(RING)]
        squared, feat_part, feat_done = t.sem("squared"), t.sem("feat_part"), t.sem("feat_done")
        stat_mm, stat_copied, stat_turned = t.sem("stat_mm"), t.sem("stat_copied"), t.sem("stat_turned")
        stats_ready, mean_sq_ready = t.sem("stats_ready"), t.sem("mean_sq_ready")
        var_ready, var_eps, rstd_ready = t.sem("var_ready"), t.sem("var_eps"), t.sem("rstd_ready")
        feat_turned, feat_ready = t.sem("feat_turned"), t.sem("feat_ready")
        q_summed, q_centred, q_squared = t.sem("q_summed"), t.sem("q_centred"), t.sem("q_squared")
        q_var_ready, q_var_eps, q_rstd_ready = t.sem("q_var_ready"), t.sem("q_var_eps"), t.sem("q_rstd_ready")
        q_hat_ready, q_turned, q_hatT_ready = t.sem("q_hat_ready"), t.sem("q_turned"), t.sem("q_hatT_ready")
        q_mm, q_ready, feat_c_ready = t.sem("q_mm"), t.sem("q_ready"), t.sem("feat_c_ready")
        k_mm, kq_done, logits_raw, logits_ready = t.sem("k_mm"), t.sem("kq_done"), t.sem("logits_raw"), t.sem("logits_ready")
        top_ready, shifted, exp_ready = t.sem("top_ready"), t.sem("shifted"), t.sem("exp_ready")
        weight_ready, denom_ready, inv_ready = t.sem("weight_ready"), t.sem("denom_ready"), t.sem("inv_ready")
        v_mm, wv_done, agg_part, agg_ready = t.sem("v_mm"), t.sem("wv_done"), t.sem("agg_part"), t.sem("agg_ready")
        agg_n_ready, agg_turned, aggT_ready = t.sem("agg_n_ready"), t.sem("agg_turned"), t.sem("aggT_ready")
        proj_mm, h_ready = t.sem("proj_mm"), t.sem("h_ready")

        def over_pairs(eng, first, body, tail):
            first()
            for slot in range(RING):
                body(slot, slot)
            with eng.Fori(1, PAIRS // RING - 1) as g:
                for slot in range(RING):
                    body(g * RING + slot, slot)
            for slot in range(RING):
                body(PAIRS - RING + slot, slot)
            tail()

        def known(r, least, most):
            return not isinstance(r, int) or least <= r <= most

        with nc.Block() as block:
            @block.sync
            def _(sp):
                def load(r, slot):
                    if known(r, RING, PAIRS):
                        sp.wait_ge(feat_turned, r - 1)
                    pair = x.rearrange("(r b) c (h i) w -> r (b c) i h w", b=2, i=4)[r]
                    for i in range(4):
                        sp.dma_start(x_pair[slot][:, i, :].rearrange("p (h w) -> p h w", h=16),
                                     pair[:, i]).then_inc(x_loaded[slot], 16)
                over_pairs(sp, lambda: None, load, lambda: None)

            def loaded(eng, r, slot):
                if isinstance(r, int):
                    eng.wait_ge(x_loaded[slot], 64 * (r // RING + 1))
                else:
                    eng.wait_ge(x_loaded[slot], (r - slot) * (64 // RING) + 64)

            @block.gpsimd
            def _(pool):
                def features(r, slot):
                    loaded(pool, r, slot)
                    xp = x_pair[slot]
                    pool.tensor_tensor(f1[:], xp[:, 0, :], xp[:, 1, :], ALU.add).then_inc(feat_part, 1)
                    for i in (2, 3):
                        pool.wait_ge(feat_part, 4 * r + i - 1)
                        pool.tensor_tensor(f1[:], f1[:], xp[:, i, :], ALU.add).then_inc(feat_part, 1)
                    pool.wait_ge(feat_part, 4 * r + 3)
                    f = f1[:].rearrange("p (t j) -> p t j", j=4)
                    pool.tensor_tensor(f2[:], f[:, :, 0:2], f[:, :, 2:4], ALU.add).then_inc(feat_part, 1)
                    pool.wait_ge(feat_part, 4 * r + 4)
                    wait(pool, feat_turned, r - 1)
                    pool.tensor_tensor(feat_ch[slot % 2][:], f2[:, :, 0], f2[:, :, 1], ALU.add).then_inc(feat_done, 1)

                def norms(r, slot):
                    pool.wait_ge(var_eps, r + 1)
                    wait(pool, weight_ready, 2 * (r - 2) + 2)
                    pool.tensor_tensor(rstd[slot % 2][:].rearrange("p f i j m -> p j (f i) m"),
                                       var[:].rearrange("p j (f m) -> p j f m", m=2),
                                       minus_half(k, [P, 4, 8, 2]), ALU.pow).then_inc(rstd_ready, 1)
                    pool.wait_ge(q_var_eps, r + 1)
                    pool.tensor_tensor(q_rstd[:], q_var[:], minus_half(k, [P, 4]), ALU.pow).then_inc(q_rstd_ready, 1)

                def sum_pixels(u, par):
                    wait(pool, wv_done, 4 * u + 4)
                    w = wv[par]
                    for n, half in enumerate((8, 4, 2)):
                        pool.tensor_tensor(w[:, 0:half], w[:, 0:half], w[:, half:2 * half], ALU.add).then_inc(agg_part, 1)
                        pool.wait_ge(agg_part, 3 * u + n + 1)
                    wait(pool, agg_n_ready, u - 1)
                    pool.tensor_tensor(agg[par][:], w[:, 0], w[:, 1], ALU.add).then_inc(agg_ready, 1)

                def first():
                    features(0, 0)
                    norms(0, 0)

                def body(r, slot):
                    if known(r, 0, PAIRS - 2):
                        features(r + 1, (slot + 1) % RING)
                    if known(r, 1, PAIRS):
                        sum_pixels(2 * r - 1, 1)
                    if known(r, 0, PAIRS - 2):
                        norms(r + 1, (slot + 1) % RING)
                    sum_pixels(2 * r, 0)
                over_pairs(pool, first, body, lambda: sum_pixels(2 * PAIRS - 1, 1))

            @block.scalar
            def _(act):
                def square(r, slot):
                    loaded(act, r, slot)
                    wait(act, stat_mm, r)
                    act.activation(x_sq[:], x_pair[slot][:], ACT.Square).then_inc(squared, 1)

                def copy(dst, src, after, count, done, scale=1.0):
                    act.wait_ge(after, count)
                    act.activation(dst, src, ACT.Copy, scale=scale).then_inc(done, 1)

                def prepare_a(r, slot):
                    copy(stat_rows[:].rearrange("p a b -> p (a b)"), s_bank[0:32, :], stat_mm, r + 1, stat_copied)
                    copy(stats[:].rearrange("p a b -> p (a b)"), s_bank[:, 0:128], stat_turned, r + 1, stats_ready)
                    wait(act, feat_c_ready, r - 1)
                    copy(feat[slot % 2][:], q_bank[:, 0:256], feat_turned, r + 1, feat_ready, 1.0 / 16)

                def prepare_b(r, slot):
                    act.wait_ge(q_turned, r + 1)
                    act.activation(q_hatT[:], q_bank[:, 256:512], ACT.Identity, bias=k.lnq_b[:, 0:1],
                                   scale=k.lnq_w[:, 0:1]).then_inc(q_hatT_ready, 1)
                    wait(act, kq_done, 8 * (r - 2) + 8)
                    copy(q[slot % 2][:].rearrange("p a b -> p (a b)"), q_bank[:, 0:256], q_mm, r + 1, q_ready)

                def exponential(u, par):
                    act.wait_ge(shifted, u + 1)
                    act.activation(expo[par][:], logit[par][:], ACT.Exp).then_inc(exp_ready, 1)

                def turned(u):
                    copy(aggT[:], a_bank[:, 0:128], agg_turned, u + 1, aggT_ready)

                def first():
                    square(0, 0)
                    prepare_a(0, 0)
                    prepare_b(0, 0)

                def body(r, slot):
                    more = known(r, 0, PAIRS - 2)
                    nxt = (slot + 1) % RING
                    if more:
                        square(r + 1, nxt)
                    exponential(2 * r, 0)
                    if known(r, 1, PAIRS):
                        turned(2 * r - 2)
                    if more:
                        prepare_a(r + 1, nxt)
                    exponential(2 * r + 1, 1)
                    if known(r, 1, PAIRS):
                        turned(2 * r - 1)
                    if more:
                        prepare_b(r + 1, nxt)

                def tail():
                    turned(2 * PAIRS - 2)
                    turned(2 * PAIRS - 1)
                over_pairs(act, first, body, tail)

            @block.tensor
            def _(pe):
                def pixel_stats(r, slot):
                    loaded(pe, r, slot)
                    wait(pe, stats_ready, r)
                    n = 0
                    for kind, src in enumerate((x_pair[slot], x_sq)):
                        if kind:
                            pe.wait_ge(squared, r + 1)
                        for half in range(2):
                            for i in range(4):
                                row = kind * 16 + (half * 4 + i) * 2
                                last = pe.matmul(s_bank[0:32, :], k.stat_sel[:, 30 - row:62 - row],
                                                 src[:, i, 512 * half:512 * half + 512], start=(n == 0), stop=(n == 15))
                                n += 1
                    last.then_inc(stat_mm, 1)

                def prepare_a(r, slot):
                    pe.wait_ge(stat_copied, r + 1)
                    pe.wait_ge(feat_done, r + 1)
                    wait(pe, q_ready, r)
                    for half in range(2):
                        last = pe.transpose(q_bank[:, P * half:P * half + P],
                                            feat_ch[slot % 2][:, P * half:P * half + P], k.ident[:])
                    last.then_inc(feat_turned, 1)
                    for j in range(4):
                        last = pe.transpose(s_bank[:, 32 * j:32 * j + 32], stat_rows[:, :, j], k.ident[0:32, 0:32])
                    last.then_inc(stat_turned, 1)

                def prepare_b(r, slot):
                    pe.wait_ge(q_hat_ready, r + 1)
                    for half in range(2):
                        last = pe.transpose(q_bank[:, 256 + P * half:256 + P * half + P],
                                            q_hat[:, P * half:P * half + P], k.ident[:])
                    last.then_inc(q_turned, 1)

                def queries(r, slot):
                    pe.wait_ge(q_hatT_ready, r + 1)
                    for half in range(2):
                        last = pe.matmul(q_bank[:, P * half:P * half + P], q_hatT[:, P * half:P * half + P],
                                         k.w_q[:], start=True, stop=True)
                    last.then_inc(q_mm, 1)

                def project_pixels(u, slot, half, banks, weights, done, used):
                    for i in range(4):
                        wait(pe, used, 4 * u + i - 1)
                        pixels = x_pair[slot][:, i, 512 * half:512 * half + 512].rearrange("p (t j) -> p j t", j=4)
                        for j in range(4):
                            last = pe.matmul(banks[i % 2][:, j, :], pixels[:, j, :], weights[:], start=True, stop=True)
                        last.then_inc(done, 1)

                def turn(u):
                    pe.wait_ge(agg_n_ready, u + 1)
                    wait(pe, h_ready, u)
                    pe.transpose(a_bank[:, 0:P], agg_n[:], k.ident[:]).then_inc(agg_turned, 1)

                def project(u):
                    pe.wait_ge(aggT_ready, u + 1)
                    pe.matmul(a_bank[:, P:2 * P], aggT[:], k.w_proj[:], start=True, stop=True).then_inc(proj_mm, 1)

                def first():
                    pixel_stats(0, 0)
                    prepare_a(0, 0)
                    prepare_b(0, 0)
                    queries(0, 0)

                def body(r, slot):
                    more, nxt = known(r, 0, PAIRS - 2), (slot + 1) % RING
                    before = known(r, 1, PAIRS)
                    project_pixels(2 * r, slot, 0, k_bank, k.w_k, k_mm, kq_done)
                    if before:
                        turn(2 * r - 2)
                    if more:
                        pixel_stats(r + 1, nxt)
                    if before:
                        project_pixels(2 * r - 1, (slot - 1) % RING, 1, v_bank, k.w_v, v_mm, wv_done)
                        project(2 * r - 2)
                    if more:
                        prepare_a(r + 1, nxt)
                    project_pixels(2 * r + 1, slot, 1, k_bank, k.w_k, k_mm, kq_done)
                    if before:
                        turn(2 * r - 1)
                    if more:
                        prepare_b(r + 1, nxt)
                    project_pixels(2 * r, slot, 0, v_bank, k.w_v, v_mm, wv_done)
                    if before:
                        project(2 * r - 1)
                    if more:
                        queries(r + 1, nxt)

                def tail():
                    project_pixels(2 * PAIRS - 1, RING - 1, 1, v_bank, k.w_v, v_mm, wv_done)
                    for u in (2 * PAIRS - 2, 2 * PAIRS - 1):
                        turn(u)
                        project(u)
                over_pairs(pe, first, body, tail)

            @block.vector
            def _(dve):
                def pixel_variance(r, slot):
                    dve.wait_ge(stats_ready, r + 1)
                    dve.tensor_tensor(mean_sq[:], stats[:, :, 0:16], stats[:, :, 0:16], ALU.mult).then_inc(mean_sq_ready, 1)
                    dve.wait_ge(mean_sq_ready, r + 1)
                    wait(dve, rstd_ready, r)
                    dve.tensor_tensor(var[:], stats[:, :, 16:32], mean_sq[:], ALU.subtract).then_inc(var_ready, 1)
                    dve.wait_ge(var_ready, r + 1)
                    dve.tensor_scalar(var[:], var[:], 0.0, EPS, ALU.max, ALU.add).then_inc(var_eps, 1)

                def normalise_means(r, slot):
                    f = feat[slot % 2][:].rearrange("p (g c) -> p g c", g=4)
                    cent = q_cent[:].rearrange("p (g c) -> p g c", g=4)
                    dve.wait_ge(feat_ready, r + 1)
                    dve.tensor_reduce(q_sum[:], f, AX, ALU.add).then_inc(q_summed, 1)
                    dve.wait_ge(q_summed, r + 1)
                    dve.scalar_tensor_tensor(out=cent, in0=spread(q_sum[:], 2, 64), scalar=-1.0 / 64, in1=f,
                                             op0=ALU.mult, op1=ALU.add).then_inc(q_centred, 1)
                    dve.wait_ge(q_centred, r + 1)
                    dve.tensor_tensor(q_sq, q_cent[:], q_cent[:], ALU.mult).then_inc(q_squared, 1)
                    dve.wait_ge(q_squared, r + 1)
                    wait(dve, q_rstd_ready, r)
                    dve.tensor_reduce(q_var[:], q_sq.rearrange("p (g c) -> p g c", g=4), AX, ALU.add).then_inc(q_var_ready, 1)
                    dve.wait_ge(q_var_ready, r + 1)
                    dve.tensor_scalar(q_var[:], q_var[:], 1.0 / 64, EPS, ALU.mult, ALU.add).then_inc(q_var_eps, 1)

                def residual(r, slot):
                    wait(dve, h_ready, 2 * (r - 2) + 2)
                    dve.tensor_tensor(feat_c[slot % 2][:].rearrange("p (f m) -> p f m", f=2),
                                      feat[slot % 2][:].rearrange("p (f m) -> p f m", f=2),
                                      spread(k.tok_const[:], 1, 2), ALU.add).then_inc(feat_c_ready, 1)

                def scale_means(r, slot):
                    dve.wait_ge(q_rstd_ready, r + 1)
                    wait(dve, q_turned, r)
                    dve.tensor_tensor(q_hat[:].rearrange("p (g c) -> p g c", g=4),
                                      q_cent[:].rearrange("p (g c) -> p g c", g=4),
                                      spread(q_rstd[:], 2, 64), ALU.mult).then_inc(q_hat_ready, 1)

                def logits(u, r, slot, half):
                    par = half
                    dve.wait_ge(q_ready, r + 1)
                    for i in range(4):
                        dve.wait_ge(k_mm, 4 * u + i + 1)
                        dve.tensor_tensor(kq[:, 4 * i:4 * i + 4, :], k_bank[i % 2][:],
                                          spread(q[slot % 2][:, half, :], 1, 4), ALU.mult).then_inc(kq_done, 1)
                    dve.wait_ge(kq_done, 4 * u + 4)
                    wait(dve, exp_ready, u - 1)
                    dve.tensor_reduce(logit[par][:], kq[:].rearrange("p n (h d) -> p (n h) d", d=8), AX, ALU.add).then_inc(logits_raw, 1)
                    dve.wait_ge(logits_raw, u + 1)
                    dve.wait_ge(rstd_ready, r + 1)
                    rs = rstd[slot % 2][:, half].rearrange("p i j m -> p (i j m)")
                    dve.tensor_tensor(logit[par][:].rearrange("p (a h) -> p a h", h=8),
                                      logit[par][:].rearrange("p (a h) -> p a h", h=8),
                                      spread(rs, 2, 8), ALU.mult).then_inc(logits_ready, 1)
                    dve.wait_ge(logits_ready, u + 1)
                    dve.tensor_reduce(top[:], logit[par][:].rearrange("p (n g) -> p g n", g=16), AX, ALU.max).then_inc(top_ready, 1)
                    dve.wait_ge(top_ready, u + 1)
                    dve.tensor_tensor(logit[par][:].rearrange("p (n g) -> p n g", g=16),
                                      logit[par][:].rearrange("p (n g) -> p n g", g=16),
                                      spread(top[:], 1, 16), ALU.subtract).then_inc(shifted, 1)

                def weigh_values(u, slot, half):
                    par = half
                    dve.wait_ge(exp_ready, u + 1)
                    wait(dve, wv_done, 4 * u)
                    rs = rstd[slot % 2][:, half].rearrange("p i j m -> p (i j m)")
                    dve.tensor_tensor(weight[:].rearrange("p (a h) -> p a h", h=8),
                                      expo[par][:].rearrange("p (a h) -> p a h", h=8),
                                      spread(rs, 2, 8), ALU.mult).then_inc(weight_ready, 1)
                    dve.tensor_reduce(denom[:], expo[par][:].rearrange("p (n g) -> p g n", g=16), AX, ALU.add).then_inc(denom_ready, 1)
                    dve.wait_ge(denom_ready, u + 1)
                    dve.reciprocal(inv[par][:], denom[:]).then_inc(inv_ready, 1)
                    dve.wait_ge(weight_ready, u + 1)
                    wait(dve, agg_ready, u - 1)
                    for i in range(4):
                        dve.wait_ge(v_mm, 4 * u + i + 1)
                        dve.tensor_tensor(wv[par][:, 4 * i:4 * i + 4, :].rearrange("p n (h d) -> p (n h) d", d=8),
                                          v_bank[i % 2][:].rearrange("p n (h d) -> p (n h) d", d=8),
                                          spread(weight[:, 64 * i:64 * i + 64], 2, 8), ALU.mult).then_inc(wv_done, 1)

                def normalise(u, half):
                    dve.wait_ge(agg_ready, u + 1)
                    dve.wait_ge(inv_ready, u + 1)
                    wait(dve, agg_turned, u)
                    dve.tensor_tensor(agg_n[:].rearrange("p (g d) -> p g d", d=8),
                                      agg[half][:].rearrange("p (g d) -> p g d", d=8),
                                      spread(inv[half][:], 2, 8), ALU.mult).then_inc(agg_n_ready, 1)

                def finish(u, r, slot, half):
                    dve.wait_ge(proj_mm, u + 1)
                    dve.wait_ge(feat_c_ready, r + 1)
                    dve.tensor_tensor(k.h_tok[:, bass.ds(2 * r, 2), half, :],
                                      a_bank[:, P:2 * P].rearrange("p (m c) -> p m c", m=2),
                                      feat_c[slot % 2][:, P * half:P * half + P].rearrange("p (m c) -> p m c", m=2),
                                      ALU.add).then_inc(h_ready, 1)

                def first():
                    pixel_variance(0, 0)
                    normalise_means(0, 0)
                    scale_means(0, 0)
                    residual(0, 0)

                def body(r, slot):
                    more, nxt, prev = known(r, 0, PAIRS - 2), (slot + 1) % RING, (slot - 1) % RING
                    before = known(r, 1, PAIRS)
                    logits(2 * r, r, slot, 0)
                    if before:
                        normalise(2 * r - 2, 0)
                        weigh_values(2 * r - 1, prev, 1)
                        finish(2 * r - 2, r - 1, prev, 0)
                    if more:
                        pixel_variance(r + 1, nxt)
                        normalise_means(r + 1, nxt)
                    logits(2 * r + 1, r, slot, 1)
                    if more:
                        scale_means(r + 1, nxt)
                    if before:
                        normalise(2 * r - 1, 1)
                    weigh_values(2 * r, slot, 0)
                    if before:
                        finish(2 * r - 1, r - 1, prev, 1)
                    if more:
                        residual(r + 1, nxt)

                def tail():
                    last = PAIRS - 1
                    weigh_values(2 * last + 1, RING - 1, 1)
                    for half in range(2):
                        normalise(2 * last + half, half)
                        finish(2 * last + half, last, RING - 1, half)
                over_pairs(dve, first, body, tail)


def centred_and_scaled(t, name, groups):
    return dict(sum=t.sb(name + "_sum", [P, groups]), cent=t.sb(name + "_cent", [P, groups, 64]),
                sq=t.sb(name + "_sq", [P, groups, 64]), var=t.sb(name + "_var", [P, groups]),
                split=[t.sb(f"{name}_split{i}", [P, groups, 2, 64], F16) for i in range(2)])


def normalise_and_turn(nc, source_of, target_of, chunks, groups, var_scale, var_add, k, affine):
    banks = groups // 8
    with ExitStack() as stack:
        t = Memory(nc, stack, "attn_" if affine else "ffn_")
        b = centred_and_scaled(t, "norm", groups)
        bank = [t.ps(f"turn{i}", [P, 8, P], F16) for i in range(2 * banks)]
        summed, centred, squared, varied = t.sem("summed"), t.sem("centred"), t.sem("squared"), t.sem("varied")
        var_added, rooted, scaled = t.sem("var_added"), t.sem("rooted"), t.sem("scaled")
        split_hi, split_ready, turned, moved = t.sem("split_hi"), t.sem("split_ready"), t.sem("turned"), t.sem("moved")
        passes = 3 if affine else 1

        def over_chunks(eng, body):
            for c in range(2):
                body(c, c)
            with eng.Fori(1, chunks // 2) as g:
                for c in range(2):
                    body(2 * g + c, c)

        with nc.Block() as block:
            @block.vector
            def _(dve):
                def body(n, par):
                    h = source_of(n)
                    dve.tensor_reduce(b["sum"][:], h, AX, ALU.add).then_inc(summed, 1)
                    dve.wait_ge(summed, n + 1)
                    wait(dve, squared, n)
                    dve.scalar_tensor_tensor(out=b["cent"][:], in0=spread(b["sum"][:], 2, 64), scalar=-1.0 / 64,
                                             in1=h, op0=ALU.mult, op1=ALU.add).then_inc(centred, 1)
                    dve.wait_ge(squared, n + 1)
                    wait(dve, rooted, n)
                    dve.tensor_reduce(b["var"][:], b["sq"][:], AX, ALU.add).then_inc(varied, 1)
                    dve.wait_ge(varied, n + 1)
                    dve.tensor_scalar(b["var"][:], b["var"][:], var_scale, var_add, ALU.mult, ALU.add).then_inc(var_added, 1)
                    dve.wait_ge(rooted, n + 1)
                    dve.tensor_tensor(b["cent"][:], b["cent"][:], spread(b["var"][:], 2, 64), ALU.mult).then_inc(scaled, 1)
                    dve.wait_ge(scaled, passes * n + 1)
                    if affine:
                        dve.tensor_tensor(b["cent"][:], b["cent"][:], spread(k.gamma_row[:], 1, groups), ALU.mult).then_inc(scaled, 1)
                        dve.wait_ge(scaled, passes * n + 2)
                        dve.tensor_tensor(b["cent"][:], b["cent"][:], spread(k.beta_row[:], 1, groups), ALU.add).then_inc(scaled, 1)
                        dve.wait_ge(scaled, passes * n + 3)
                    wait(dve, turned, banks * (n - 1))
                    s = b["split"][par]
                    dve.tensor_copy(s[:, :, 0, :], b["cent"][:]).then_inc(split_hi, 1)
                    dve.wait_ge(split_hi, n + 1)
                    dve.tensor_tensor(s[:, :, 1, :], b["cent"][:], s[:, :, 0, :], ALU.subtract).then_inc(split_ready, 1)
                over_chunks(dve, body)

            @block.gpsimd
            def _(pool):
                def body(n, par):
                    pool.wait_ge(var_added, n + 1)
                    pool.tensor_tensor(b["var"][:], b["var"][:], minus_half(k, [P, groups]), ALU.pow).then_inc(rooted, 1)
                over_chunks(pool, body)

            @block.tensor
            def _(pe):
                def body(n, par):
                    pe.wait_ge(split_ready, n + 1)
                    for a in range(banks):
                        wait(pe, moved, banks * (n - 2) + a + 1)
                        for i in range(8):
                            last = pe.transpose(bank[par * banks + a][:, i, :],
                                                b["split"][par][:, 8 * a + i].rearrange("p s c -> p (s c)"), k.ident16[:])
                        last.then_inc(turned, 1)
                over_chunks(pe, body)

            @block.scalar
            def _(act):
                def body(n, par):
                    act.wait_ge(centred, n + 1)
                    wait(act, varied, n)
                    act.activation(b["sq"][:], b["cent"][:], ACT.Square).then_inc(squared, 1)
                    if isinstance(n, int) and n == 0:
                        return
                    move(n - 1, 1 - par)

                def move(n, par):
                    for a in range(banks):
                        act.wait_ge(turned, banks * n + a + 1)
                        act.activation(target_of(n, a), bank[par * banks + a][:], ACT.Copy).then_inc(moved, 1)
                over_chunks(act, body)
                move(chunks - 1, 1)


def tied_scores(nc, zT, h_half, h_source, k):
    with ExitStack() as stack:
        t = Memory(nc, stack)
        qk = [t.sb(f"qk{i}", [P, 2, 2, 64, 32]) for i in range(2)]
        score, top, denom, inv = t.sb("score", [P, 4, 64]), t.sb("stop", [P, 4]), t.sb("sdenom", [P, 4]), t.sb("sinv", [P, 4])
        att2 = t.sb("att2", [P, 4, 64, 2])
        bank = [t.ps(f"qk_bank{i}", [P, 4, 2, 2, 32]) for i in range(4)]
        s_bank = t.ps("score_bank", [P, 4, 2, 64])
        t_bank = [t.ps(f"att_bank{i}", [P, 512]) for i in range(2)]
        projected, moved_a, moved_v, summed = t.sem("projected"), t.sem("moved_a"), t.sem("moved_v"), t.sem("summed")
        vec, exp_ready, att_turned, att_used = t.sem("vec"), t.sem("exp_ready"), t.sem("att_turned"), t.sem("att_used")
        h_loaded = t.sem("h_loaded")
        UNITS = [(g, j) for g in range(4) for j in range(3)]

        def move(eng, u, a, done, op):
            eng.wait_ge(projected, 16 * u + a + 1)
            wait(eng, summed, u - 1)
            for kind in range(2):
                last = op(qk[u % 2][:, kind, :, 4 * a:4 * a + 4, :],
                          bank[a % 4][:, :, kind].rearrange("p s h c -> p h s c"))
            last.then_inc(done, 1)

        with nc.Block() as block:
            @block.sync
            def _(sp):
                sp.dma_start(h_half, h_source).then_inc(h_loaded, 16)
                sp.wait_ge(h_loaded, 16)

            @block.tensor
            def _(pe):
                def project(u, g, j):
                    for s in range(64):
                        a = s // 4
                        if s % 4 == 0:
                            n = 16 * u + a - 4
                            wait(pe, moved_a if a % 2 == 0 else moved_v, n // 2 + 1 if n >= 0 else 0)
                        for part in range(2):
                            last = pe.matmul(bank[a % 4][:, s % 4].rearrange("p k h c -> p (k h c)"),
                                             zT[:, s, P * j:P * j + P], k.w_qk[:, part, P * g:P * g + P],
                                             start=(part == 0), stop=(part == 1))
                        if s % 4 == 3:
                            last.then_inc(projected, 1)

                def score_sums(u, g, j):
                    pe.wait_ge(moved_a, 8 * u + 8)
                    pe.wait_ge(moved_v, 8 * u + 8)
                    q = qk[u % 2][:].rearrange("p k h s c -> p k (h s) c")
                    for c in range(32):
                        last = pe.matmul(s_bank[:, g].rearrange("p h t -> p (h t)"), q[:, 0, :, c], q[:, 1, :, c],
                                         start=(j == 0 and c == 0), stop=(j == 2 and c == 31))
                    last.then_inc(summed, 1)
                for u, (g, j) in enumerate(UNITS):
                    project(u, g, j)
                    if u:
                        score_sums(u - 1, *UNITS[u - 1])
                score_sums(len(UNITS) - 1, *UNITS[-1])
                pe.wait_ge(vec, 6)
                for g in range(4):
                    wait(pe, att_used, g - 1)
                    pe.transpose(t_bank[g % 2][:, 0:P], att2[:, g].rearrange("p t a -> p (t a)"), k.ident[:]).then_inc(att_turned, 1)

            @block.scalar
            def _(act):
                for u in range(len(UNITS)):
                    for a in range(0, 16, 2):
                        move(act, u, a, moved_a, lambda o, i: act.activation(o, i, ACT.Copy, scale=1.0 / 64))
                act.wait_ge(vec, 3)
                act.activation(score[:], score[:], ACT.Exp).then_inc(exp_ready, 1)

            @block.vector
            def _(dve):
                for u in range(len(UNITS)):
                    for a in range(1, 16, 2):
                        move(dve, u, a, moved_v, lambda o, i: dve.tensor_scalar(o, i, 1.0 / 64, None, ALU.mult))
                dve.wait_ge(summed, len(UNITS))
                scale = 32 ** -0.5 * 384 ** -0.5
                for h in range(2):
                    last = dve.tensor_scalar(score[64 * h:64 * h + 64], s_bank[64 * h:64 * h + 64, :, h, :], scale, None, ALU.mult)
                last.then_inc(vec, 1)
                dve.wait_ge(vec, 1)
                dve.tensor_reduce(top[:], score[:], AX, ALU.max).then_inc(vec, 1)
                dve.wait_ge(vec, 2)
                dve.tensor_tensor(score[:], score[:], spread(top[:], 2, 64), ALU.subtract).then_inc(vec, 1)
                dve.wait_ge(exp_ready, 1)
                dve.tensor_reduce(denom[:], score[:], AX, ALU.add).then_inc(vec, 1)
                dve.wait_ge(vec, 4)
                dve.reciprocal(inv[:], denom[:]).then_inc(vec, 1)
                dve.wait_ge(vec, 5)
                for a in range(2):
                    last = dve.tensor_tensor(att2[:, :, :, a], score[:], spread(inv[:], 2, 64), ALU.mult)
                last.then_inc(vec, 1)
                for g in range(4):
                    dve.wait_ge(att_turned, g + 1)
                    for h in range(2):
                        last = dve.tensor_tensor(k.att_blocks[:, 2 * g + h].rearrange("p (s a) -> p s a", a=2),
                                                 spread(t_bank[g % 2][:, 64 * h:64 * h + 64], 2, 2),
                                                 spread(k.parity[:], 1, 64), ALU.mult)
                    last.then_inc(att_used, 1)


def tied_output(nc, zT, h_half, k):
    CH, CHUNKS = 8, 24
    with ExitStack() as stack:
        t = Memory(nc, stack)
        v = [t.sb(f"v{i}", [P, CH, 256]) for i in range(2)]
        gate = [t.sb(f"gate{i}", [P, CH, 256]) for i in range(2)]
        gated = [t.sb(f"gated{i}", [P, CH, 256]) for i in range(2)]
        gatedT = [t.sb(f"gatedT{i}", [P, 4, P]) for i in range(2)]
        vg_bank = [t.ps(f"vg_bank{i}", [P, 512]) for i in range(2)]
        o_bank = [t.ps(f"o_bank{i}", [P, 2, CH, 32]) for i in range(2)]
        t_bank = [t.ps(f"gt_bank{i}", [P, 4, P]) for i in range(2)]
        r_bank = t.ps("r_bank", [P, CH, 64])
        vg_mm, v_ready, gate_raw, gate_ready = t.sem("vg_mm"), t.sem("v_ready"), t.sem("gate_raw"), t.sem("gate_ready")
        mixed, gated_ready, turned, moved = t.sem("mixed"), t.sem("gated_ready"), t.sem("turned"), t.sem("moved")
        out_mm, added, biased = t.sem("out_mm"), t.sem("added"), t.sem("biased")

        def over_chunks(eng, body, tail=None):
            for n in range(2):
                body(n, n)
            with eng.Fori(1, CHUNKS // 2) as g:
                for n in range(2):
                    body(2 * g + n, n)
            if tail:
                tail()

        def started(n):
            return not isinstance(n, int) or n >= 0

        zcols = zT[:].rearrange("p b l -> p (b l)").rearrange("p (t l) -> p l t", l=192)
        with nc.Block() as block:
            @block.tensor
            def _(pe):
                def project(n, par):
                    for i in range(CH):
                        wait(pe, v_ready, CH * n + i - 1)
                        wait(pe, gate_raw, CH * n + i - 1)
                        for part in range(2):
                            last = pe.matmul(vg_bank[i % 2][:], zcols[:, n * CH + i, :], k.w_vg[:, part],
                                             start=(part == 0), stop=(part == 1))
                        last.then_inc(vg_mm, 1)

                def mix(n, par):
                    pe.wait_ge(v_ready, CH * n + CH)
                    for a in range(4):
                        wait(pe, gated_ready, 4 * n + a - 1)
                        for h in range(2):
                            head = 2 * a + h
                            last = pe.matmul(o_bank[a % 2][:, h], k.att_blocks[:, head],
                                             v[par][:, :, 32 * head:32 * head + 32], start=True, stop=True)
                        last.then_inc(mixed, 1)

                def turn(n, par):
                    pe.wait_ge(gated_ready, 4 * n + 4)
                    for a in range(4):
                        wait(pe, moved, 4 * n + a - 1)
                        for i in range(2):
                            for half in range(2):
                                last = pe.transpose(t_bank[a % 2][:, 2 * i + half],
                                                    gated[par][:, 2 * a + i, P * half:P * half + P], k.ident[:])
                        last.then_inc(turned, 1)
                        if a:
                            output(n, a - 1)
                    output(n, 3)

                def output(n, a):
                    pe.wait_ge(moved, 4 * n + a + 1)
                    if a == 0:
                        wait(pe, added, n)
                    for i in range(2):
                        for half in range(2):
                            last = pe.matmul(r_bank[:, 2 * a + i], gatedT[a % 2][:, 2 * i + half], k.attn_wo[:, half],
                                             start=(half == 0), stop=(half == 1))
                    last.then_inc(out_mm, 1)

                def body(n, par):
                    project(n, par)
                    if started(n - 1):
                        turn(n - 1, 1 - par)
                    mix(n, par)
                over_chunks(pe, body, lambda: turn(CHUNKS - 1, 1))

            @block.scalar
            def _(act):
                def values(n, par):
                    wait(act, mixed, 4 * (n - 2) + 4)
                    for i in range(CH):
                        act.wait_ge(vg_mm, CH * n + i + 1)
                        act.activation(v[par][:, i], vg_bank[i % 2][:, 0:256], ACT.Copy, scale=1.0 / 64).then_inc(v_ready, 1)

                def gates(n, par):
                    act.wait_ge(gate_raw, CH * n + CH)
                    act.activation(gate[par][:], gate[par][:], ACT.Sigmoid).then_inc(gate_ready, 1)

                def move(n, par):
                    for a in range(4):
                        act.wait_ge(turned, 4 * n + a + 1)
                        wait(act, out_mm, 4 * n + a - 1)
                        act.activation(gatedT[a % 2][:], t_bank[a % 2][:], ACT.Copy).then_inc(moved, 1)

                def body(n, par):
                    values(n, par)
                    gates(n, par)
                    if started(n - 1):
                        move(n - 1, 1 - par)
                over_chunks(act, body, lambda: move(CHUNKS - 1, 1))

            @block.vector
            def _(dve):
                dve.tensor_tensor(h_half, h_half, spread(k.attn_bo_row[:], 1, 192), ALU.add).then_inc(biased, 1)

                def gates(n, par):
                    for i in range(CH):
                        dve.wait_ge(vg_mm, CH * n + i + 1)
                        dve.wait_ge(v_ready, CH * n + i + 1)
                        dve.scalar_tensor_tensor(out=gate[par][:, i], in0=vg_bank[i % 2][:, 256:512], scalar=1.0 / 64,
                                                 in1=k.bg_row[:], op0=ALU.mult, op1=ALU.add).then_inc(gate_raw, 1)

                def multiply(n, par):
                    dve.wait_ge(gate_ready, n + 1)
                    wait(dve, turned, 4 * (n - 2) + 4)
                    for a in range(4):
                        dve.wait_ge(mixed, 4 * n + a + 1)
                        view = "p i (h c) -> p h i c"
                        dve.tensor_tensor(gated[par][:, :, 64 * a:64 * a + 64].rearrange(view, h=2), o_bank[a % 2][:],
                                          gate[par][:, :, 64 * a:64 * a + 64].rearrange(view, h=2), ALU.mult).then_inc(gated_ready, 1)

                def add(n):
                    dve.wait_ge(out_mm, 4 * n + 4)
                    dve.wait_ge(biased, 1)
                    dve.tensor_tensor(h_half[:, bass.ds(n * CH, CH), :], h_half[:, bass.ds(n * CH, CH), :], r_bank[:],
                                      ALU.add).then_inc(added, 1)

                def body(n, par):
                    gates(n, par)
                    if started(n - 1):
                        add(n - 1)
                    multiply(n, par)
                over_chunks(dve, body, lambda: add(CHUNKS - 1))


def feed_forward(nc, zT, h_dram, out, k):
    B, L, RING = 64, 384, 4
    with ExitStack() as stack:
        t = Memory(nc, stack)
        w_sel = [t.sb(f"w_sel{i}", [P, 2, P + 1]) for i in range(RING)]
        hid = [[t.sb(f"hid{n}_{i}", [P, L]) for i in range(2)] for n in range(3)]
        res = [t.sb(f"res{i}", [P, 3, 64]) for i in range(RING)]
        final = [t.sb(f"final{i}", [P, 3, 64]) for i in range(RING)]
        bank = [[t.ps(f"ff_bank{n}_{i}", [P, 512]) for i in range(2)] for n in range(4)]
        selected, res_ready = t.sem("selected"), [t.sem(f"res_ready{i}") for i in range(RING)]
        mm = [t.sem(f"mm{n}") for n in range(4)]
        relu = [t.sem(f"relu{n}") for n in range(3)]
        res_biased, final_ready, stored = t.sem("res_biased"), t.sem("final_ready"), [t.sem(f"stored{i}") for i in range(RING)]

        def count(semaphore_step, b, slot):
            if isinstance(b, int):
                return semaphore_step * (b // RING + 1)
            return (b - slot) * (semaphore_step // RING) + semaphore_step

        def over_rows(eng, body, skew):
            for s in range(RING):
                body(s, s)
            with eng.Fori(1, B // RING) as g:
                for s in range(RING):
                    body(g * RING + s, s)
            for s in range(skew):
                body(B + s, s)

        def inside(b):
            return not isinstance(b, int) or 0 <= b < B

        with nc.Block() as block:
            @block.gpsimd
            def _(pool):
                experts = k.w_exp[:].rearrange("p (l e) c -> p l e c", l=2)

                def body(b, slot):
                    wait(pool, relu[2], b - RING + 1)
                    e = pool.value_load(k.route[0:1, bass.ds(b, 1)], min_val=0, max_val=15)
                    pool.tensor_copy(w_sel[slot][:].unsqueeze(2), experts[:, :, bass.ds(e, 1), :]).then_inc(selected, 1)
                over_rows(pool, body, 0)

            @block.sync
            def _(sp):
                def store(b, slot):
                    wait(sp, final_ready, b + 1)
                    sp.dma_start(out[b].rearrange("(j p) c -> p j c", p=P), final[slot][:]).then_inc(stored[slot], 16)

                def body(b, slot):
                    if inside(b):
                        wait(sp, final_ready, b - RING + 1)
                        sp.dma_start(res[slot][:], h_dram[b].rearrange("(j p) c -> p j c", p=P)).then_inc(res_ready[slot], 16)
                    if inside(b - 3):
                        store(b - 3, (slot - 3) % RING)
                over_rows(sp, body, 3)
                for s in range(RING):
                    sp.wait_ge(stored[s], 16 * (B // RING))

            @block.tensor
            def _(pe):
                def layer(n, b, slot):
                    par = slot % 2
                    dst = bank[n][par]
                    if n < 3:
                        wait(pe, relu[n], b - 1)
                    else:
                        wait(pe, final_ready, b - 1)
                    if n == 0:
                        tokens = zT.rearrange("p l (b a) -> p b a l", a=2)[:, bass.ds(b, 1)]
                        for part, weights in enumerate((k.wi_hi, k.wi_lo)):
                            last = pe.matmul(dst[:, 0:L].rearrange("p (o a l) -> p o a l", o=1, a=2), weights[:], tokens,
                                             start=(part == 0), stop=(part == 1))
                    elif n < 3:
                        pe.wait_ge(relu[n - 1], b + 1)
                        pe.wait_ge(selected, b + 1)
                        last = pe.matmul(dst[:, 0:L], w_sel[slot][:, n - 1, 0:P], hid[n - 1][par][:], start=True, stop=True)
                    else:
                        pe.wait_ge(relu[2], b + 1)
                        for j in range(3):
                            last = pe.matmul(dst[:, 64 * j:64 * j + 64], hid[2][par][:, P * j:P * j + P], k.ffn_wo[:],
                                             start=True, stop=True)
                    last.then_inc(mm[n], 1)

                def body(b, slot):
                    for n in (3, 2, 1, 0):
                        if inside(b - n):
                            layer(n, b - n, (slot - n) % RING)
                over_rows(pe, body, 3)

            @block.scalar
            def _(act):
                def relu_of(n, b, slot):
                    par = slot % 2
                    act.wait_ge(mm[n], b + 1)
                    wait(act, mm[n + 1], b - 1)
                    bias = k.bi[:, 0:1] if n == 0 else w_sel[slot][:, n - 1, P:P + 1]
                    act.activation(hid[n][par][:], bank[n][par][:, 0:L], ACT.Relu, bias=bias,
                                   scale=1.0 / 64 if n == 0 else 1.0).then_inc(relu[n], 1)

                def body(b, slot):
                    for n in (2, 0):
                        if inside(b - n):
                            relu_of(n, b - n, (slot - n) % RING)
                over_rows(act, body, 2)

            @block.vector
            def _(dve):
                def hidden(b, slot):
                    par = slot % 2
                    dve.wait_ge(mm[1], b + 1)
                    wait(dve, mm[2], b - 1)
                    dve.tensor_scalar(hid[1][par][:], bank[1][par][:, 0:L], w_sel[slot][:, 0, P:P + 1], 0.0,
                                      ALU.add, ALU.max).then_inc(relu[1], 1)

                def finish(b, slot):
                    dve.wait_ge(res_ready[slot], count(16, b, slot))
                    dve.tensor_tensor(res[slot][:], res[slot][:], spread(k.ffn_bo_row[:], 1, 3), ALU.add).then_inc(res_biased, 1)
                    dve.wait_ge(res_biased, b + 1)
                    dve.wait_ge(mm[3], b + 1)
                    if inside(b - RING):
                        dve.wait_ge(stored[slot], count(16, b, slot) - 16)
                    dve.tensor_tensor(final[slot][:], bank[3][slot % 2][:, 0:192].rearrange("p (j c) -> p j c", j=3),
                                      res[slot][:], ALU.add).then_inc(final_ready, 1)

                def body(b, slot):
                    for n, step in ((3, finish), (1, hidden)):
                        if inside(b - n):
                            step(b - n, (slot - n) % RING)
                over_rows(dve, body, 3)


class Kept:

    def __init__(self, m):
        sb = m.sb
        self.ident, self.ident16, self.parity = sb("ident", [P, P]), sb("ident16", [P, P], F16), sb("parity", [P, 2])
        self.half = sb("minus_half", [P, 1])
        self.stat_sel = sb("stat_sel", [P, 62])
        self.w_k, self.w_v, self.w_q, self.w_proj = (sb(n, [P, P]) for n in ("w_k", "w_v", "w_q", "w_proj"))
        self.lnq_w, self.lnq_b, self.bi = sb("lnq_w", [P, 1]), sb("lnq_b", [P, 1]), sb("bi", [P, 1])
        self.tok_const = sb("tok_const", [P, P])
        self.gamma_row, self.beta_row = sb("gamma_row", [P, 64]), sb("beta_row", [P, 64])
        self.attn_bo_row, self.ffn_bo_row = sb("attn_bo_row", [P, 64]), sb("ffn_bo_row", [P, 64])
        self.bg_row, self.attn_wo = sb("bg_row", [P, 256]), sb("attn_wo", [P, 2, 64])
        self.w_qk, self.w_vg = sb("w_qk", [P, 2, 512], F16), sb("w_vg", [P, 2, 512], F16)
        self.wi_hi, self.wi_lo, self.ffn_wo = sb("wi_hi", [P, P], F16), sb("wi_lo", [P, P], F16), sb("ffn_wo", [P, 64])
        self.w_exp = sb("w_exp", [P, 32, P + 1])
        self.route = sb("route", [1, 64], I32)


def early_fusion(nc, x, w, out):
    B, L, C = 64, 384, 64
    h_dram = nc.dram_tensor("h_scratch", (B, L, C), F32, kind="Internal").ap()
    h2_dram = nc.dram_tensor("h2_scratch", (B, L, C), F32, kind="Internal").ap()
    halves = "b (a l) c -> (b a) l c"
    with ExitStack() as outer:
        m = Memory(nc, outer)
        k = Kept(m)
        tokens_buffer = m.sb("tokens_buffer", [P, B * L * C // P])
        k.h_tok = tokens_buffer[:].rearrange("p (b j c) -> p b j c", j=3, c=C)
        h_half = tokens_buffer[:].rearrange("p (l c) -> p l c", c=C)
        setup_weights(nc, m, w, k)
        local_attention(nc, x, k)
        with nc.semaphore("h_stored") as h_stored, nc.Block() as block:
            @block.sync
            def _(sp):
                for j in range(3):
                    sp.dma_start(h_dram[:, P * j:P * j + P, :].rearrange("b t c -> t b c"),
                                 k.h_tok[:, :, j, :]).then_inc(h_stored, 16)
                sp.wait_ge(h_stored, 48)
        zT = m.sb("zT", [P, B, L], F16)
        k.att_blocks = m.sb("att_blocks", [P, 8, P])
        tokens = k.h_tok.rearrange("p b j c -> p (b j) c")
        columns = zT[:].rearrange("p b (j t) -> p (b j) t", j=3)
        normalise_and_turn(nc, lambda n: tokens[:, bass.ds(n * 24, 24), :],
                           lambda n, a: columns[:, bass.ds(n * 24 + 8 * a, 8), :],
                           8, 24, (1 + EPS) / C, EPS * EPS, k, True)
        tied_scores(nc, zT, h_half, h_dram.rearrange(halves, a=2), k)
        tied_output(nc, zT, h_half, k)
        with nc.semaphore("h2_stored") as h2_stored, nc.Block() as block:
            @block.sync
            def _(sp):
                sp.dma_start(h2_dram.rearrange(halves, a=2), h_half).then_inc(h2_stored, 16)
                sp.wait_ge(h2_stored, 16)
        z2 = zT[:].rearrange("p b l -> p (b l)").rearrange("p (l t) -> p l t", t=P)
        normalise_and_turn(nc, lambda n: h_half[:, bass.ds(n * 24, 24), :],
                           lambda n, a: z2[:, bass.ds(n * 24 + 8 * a, 8), :],
                           8, 24, 1.0 / C, EPS, k, False)
        feed_forward(nc, z2, h2_dram, out, k)


_OUT = (64, 384, 64)


def kernel(**inputs):
    from concourse import bacc
    from concourse.bass_utils import run_bass_kernel_spmd

    nc = bacc.Bacc("TRN2", target_bir_lowering=False, num_devices=1)
    arrays, weights = {}, {}
    for name, value in inputs.items():
        a = np.ascontiguousarray(value)
        arrays[f"in_{name}"] = a
        ap = nc.dram_tensor(f"in_{name}", a.shape, mybir.dt.from_np(a.dtype), kind="ExternalInput").ap()
        weights[name[3:] if name.startswith("L0_") else name] = ap
    out = nc.dram_tensor("out", _OUT, F32, kind="ExternalOutput").ap()
    x = weights.pop("x")
    early_fusion(nc, x, weights, out)
    return run_bass_kernel_spmd(nc, [arrays], core_ids=[0]).results[0]["out"]
```

```python
from contextlib import ExitStack

import numpy as np

import concourse.bass as bass
from concourse import mybir

ALU = mybir.AluOpType
ACT = mybir.ActivationFunctionType
AX = mybir.AxisListType.X
F32 = mybir.dt.float32
F16 = mybir.dt.float16
I32 = mybir.dt.int32
NEWTON = 3
ROOT_STEPS = 3 * NEWTON + 1

P = 128
EPS = 1e-5


def wait(eng, semaphore, value):
    if isinstance(value, int) and value <= 0:
        return
    eng.wait_ge(semaphore, value)


def spread(ap, axis, count):
    ap = ap.unsqueeze(axis)
    shape = list(ap.shape)
    shape[axis] = count
    return ap.to_broadcast(shape)


def guess_root(dve, step, var, root):
    step(dve.tensor_scalar(root.bitcast(I32), var.bitcast(I32), 1, None, ALU.logical_shift_right))
    step(dve.tensor_scalar(root.bitcast(I32), root.bitcast(I32), -1.0, float(0x5F3759DF), ALU.mult, ALU.add))


def newton_root(dve, step, var, root, half_sq, out):
    step(dve.scalar_tensor_tensor(out=half_sq, in0=root, scalar=-0.5, in1=root, op0=ALU.mult, op1=ALU.mult))
    step(dve.tensor_tensor(half_sq, half_sq, var, ALU.mult))
    return dve.scalar_tensor_tensor(out=out, in0=half_sq, scalar=1.5, in1=root, op0=ALU.add, op1=ALU.mult)


class Memory:

    def __init__(self, nc, stack, prefix=""):
        self.nc, self.stack, self.prefix = nc, stack, prefix

    def sb(self, name, shape, dtype=F32):
        return self.stack.enter_context(self.nc.sbuf_tensor(self.prefix + name, shape, dtype))

    def ps(self, name, shape, dtype=F32):
        return self.stack.enter_context(self.nc.psum_tensor(self.prefix + name, shape, dtype))

    def sem(self, name):
        return self.stack.enter_context(self.nc.semaphore(self.prefix + name))


def setup_weights(nc, m, w, k):
    with ExitStack() as stack:
        t = Memory(nc, stack)
        C = 64
        wkv = t.sb("wkv", [P, C])
        wv = t.sb("wv", [C, C])
        wq2 = t.sb("wq2", [C, 2, C])
        proj2 = t.sb("proj2", [C, 2, C])
        kvw_row = t.sb("kvw_row", [P, C])
        kvb_row = t.sb("kvb_row", [C, C])
        wkv_sum = t.sb("wkv_sum", [P, 1])
        wkv2 = t.sb("wkv2", [P, 2, C])
        wvb = t.sb("wvb", [C, C])
        vbias = t.sb("vbias", [C, 1])
        ones = t.sb("ones", [C, P])
        vbias_cols = t.sb("vbias_cols", [C, P])
        projT = t.sb("projT", [C, C])
        projb_row = t.sb("projb_row", [P, C])
        qkvg = t.sb("qkvg", [P, 4, 256])
        qkvg_s = t.sb("qkvg_s", [P, 1024])
        wr = t.sb("wr", [P, 32, P])
        ws = t.sb("ws", [P, 2, P])
        brs = t.sb("brs", [32, P])
        bss = t.sb("bss", [32, P])
        wi = t.sb("wi", [P, 2, C])
        wi_s = t.sb("wi_s", [P, P])
        wo_nat = t.sb("wo_nat", [C, P])
        bank = [t.ps(f"sbank{i}", [P, 512]) for i in range(2)]
        loaded, zeroed, made = t.sem("loaded"), t.sem("zeroed"), t.sem("made")
        vec, product, moved = t.sem("vec"), t.sem("product"), t.sem("moved")
        n_loads = [0]

        with nc.Block() as block:
            @block.sync
            def _(sp):
                def load(dst, src):
                    sp.dma_start(dst, src).then_inc(loaded, 16)
                    n_loads[0] += 16
                load(wkv[:], w["tok_Wkv"])
                load(wv[:], w["tok_Wkv"][C:2 * C, :])
                for d in range(2):
                    load(wq2[:, d, :], w["tok_Wq"])
                    load(proj2[:, d, :], w["tok_proj_w"])
                    load(k.lnq_w[d * C:(d + 1) * C, :], w["tok_ln_q_w"].unsqueeze(1))
                    load(k.lnq_b[d * C:(d + 1) * C, :], w["tok_ln_q_b"].unsqueeze(1))
                    for n, name in enumerate(("attn_Wq", "attn_Wk", "attn_Wv", "attn_Wg")):
                        load(qkvg[d * C:(d + 1) * C, n, :], w[name])
                    load(wi[:, d, :], w["ffn_Wi"])
                load(kvw_row[:], w["tok_ln_kv_w"].partition_broadcast(P))
                load(kvb_row[:], w["tok_ln_kv_b"].partition_broadcast(C))
                load(projb_row[:], w["tok_proj_b"].partition_broadcast(P))
                load(k.gamma_row[:], w["attn_gamma"].partition_broadcast(P))
                load(k.beta_row[:], w["attn_beta"].partition_broadcast(P))
                load(k.bg_row[:], w["attn_bg"].partition_broadcast(P))
                load(k.attn_bo_row[:], w["attn_bo"].partition_broadcast(P))
                load(k.ffn_bo_row[:], w["ffn_bo"].partition_broadcast(P))
                load(k.attn_wo[:], w["attn_Wo"].rearrange("(k p) c -> p k c", k=2))
                load(wr[:], w["ffn_Wr"].rearrange("l e o i -> o (l e) i"))
                load(ws[:], w["ffn_Ws"].rearrange("l s o i -> o (l s) i"))
                load(brs[:], w["ffn_br"].rearrange("l e o -> (l e) o"))
                for n in range(2):
                    load(bss[16 * n:16 * n + 16, :], w["ffn_bs"][n, 0].partition_broadcast(16))
                load(wo_nat[:], w["ffn_Wo"])
                load(k.bi[:], w["ffn_bi"].unsqueeze(1))
                load(k.route[:], w["ffn_route_id"].unsqueeze(0))
                load(k.h_tok[:, :, 2, :], w["txt"].rearrange("b t c -> t b c"))

            @block.gpsimd
            def _(pool):
                clear = [(k.ident, 0.0), (k.parity, 0.0), (k.centre, 0.0), (k.w_k, 0.0), (k.w_v, 0.0),
                         (k.w_q, 0.0), (k.w_proj, 0.0), (ones, 1.0)]
                for tile, value in clear:
                    pool.memset(tile[:], value).then_inc(zeroed, 1)
                pool.wait_ge(zeroed, len(clear))
                pool.affine_select(out=k.ident[:], in_=k.ident[:], compare_op=ALU.not_equal, fill=1.0,
                                   base=0, pattern=[[-1, P]], channel_multiplier=1).then_inc(made, 1)
                pool.wait_ge(made, 1)
                pool.tensor_copy(k.ident16[:], k.ident[:]).then_inc(made, 1)

            steps = [0]

            @block.vector
            def _(dve):
                def step(instruction):
                    steps[0] += 1
                    instruction.then_inc(vec, 1)
                    dve.wait_ge(vec, steps[0])
                dve.wait_ge(loaded, n_loads[0])
                dve.wait_ge(made, 2)
                for img in range(2):
                    step(dve.memset(k.centre[64 * img:64 * img + 64, 64 * img:64 * img + 64], -1.0 / C))
                step(dve.tensor_tensor(k.centre[:], k.centre[:], k.ident[:], ALU.add))
                step(dve.tensor_reduce(k.parity[:], k.ident[:].rearrange("p (t a) -> p a t", a=2), AX, ALU.add))
                step(dve.tensor_tensor(wkv[:], wkv[:], kvw_row[:], ALU.mult))
                step(dve.tensor_reduce(wkv_sum[:], wkv[:], AX, ALU.add))
                step(dve.tensor_scalar(wkv_sum[:], wkv_sum[:], -1.0 / C, None, ALU.mult))
                for d in range(2):
                    step(dve.tensor_scalar(wkv2[:, d, :], wkv[:], wkv_sum[:, 0:1], None, ALU.add))
                step(dve.tensor_tensor(wvb[:], wv[:], kvb_row[:], ALU.mult))
                step(dve.tensor_reduce(vbias[:], wvb[:], AX, ALU.add))
                step(dve.tensor_scalar(vbias_cols[:], ones[:], vbias[:, 0:1], None, ALU.mult))
                step(dve.tensor_scalar(qkvg_s[:], qkvg[:].rearrange("p a b -> p (a b)"), 64.0, None, ALU.mult))
                split = [(k.w_qk[:, 0].rearrange("p (g a h c) -> p a g h c", g=4, a=2, h=2)[:, n],
                          k.w_qk[:, 1].rearrange("p (g a h c) -> p a g h c", g=4, a=2, h=2)[:, n],
                          qkvg_s[:, 256 * n:256 * n + 256].rearrange("p (g h c) -> p g h c", g=4, h=2))
                         for n in range(2)]
                split.append((k.w_vg[:, 0], k.w_vg[:, 1], qkvg_s[:, 512:1024]))
                for hi, lo, whole in split:
                    step(dve.tensor_copy(hi, whole))
                    step(dve.tensor_tensor(lo, whole, hi, ALU.subtract))
                for n in range(2):
                    step(dve.tensor_tensor(ws[:, n, :], ws[:, n, :], k.ident[:], ALU.add))
                    for e in range(16):
                        step(dve.tensor_tensor(wr[:, 16 * n + e, :], wr[:, 16 * n + e, :], ws[:, n, :], ALU.add))
                step(dve.tensor_tensor(brs[:], brs[:], bss[:], ALU.add))

                def copy(n, dst, src, scale=1.0):
                    dve.wait_ge(product, n + 1)
                    dve.tensor_scalar(dst, src, scale, None, ALU.mult).then_inc(moved, 1)

                def halves(n, dst, src_of, scale=1.0):
                    dve.wait_ge(product, n + 1)
                    dve.tensor_scalar(dst[0:64, 0:64], src_of(0), scale, None, ALU.mult)
                    dve.tensor_scalar(dst[64:128, 64:128], src_of(1), scale, None, ALU.mult).then_inc(moved, 1)
                dve.wait_ge(product, 1)
                for j, dst in enumerate((k.w_k, k.w_v)):
                    dve.tensor_copy(dst[0:64, 0:64], bank[0][0:64, 64 * j:64 * j + 64])
                    last = dve.tensor_copy(dst[64:128, 64:128], bank[0][64:128, 64 * j:64 * j + 64])
                last.then_inc(moved, 1)
                halves(1, k.w_q, lambda i: bank[1][64 * i:64 * i + 64, 0:64], C ** -0.5)
                halves(2, k.w_proj, lambda i: bank[0][64 * i:64 * i + 64, 0:64])
                dve.wait_ge(product, 4)
                dve.tensor_copy(projT[:], bank[1][0:64, 0:64]).then_inc(moved, 1)
                dve.wait_ge(product, 5)
                for half in range(2):
                    last = dve.tensor_tensor(k.tok_const[:, 64 * half:64 * half + 64], bank[0][:, 0:64],
                                             projb_row[:], ALU.add)
                last.then_inc(moved, 1)
                dve.wait_ge(product, 6)
                dve.tensor_scalar(wi_s[:], bank[1][:, 0:128], 64.0, None, ALU.mult).then_inc(moved, 1)
                dve.wait_ge(moved, 6)
                step(dve.tensor_copy(k.wi_hi[:], wi_s[:]))
                step(dve.tensor_tensor(k.wi_lo[:], wi_s[:], k.wi_hi[:], ALU.subtract))
                copy(6, k.ffn_wo[:], bank[0][:, 0:64])
                copy(7, k.w_exp[:, :, P], bank[1][:, 0:32])
                for e in range(32):
                    copy(8 + e, k.w_exp[:, e, 0:P], bank[e % 2][:, 0:128])

            @block.tensor
            def _(pe):
                pe.wait_ge(made, 2)
                pe.wait_ge(vec, steps[0] - 2)
                n = [0]

                def start():
                    if n[0] >= 2:
                        pe.wait_ge(moved, n[0] - 1)
                    n[0] += 1
                    return bank[(n[0] - 1) % 2]
                pe.transpose(start()[:, 0:128], wkv2[:].rearrange("p a b -> p (a b)"), k.ident[:]).then_inc(product, 1)
                for src in (wq2, proj2, proj2):
                    pe.transpose(start()[:, 0:64], src[:].rearrange("p a b -> p (a b)"),
                                 k.ident[0:64, 0:64]).then_inc(product, 1)
                b = start()
                pe.wait_ge(moved, 4)
                pe.matmul(b[:, 0:64], vbias_cols[:], projT[:], start=True, stop=True).then_inc(product, 1)
                pe.transpose(start()[:, 0:128], wi[:].rearrange("p a b -> p (a b)"), k.ident[:]).then_inc(product, 1)
                pe.transpose(start()[:, 0:64], wo_nat[:], k.ident[0:64, 0:64]).then_inc(product, 1)
                pe.transpose(start()[:, 0:32], brs[:], k.ident[0:32, 0:32]).then_inc(product, 1)
                for e in range(32):
                    pe.transpose(start()[:, 0:128], wr[:, e, :], k.ident[:]).then_inc(product, 1)


def local_attention(nc, x, k):
    PAIRS, RING = 32, 4
    ROOTING = ROOT_STEPS + 1
    with ExitStack() as stack:
        t = Memory(nc, stack)
        x_pair = [t.sb(f"x_pair{i}", [P, 4, 1024]) for i in range(RING)]
        f1, f2 = t.sb("f1", [P, 512]), t.sb("f2", [P, P, 2])
        feat_ch = [t.sb(f"feat_ch{i}", [P, 2, P]) for i in range(2)]
        squares, var = [t.sb(f"squares{i}", [P, 34, 2]) for i in range(2)], t.sb("var", [P, 68])
        mean_sq = t.sb("mean_sq", [P, 4, 64])
        root, half_sq = t.sb("root", [P, 68]), t.sb("half_sq", [P, 68])
        rstd = [t.sb(f"rstd{i}", [P, 34, 2]) for i in range(2)]
        feat = [t.sb(f"feat{i}", [P, 256]) for i in range(2)]
        feat_c = [t.sb(f"feat_c{i}", [P, 256]) for i in range(2)]
        q_hat, q_hatT = t.sb("q_hat", [P, 256]), t.sb("q_hatT", [P, 256])
        q = [t.sb(f"q{i}", [P, 2, P]) for i in range(2)]
        kq = t.sb("kq", [P, 16, P])
        logit = [t.sb(f"logit{i}", [P, 256]) for i in range(2)]
        expo = [t.sb(f"expo{i}", [P, 256]) for i in range(2)]
        top = t.sb("top", [P, 16])
        weight = t.sb("weight", [P, 256])
        denom = t.sb("denom", [P, 16])
        inv = [t.sb(f"inv{i}", [P, 16]) for i in range(2)]
        wv = [t.sb(f"wv{i}", [P, 16, P]) for i in range(2)]
        agg = [t.sb(f"agg{i}", [P, P]) for i in range(2)]
        agg_n, aggT = t.sb("agg_n", [P, P]), t.sb("aggT", [P, P])
        k_bank = [t.ps(f"k_bank{i}", [P, 4, P]) for i in range(2)]
        v_bank = [t.ps(f"v_bank{i}", [P, 4, P]) for i in range(2)]
        x_bank = [t.ps(f"x_bank{i}", [P, 4, 2, 64]) for i in range(2)]
        q_bank, a_bank = t.ps("q_bank", [P, 512]), t.ps("a_bank", [P, 512])

        x_loaded = [t.sem(f"x_loaded{i}") for i in range(RING)]
        feat_part, feat_done, x_turned, squared = t.sem("feat_part"), t.sem("feat_done"), t.sem("x_turned"), t.sem("squared")
        feat_turned, feat_ready, feat_squared = t.sem("feat_turned"), t.sem("feat_ready"), t.sem("feat_squared")
        rooting, rstd_ready = t.sem("rooting"), t.sem("rstd_ready")
        q_hat_ready, q_turned, q_hatT_ready = t.sem("q_hat_ready"), t.sem("q_turned"), t.sem("q_hatT_ready")
        q_mm, q_ready, feat_c_ready = t.sem("q_mm"), t.sem("q_ready"), t.sem("feat_c_ready")
        k_mm, kq_done, logits_raw, logits_ready = t.sem("k_mm"), t.sem("kq_done"), t.sem("logits_raw"), t.sem("logits_ready")
        top_ready, shifted, exp_ready = t.sem("top_ready"), t.sem("shifted"), t.sem("exp_ready")
        weight_ready, denom_ready, inv_ready = t.sem("weight_ready"), t.sem("denom_ready"), t.sem("inv_ready")
        v_mm, wv_done, agg_part, agg_ready = t.sem("v_mm"), t.sem("wv_done"), t.sem("agg_part"), t.sem("agg_ready")
        agg_n_ready, agg_turned, aggT_ready = t.sem("agg_n_ready"), t.sem("agg_turned"), t.sem("aggT_ready")
        proj_mm, h_ready = t.sem("proj_mm"), t.sem("h_ready")

        def over_pairs(eng, first, body, tail):
            first()
            for slot in range(RING):
                body(slot, slot)
            with eng.Fori(1, PAIRS // RING - 1) as g:
                for slot in range(RING):
                    body(g * RING + slot, slot)
            for slot in range(RING):
                body(PAIRS - RING + slot, slot)
            tail()

        def known(r, least, most):
            return not isinstance(r, int) or least <= r <= most

        with nc.Block() as block:
            @block.sync
            def _(sp):
                def load(r, slot):
                    if known(r, RING, PAIRS):
                        sp.wait_ge(feat_turned, r - 1)
                    pair = x.rearrange("(r b) c (h i) w -> r (b c) i h w", b=2, i=4)[r]
                    for i in range(4):
                        sp.dma_start(x_pair[slot][:, i, :].rearrange("p (h w) -> p h w", h=16),
                                     pair[:, i]).then_inc(x_loaded[slot], 16)
                over_pairs(sp, lambda: None, load, lambda: None)

            def loaded(eng, r, slot):
                if isinstance(r, int):
                    eng.wait_ge(x_loaded[slot], 64 * (r // RING + 1))
                else:
                    eng.wait_ge(x_loaded[slot], (r - slot) * (64 // RING) + 64)

            @block.gpsimd
            def _(pool):
                def features(r, slot, half):
                    u = 2 * r + half
                    loaded(pool, r, slot)
                    xp = x_pair[slot][:, :, 512 * half:512 * half + 512]
                    wait(pool, feat_done, u)
                    pool.tensor_tensor(f1[:], xp[:, 0, :], xp[:, 1, :], ALU.add).then_inc(feat_part, 1)
                    for i in (2, 3):
                        pool.wait_ge(feat_part, 4 * u + i - 1)
                        pool.tensor_tensor(f1[:], f1[:], xp[:, i, :], ALU.add).then_inc(feat_part, 1)
                    pool.wait_ge(feat_part, 4 * u + 3)
                    f = f1[:].rearrange("p (t j) -> p t j", j=4)
                    pool.tensor_tensor(f2[:], f[:, :, 0:2], f[:, :, 2:4], ALU.add).then_inc(feat_part, 1)
                    pool.wait_ge(feat_part, 4 * u + 4)
                    wait(pool, feat_turned, r - 1)
                    pool.tensor_tensor(feat_ch[slot % 2][:, half, :], f2[:, :, 0], f2[:, :, 1], ALU.add).then_inc(feat_done, 1)

                def sum_pixels(u, par):
                    wait(pool, wv_done, 4 * u + 4)
                    w = wv[par]
                    for n, half in enumerate((8, 4, 2)):
                        pool.tensor_tensor(w[:, 0:half], w[:, 0:half], w[:, half:2 * half], ALU.add).then_inc(agg_part, 1)
                        pool.wait_ge(agg_part, 3 * u + n + 1)
                    wait(pool, agg_n_ready, u - 1)
                    pool.tensor_tensor(agg[par][:], w[:, 0], w[:, 1], ALU.add).then_inc(agg_ready, 1)

                def first():
                    for r in range(2):
                        for half in range(2):
                            features(r, r, half)

                def body(r, slot):
                    more = known(r, 0, PAIRS - 3)
                    if more:
                        features(r + 2, (slot + 2) % RING, 0)
                    if known(r, 1, PAIRS):
                        sum_pixels(2 * r - 1, 1)
                    if more:
                        features(r + 2, (slot + 2) % RING, 1)
                    sum_pixels(2 * r, 0)
                over_pairs(pool, first, body, lambda: sum_pixels(2 * PAIRS - 1, 1))

            @block.scalar
            def _(act):
                def copy(dst, src, after, count, done, scale=1.0):
                    act.wait_ge(after, count)
                    act.activation(dst, src, ACT.Copy, scale=scale).then_inc(done, 1)

                def square_pixels(r, slot, half, i):
                    step = 8 * r + 4 * half + i
                    act.wait_ge(x_turned, step + 1)
                    if half == 0 and i == 0:
                        wait(act, rooting, ROOTING * (r - 2) + 1)
                    for j in range(4):
                        for img in range(2):
                            group = 16 * half + 4 * i + j
                            act.activation(x_bank[i % 2][:, j, img], x_bank[i % 2][:, j, img], ACT.Square,
                                           accum_out=squares[slot % 2][:, group, img:img + 1]).then_inc(squared, 1)

                def patch_means(r, slot):
                    wait(act, feat_c_ready, r - 1)
                    copy(feat[slot % 2][:], q_bank[:, 0:256], feat_turned, r + 1, feat_ready, 1.0 / 16)
                    wait(act, feat_squared, 4 * r)
                    for n in range(4):
                        act.activation(mean_sq[:, n], q_bank[:, 256 + 64 * n:320 + 64 * n], ACT.Square, scale=1.0 / 16,
                                       accum_out=squares[slot % 2][:, 32 + n // 2, n % 2:n % 2 + 1]).then_inc(feat_squared, 1)

                def affine_means(r):
                    act.wait_ge(q_turned, r + 1)
                    act.activation(q_hatT[:], q_bank[:, 0:256], ACT.Identity, bias=k.lnq_b[:, 0:1],
                                   scale=k.lnq_w[:, 0:1]).then_inc(q_hatT_ready, 1)

                def move_queries(r, slot):
                    wait(act, kq_done, 8 * (r - 2) + 8)
                    copy(q[slot % 2][:].rearrange("p a b -> p (a b)"), q_bank[:, 256:512], q_mm, r + 1, q_ready)

                def exponential(u, par):
                    act.wait_ge(shifted, u + 1)
                    act.activation(expo[par][:], logit[par][:], ACT.Exp).then_inc(exp_ready, 1)

                def turned(u):
                    copy(aggT[:], a_bank[:, 0:128], agg_turned, u + 1, aggT_ready)

                def first():
                    for half in range(2):
                        for i in range(4):
                            square_pixels(0, 0, half, i)
                    patch_means(0, 0)
                    for i in range(4):
                        square_pixels(1, 1, 0, i)

                def body(r, slot):
                    more = known(r, 0, PAIRS - 2)
                    before = known(r, 1, PAIRS)
                    for half in range(2):
                        u = 2 * r + half
                        for i in range(4):
                            if half == 0 and i == 1:
                                affine_means(r)
                                move_queries(r, slot)
                            if i == 1 and (half or before):
                                exponential(u - 1, 1 - half)
                            if half and known(r, 0, PAIRS - 3):
                                square_pixels(r + 2, slot, 0, i)
                            if half == 0 and more:
                                square_pixels(r + 1, (slot + 1) % RING, 1, i)
                        if before:
                            turned(u - 2)
                        if more and half == 0:
                            patch_means(r + 1, (slot + 1) % RING)

                def tail():
                    exponential(2 * PAIRS - 1, 1)
                    turned(2 * PAIRS - 2)
                    turned(2 * PAIRS - 1)
                over_pairs(act, first, body, tail)

            @block.tensor
            def _(pe):
                def turn_pixels(r, slot, half, i):
                    step = 8 * r + 4 * half + i
                    if half == 0 and i == 0:
                        loaded(pe, r, slot)
                    wait(pe, squared, 8 * step - 8)
                    pixels = x_pair[slot][:, i, 512 * half:512 * half + 512].rearrange("p (t j) -> p j t", j=4)
                    for j in range(4):
                        last = pe.matmul(x_bank[i % 2][:, j].rearrange("p m c -> p (m c)"), pixels[:, j, :], k.centre[:],
                                         start=True, stop=True)
                    last.then_inc(x_turned, 1)

                def prepare_a(r, slot):
                    pe.wait_ge(feat_done, 2 * r + 2)
                    wait(pe, q_ready, r)
                    for half in range(2):
                        pe.transpose(q_bank[:, P * half:P * half + P], feat_ch[slot % 2][:, half, :], k.ident[:])
                    for half in range(2):
                        last = pe.matmul(q_bank[:, 256 + P * half:256 + P * half + P], feat_ch[slot % 2][:, half, :],
                                         k.centre[:], start=True, stop=True)
                    last.then_inc(feat_turned, 1)

                def prepare_b(r, slot):
                    pe.wait_ge(q_hat_ready, r + 1)
                    for half in range(2):
                        last = pe.transpose(q_bank[:, P * half:P * half + P],
                                            q_hat[:, P * half:P * half + P], k.ident[:])
                    last.then_inc(q_turned, 1)

                def queries(r, slot):
                    pe.wait_ge(q_hatT_ready, r + 1)
                    for half in range(2):
                        last = pe.matmul(q_bank[:, 256 + P * half:256 + P * half + P], q_hatT[:, P * half:P * half + P],
                                         k.w_q[:], start=True, stop=True)
                    last.then_inc(q_mm, 1)

                def project_pixels(u, slot, half, i, banks, weights, done, used):
                    wait(pe, used, 4 * u + i - 1)
                    pixels = x_pair[slot][:, i, 512 * half:512 * half + 512].rearrange("p (t j) -> p j t", j=4)
                    for j in range(4):
                        last = pe.matmul(banks[i % 2][:, j, :], pixels[:, j, :], weights[:], start=True, stop=True)
                    last.then_inc(done, 1)

                def keys(u, slot, half, i):
                    project_pixels(u, slot, half, i, k_bank, k.w_k, k_mm, kq_done)

                def values(u, slot, half, i):
                    project_pixels(u, slot, half, i, v_bank, k.w_v, v_mm, wv_done)

                def turn(u):
                    pe.wait_ge(agg_n_ready, u + 1)
                    wait(pe, h_ready, u)
                    pe.transpose(a_bank[:, 0:P], agg_n[:], k.ident[:]).then_inc(agg_turned, 1)

                def project(u):
                    pe.wait_ge(aggT_ready, u + 1)
                    pe.matmul(a_bank[:, P:2 * P], aggT[:], k.w_proj[:], start=True, stop=True).then_inc(proj_mm, 1)

                def first():
                    for half in range(2):
                        for i in range(4):
                            turn_pixels(0, 0, half, i)
                    prepare_a(0, 0)
                    for i in range(4):
                        turn_pixels(1, 1, 0, i)

                def body(r, slot):
                    more, nxt, prev = known(r, 0, PAIRS - 2), (slot + 1) % RING, (slot - 1) % RING
                    before = known(r, 1, PAIRS)
                    for half in range(2):
                        u = 2 * r + half
                        place = (u - 1, slot, 0) if half else (u - 1, prev, 1)
                        for i in range(4):
                            if half == 0 and i == 1:
                                prepare_b(r, slot)
                            if half and known(r, 0, PAIRS - 3):
                                turn_pixels(r + 2, (slot + 2) % RING, 0, i)
                            if half == 0 and more:
                                turn_pixels(r + 1, nxt, 1, i)
                            if half == 0 and i == 1:
                                queries(r, slot)
                            keys(u, slot, half, i)
                            if half or before:
                                values(*place, i)
                        if before:
                            turn(u - 2)
                        if more and half == 0:
                            prepare_a(r + 1, nxt)
                        if before:
                            project(u - 2)

                def tail():
                    for i in range(4):
                        values(2 * PAIRS - 1, RING - 1, 1, i)
                    for u in (2 * PAIRS - 2, 2 * PAIRS - 1):
                        turn(u)
                        project(u)
                over_pairs(pe, first, body, tail)

            @block.vector
            def _(dve):
                def root_part(r, slot, i):
                    n = [ROOTING * r + (0, 3, 6, 9)[i]]

                    def step(instruction):
                        instruction.then_inc(rooting, 1)
                        n[0] = n[0] + 1
                        dve.wait_ge(rooting, n[0])
                    if i == 0:
                        dve.wait_ge(feat_squared, 4 * r + 4)
                        dve.wait_ge(squared, 64 * r + 64)
                        step(dve.tensor_scalar(var[:], squares[slot % 2][:].rearrange("p g m -> p (g m)"), 1.0 / 64, EPS,
                                               ALU.mult, ALU.add))
                        guess_root(dve, step, var[:], root[:])
                    elif i < NEWTON:
                        step(newton_root(dve, step, var[:], root[:], half_sq[:], root[:]))
                    else:
                        wait(dve, wv_done, 8 * (r - 1))
                        newton_root(dve, step, var[:], root[:], half_sq[:],
                                    rstd[slot % 2][:].rearrange("p g m -> p (g m)")).then_inc(rstd_ready, 1)

                def normalise_means(r, slot):
                    view = "p (g c) -> p g c"
                    dve.wait_ge(rstd_ready, r + 1)
                    wait(dve, q_turned, r)
                    dve.scalar_tensor_tensor(out=q_hat[:].rearrange(view, g=4), in0=q_bank[:, 256:512].rearrange(view, g=4),
                                             scalar=1.0 / 16, in1=spread(rstd[slot % 2][:, 32:34].rearrange("p g m -> p (g m)"), 2, 64),
                                             op0=ALU.mult, op1=ALU.mult).then_inc(q_hat_ready, 1)

                def residual(r, slot):
                    wait(dve, h_ready, 2 * (r - 2) + 2)
                    dve.wait_ge(feat_ready, r + 1)
                    dve.tensor_tensor(feat_c[slot % 2][:].rearrange("p (f m) -> p f m", f=2),
                                      feat[slot % 2][:].rearrange("p (f m) -> p f m", f=2),
                                      spread(k.tok_const[:], 1, 2), ALU.add).then_inc(feat_c_ready, 1)

                def score(u, r, slot, half, i):
                    dve.wait_ge(k_mm, 4 * u + i + 1)
                    dve.tensor_tensor(kq[:, 4 * i:4 * i + 4, :], k_bank[i % 2][:],
                                      spread(q[slot % 2][:, half, :], 1, 4), ALU.mult).then_inc(kq_done, 1)

                def sum_scores(u, half):
                    dve.wait_ge(kq_done, 4 * u + 4)
                    wait(dve, exp_ready, u - 1)
                    dve.tensor_reduce(logit[half][:], kq[:].rearrange("p n (h d) -> p (n h) d", d=8), AX, ALU.add).then_inc(logits_raw, 1)

                def shift(u, r, slot, par):
                    half = par
                    dve.wait_ge(logits_raw, u + 1)
                    dve.wait_ge(rstd_ready, r + 1)
                    rs = rstd[slot % 2][:, 16 * half:16 * half + 16].rearrange("p g m -> p (g m)")
                    dve.tensor_tensor(logit[par][:].rearrange("p (a h) -> p a h", h=8),
                                      logit[par][:].rearrange("p (a h) -> p a h", h=8),
                                      spread(rs, 2, 8), ALU.mult).then_inc(logits_ready, 1)
                    dve.wait_ge(logits_ready, u + 1)
                    dve.tensor_reduce(top[:], logit[par][:].rearrange("p (n g) -> p g n", g=16), AX, ALU.max).then_inc(top_ready, 1)
                    dve.wait_ge(top_ready, u + 1)
                    dve.tensor_tensor(logit[par][:].rearrange("p (n g) -> p n g", g=16),
                                      logit[par][:].rearrange("p (n g) -> p n g", g=16),
                                      spread(top[:], 1, 16), ALU.subtract).then_inc(shifted, 1)

                def weights(u, slot, half):
                    dve.wait_ge(exp_ready, u + 1)
                    wait(dve, wv_done, 4 * u)
                    rs = rstd[slot % 2][:, 16 * half:16 * half + 16].rearrange("p g m -> p (g m)")
                    dve.tensor_tensor(weight[:].rearrange("p (a h) -> p a h", h=8),
                                      expo[half][:].rearrange("p (a h) -> p a h", h=8),
                                      spread(rs, 2, 8), ALU.mult).then_inc(weight_ready, 1)
                    dve.tensor_reduce(denom[:], expo[half][:].rearrange("p (n g) -> p g n", g=16), AX, ALU.add).then_inc(denom_ready, 1)
                    dve.wait_ge(denom_ready, u + 1)
                    dve.reciprocal(inv[half][:], denom[:]).then_inc(inv_ready, 1)
                    dve.wait_ge(weight_ready, u + 1)
                    wait(dve, agg_ready, u - 1)

                def weigh(u, half, i):
                    dve.wait_ge(v_mm, 4 * u + i + 1)
                    dve.tensor_tensor(wv[half][:, 4 * i:4 * i + 4, :].rearrange("p n (h d) -> p (n h) d", d=8),
                                      v_bank[i % 2][:].rearrange("p n (h d) -> p (n h) d", d=8),
                                      spread(weight[:, 64 * i:64 * i + 64], 2, 8), ALU.mult).then_inc(wv_done, 1)

                def normalise(u, half):
                    dve.wait_ge(agg_ready, u + 1)
                    dve.wait_ge(inv_ready, u + 1)
                    wait(dve, agg_turned, u)
                    dve.tensor_tensor(agg_n[:].rearrange("p (g d) -> p g d", d=8),
                                      agg[half][:].rearrange("p (g d) -> p g d", d=8),
                                      spread(inv[half][:], 2, 8), ALU.mult).then_inc(agg_n_ready, 1)

                def finish(u, r, slot, half):
                    dve.wait_ge(proj_mm, u + 1)
                    dve.wait_ge(feat_c_ready, r + 1)
                    dve.tensor_tensor(k.h_tok[:, bass.ds(2 * r, 2), half, :],
                                      a_bank[:, P:2 * P].rearrange("p (m c) -> p m c", m=2),
                                      feat_c[slot % 2][:, P * half:P * half + P].rearrange("p (m c) -> p m c", m=2),
                                      ALU.add).then_inc(h_ready, 1)

                def first():
                    for i in range(4):
                        root_part(0, 0, i)
                    normalise_means(0, 0)
                    residual(0, 0)

                def body(r, slot):
                    more, nxt, prev = known(r, 0, PAIRS - 2), (slot + 1) % RING, (slot - 1) % RING
                    before = known(r, 1, PAIRS)
                    for half in range(2):
                        u = 2 * r + half
                        if half or before:
                            weights(u - 1, slot if half else prev, 1 - half)
                        dve.wait_ge(q_ready, r + 1)
                        for i in range(4):
                            score(u, r, slot, half, i)
                            if half or before:
                                weigh(u - 1, 1 - half, i)
                            if before and i == 2:
                                normalise(u - 2, half)
                            if more and half and i:
                                root_part(r + 1, nxt, i)
                        if more and half:
                            normalise_means(r + 1, nxt)
                        sum_scores(u, half)
                        if more and half == 0:
                            root_part(r + 1, nxt, 0)
                        shift(u, r, slot, half)
                        if before:
                            finish(u - 2, r - 1, prev, half)
                        if more and half:
                            residual(r + 1, nxt)

                def tail():
                    last = PAIRS - 1
                    weights(2 * last + 1, RING - 1, 1)
                    for i in range(4):
                        weigh(2 * last + 1, 1, i)
                    for half in range(2):
                        normalise(2 * last + half, half)
                        finish(2 * last + half, last, RING - 1, half)
                over_pairs(dve, first, body, tail)


def normalise_and_turn(nc, tokens, target_of, stores, var_scale, var_add, k, affine):
    ALL, GROUPS = 192, 24
    chunks, banks = ALL // GROUPS, GROUPS // 8
    with ExitStack() as stack:
        t = Memory(nc, stack, "attn_" if affine else "ffn_")
        stats = t.sb("stats", [P, ALL // 2, 2, 3])
        var, root, half_sq, rstd = (t.sb(n, [P, ALL]) for n in ("var", "root", "half_sq", "rstd"))
        normed = [t.sb(f"normed{i}", [P, GROUPS, 64]) for i in range(2)]
        split = [t.sb(f"split{i}", [P, GROUPS, 2, 64], F16) for i in range(2)]
        bank = [t.ps(f"turn{i}", [P, 8, P], F16) for i in range(2 * banks)]
        stored, measured, rooting, rstd_ready = t.sem("stored"), t.sem("measured"), t.sem("rooting"), t.sem("rstd_ready")
        centred, scaled, weighted, norm_ready = t.sem("centred"), t.sem("scaled"), t.sem("weighted"), t.sem("norm_ready")
        hi_ready, split_ready, turned, moved = t.sem("hi_ready"), t.sem("split_ready"), t.sem("turned"), t.sem("moved")

        def over_chunks(eng, body, tail=None):
            for c in range(2):
                body(c, c)
            with eng.Fori(1, chunks // 2) as g:
                for c in range(2):
                    body(2 * g + c, c)
            if tail:
                tail()

        def started(n):
            return not isinstance(n, int) or n >= 0

        with nc.Block() as block:
            @block.sync
            def _(sp):
                for dst, src in stores:
                    sp.dma_start(dst, src).then_inc(stored, 16)
                sp.wait_ge(stored, 16 * len(stores))

            @block.vector
            def _(dve):
                with dve.Fori(0, chunks) as c:
                    for i in range(GROUPS // 2):
                        dve.bn_stats(stats[:, bass.ds(c * (GROUPS // 2) + i, 1)].rearrange("p g m s -> p (g m s)"),
                                     tokens[:, bass.ds(c * GROUPS + 2 * i, 2), :].rearrange("p m c -> p c m")).then_inc(measured, 1)
                dve.wait_ge(measured, ALL // 2)
                count = [0]

                def step(instruction):
                    instruction.then_inc(rooting, 1)
                    count[0] += 1
                    dve.wait_ge(rooting, count[0])
                step(dve.tensor_scalar(var[:], stats[:, :, :, 2].rearrange("p g m -> p (g m)"), var_scale, var_add,
                                       ALU.mult, ALU.add))
                guess_root(dve, step, var[:], root[:])
                for _ in range(NEWTON - 1):
                    step(newton_root(dve, step, var[:], root[:], half_sq[:], root[:]))
                newton_root(dve, step, var[:], root[:], half_sq[:], rstd[:]).then_inc(rstd_ready, 1)
                dve.wait_ge(rstd_ready, 1)
                means = stats[:].rearrange("p g m s -> p (g m) s")

                def normalise(n, par):
                    z = normed[par]
                    wait(dve, split_ready, n - 1)
                    dve.tensor_tensor(z[:], tokens[:, bass.ds(n * GROUPS, GROUPS), :],
                                      means[:, bass.ds(n * GROUPS, GROUPS), 1:2].to_broadcast([P, GROUPS, 64]),
                                      ALU.subtract).then_inc(centred, 1)
                    dve.wait_ge(centred, n + 1)
                    dve.tensor_tensor(z[:], z[:], rstd[:, bass.ds(n * GROUPS, GROUPS)].unsqueeze(2).to_broadcast([P, GROUPS, 64]),
                                      ALU.mult).then_inc(scaled if affine else norm_ready, 1)
                    if affine:
                        dve.wait_ge(scaled, n + 1)
                        dve.tensor_tensor(z[:], z[:], spread(k.gamma_row[:], 1, GROUPS), ALU.mult).then_inc(weighted, 1)

                def second_part(n, par):
                    dve.wait_ge(hi_ready, n + 1)
                    dve.tensor_tensor(split[par][:, :, 1, :], normed[par][:], split[par][:, :, 0, :],
                                      ALU.subtract).then_inc(split_ready, 1)

                def body(n, par):
                    normalise(n, par)
                    if started(n - 1):
                        second_part(n - 1, 1 - par)
                over_chunks(dve, body, lambda: second_part(chunks - 1, 1))

            if affine:
                @block.gpsimd
                def _(pool):
                    def body(n, par):
                        pool.wait_ge(weighted, n + 1)
                        pool.tensor_tensor(normed[par][:], normed[par][:], spread(k.beta_row[:], 1, GROUPS),
                                           ALU.add).then_inc(norm_ready, 1)
                    over_chunks(pool, body)

            @block.tensor
            def _(pe):
                def body(n, par):
                    pe.wait_ge(split_ready, n + 1)
                    for a in range(banks):
                        wait(pe, moved, banks * (n - 2) + a + 1)
                        for i in range(8):
                            last = pe.transpose(bank[par * banks + a][:, i, :],
                                                split[par][:, 8 * a + i].rearrange("p s c -> p (s c)"), k.ident16[:])
                        last.then_inc(turned, 1)
                over_chunks(pe, body)

            @block.scalar
            def _(act):
                def first_part(n, par):
                    act.wait_ge(norm_ready, n + 1)
                    wait(act, turned, banks * (n - 1))
                    act.activation(split[par][:, :, 0, :], normed[par][:], ACT.Copy).then_inc(hi_ready, 1)

                def move(n, par):
                    for a in range(banks):
                        act.wait_ge(turned, banks * n + a + 1)
                        act.activation(target_of(n, a), bank[par * banks + a][:], ACT.Copy).then_inc(moved, 1)

                def body(n, par):
                    first_part(n, par)
                    if started(n - 1):
                        move(n - 1, 1 - par)
                over_chunks(act, body, lambda: move(chunks - 1, 1))


def tied_scores(nc, zT, h_half, h_source, k):
    with ExitStack() as stack:
        t = Memory(nc, stack)
        qk = [t.sb(f"qk{i}", [P, 2, 2, 64, 32]) for i in range(2)]
        score, top, denom, inv = t.sb("score", [P, 4, 64]), t.sb("stop", [P, 4]), t.sb("sdenom", [P, 4]), t.sb("sinv", [P, 4])
        att2 = t.sb("att2", [P, 4, 64, 2])
        bank = [t.ps(f"qk_bank{i}", [P, 4, 2, 2, 32]) for i in range(4)]
        s_bank = t.ps("score_bank", [P, 4, 2, 64])
        t_bank = [t.ps(f"att_bank{i}", [P, 512]) for i in range(2)]
        projected, moved_a, moved_v, summed = t.sem("projected"), t.sem("moved_a"), t.sem("moved_v"), t.sem("summed")
        vec, exp_ready, att_turned, att_used = t.sem("vec"), t.sem("exp_ready"), t.sem("att_turned"), t.sem("att_used")
        h_loaded = t.sem("h_loaded")
        UNITS = [(g, j) for g in range(4) for j in range(3)]

        def move(eng, u, a, done, op):
            eng.wait_ge(projected, 16 * u + a + 1)
            wait(eng, summed, u - 1)
            for kind in range(2):
                last = op(qk[u % 2][:, kind, :, 4 * a:4 * a + 4, :],
                          bank[a % 4][:, :, kind].rearrange("p s h c -> p h s c"))
            last.then_inc(done, 1)

        with nc.Block() as block:
            @block.sync
            def _(sp):
                sp.dma_start(h_half, h_source).then_inc(h_loaded, 16)
                sp.wait_ge(h_loaded, 16)

            @block.tensor
            def _(pe):
                def project(u, g, j):
                    for s in range(64):
                        a = s // 4
                        if s % 4 == 0:
                            n = 16 * u + a - 4
                            wait(pe, moved_a if a % 2 == 0 else moved_v, n // 2 + 1 if n >= 0 else 0)
                        for part in range(2):
                            last = pe.matmul(bank[a % 4][:, s % 4].rearrange("p k h c -> p (k h c)"),
                                             zT[:, s, P * j:P * j + P], k.w_qk[:, part, P * g:P * g + P],
                                             start=(part == 0), stop=(part == 1))
                        if s % 4 == 3:
                            last.then_inc(projected, 1)

                def score_sums(u, g, j):
                    pe.wait_ge(moved_a, 8 * u + 8)
                    pe.wait_ge(moved_v, 8 * u + 8)
                    q = qk[u % 2][:].rearrange("p k h s c -> p k (h s) c")
                    for c in range(32):
                        last = pe.matmul(s_bank[:, g].rearrange("p h t -> p (h t)"), q[:, 0, :, c], q[:, 1, :, c],
                                         start=(j == 0 and c == 0), stop=(j == 2 and c == 31))
                    last.then_inc(summed, 1)
                for u, (g, j) in enumerate(UNITS):
                    project(u, g, j)
                    if u:
                        score_sums(u - 1, *UNITS[u - 1])
                score_sums(len(UNITS) - 1, *UNITS[-1])
                pe.wait_ge(vec, 6)
                for g in range(4):
                    wait(pe, att_used, g - 1)
                    pe.transpose(t_bank[g % 2][:, 0:P], att2[:, g].rearrange("p t a -> p (t a)"), k.ident[:]).then_inc(att_turned, 1)

            @block.scalar
            def _(act):
                for u in range(len(UNITS)):
                    for a in range(0, 16, 2):
                        move(act, u, a, moved_a, lambda o, i: act.activation(o, i, ACT.Copy, scale=1.0 / 64))
                act.wait_ge(vec, 3)
                act.activation(score[:], score[:], ACT.Exp).then_inc(exp_ready, 1)

            @block.vector
            def _(dve):
                for u in range(len(UNITS)):
                    for a in range(1, 16, 2):
                        move(dve, u, a, moved_v, lambda o, i: dve.tensor_scalar(o, i, 1.0 / 64, None, ALU.mult))
                dve.wait_ge(summed, len(UNITS))
                scale = 32 ** -0.5 * 384 ** -0.5
                for h in range(2):
                    last = dve.tensor_scalar(score[64 * h:64 * h + 64], s_bank[64 * h:64 * h + 64, :, h, :], scale, None, ALU.mult)
                last.then_inc(vec, 1)
                dve.wait_ge(vec, 1)
                dve.tensor_reduce(top[:], score[:], AX, ALU.max).then_inc(vec, 1)
                dve.wait_ge(vec, 2)
                dve.tensor_tensor(score[:], score[:], spread(top[:], 2, 64), ALU.subtract).then_inc(vec, 1)
                dve.wait_ge(exp_ready, 1)
                dve.tensor_reduce(denom[:], score[:], AX, ALU.add).then_inc(vec, 1)
                dve.wait_ge(vec, 4)
                dve.reciprocal(inv[:], denom[:]).then_inc(vec, 1)
                dve.wait_ge(vec, 5)
                for a in range(2):
                    last = dve.tensor_tensor(att2[:, :, :, a], score[:], spread(inv[:], 2, 64), ALU.mult)
                last.then_inc(vec, 1)
                for g in range(4):
                    dve.wait_ge(att_turned, g + 1)
                    for h in range(2):
                        last = dve.tensor_tensor(k.att_blocks[:, 2 * g + h].rearrange("p (s a) -> p s a", a=2),
                                                 spread(t_bank[g % 2][:, 64 * h:64 * h + 64], 2, 2),
                                                 spread(k.parity[:], 1, 64), ALU.mult)
                    last.then_inc(att_used, 1)


def tied_output(nc, zT, h_half, k):
    CH, CHUNKS, PEEL, LAG = 8, 24, 4, 3
    with ExitStack() as stack:
        t = Memory(nc, stack)
        v = [t.sb(f"v{i}", [P, CH, 256]) for i in range(2)]
        gate = [t.sb(f"gate{i}", [P, CH, 256]) for i in range(2)]
        gated = [t.sb(f"gated{i}", [P, CH, 256]) for i in range(2)]
        gatedT = [t.sb(f"gatedT{i}", [P, 4, P]) for i in range(2)]
        v_bank = [t.ps(f"value_bank{i}", [P, 2, 256]) for i in range(2)]
        g_bank = [t.ps(f"gate_bank{i}", [P, 2, 256]) for i in range(2)]
        o_bank = [t.ps(f"o_bank{i}", [P, 2, CH, 32]) for i in range(2)]
        t_bank, r_bank = t.ps("gt_bank", [P, 4, P]), t.ps("r_bank", [P, CH, 64])
        v_mm, g_mm, v_ready = t.sem("v_mm"), t.sem("g_mm"), t.sem("v_ready")
        gate_raw, gate_ready = t.sem("gate_raw"), t.sem("gate_ready")
        mixed, gated_ready, turned, moved = t.sem("mixed"), t.sem("gated_ready"), t.sem("turned"), t.sem("moved")
        out_mm, added, biased = t.sem("out_mm"), t.sem("added"), t.sem("biased")

        def over_chunks(eng, body):
            for n in range(PEEL):
                body(n, n % 2)
            with eng.Fori(PEEL // 2, CHUNKS // 2) as g:
                for n in range(2):
                    body(2 * g + n, n)
            for n in range(CHUNKS, CHUNKS + LAG):
                body(n, n % 2)

        def inside(n):
            return not isinstance(n, int) or 0 <= n < CHUNKS

        zcols = zT[:].rearrange("p b l -> p (b l)").rearrange("p (t l) -> p l t", l=192)
        with nc.Block() as block:
            @block.gpsimd
            def _(pool):
                pool.tensor_tensor(h_half, h_half, spread(k.attn_bo_row[:], 1, 192), ALU.add).then_inc(biased, 1)

            @block.tensor
            def _(pe):
                def project(n, a):
                    for kind, (banks, used, done) in enumerate(((v_bank, v_ready, v_mm), (g_bank, gate_raw, g_mm))):
                        wait(pe, used, 4 * n + a - 1)
                        for i in range(2):
                            for part in range(2):
                                last = pe.matmul(banks[a % 2][:, i], zcols[:, n * CH + 2 * a + i, :],
                                                 k.w_vg[:, part, 256 * kind:256 * kind + 256],
                                                 start=(part == 0), stop=(part == 1))
                        last.then_inc(done, 1)

                def mix(n, par, a):
                    pe.wait_ge(v_ready, 4 * n + 4)
                    wait(pe, gated_ready, 4 * n + a - 1)
                    for h in range(2):
                        head = 2 * a + h
                        last = pe.matmul(o_bank[a % 2][:, h], k.att_blocks[:, head],
                                         v[par][:, :, 32 * head:32 * head + 32], start=True, stop=True)
                    last.then_inc(mixed, 1)

                def turn(n, par, a):
                    pe.wait_ge(gated_ready, 4 * n + 4)
                    wait(pe, moved, 4 * n + a)
                    for i in range(2):
                        for half in range(2):
                            last = pe.transpose(t_bank[:, 2 * i + half],
                                                gated[par][:, 2 * a + i, P * half:P * half + P], k.ident[:])
                    last.then_inc(turned, 1)

                def output(n, a):
                    pe.wait_ge(moved, 4 * n + a + 1)
                    if a == 0:
                        wait(pe, added, n)
                    for i in range(2):
                        for half in range(2):
                            last = pe.matmul(r_bank[:, 2 * a + i], gatedT[a % 2][:, 2 * i + half], k.attn_wo[:, half],
                                             start=(half == 0), stop=(half == 1))
                    last.then_inc(out_mm, 1)

                def body(n, par):
                    for a in range(4):
                        if inside(n):
                            project(n, a)
                        if a == 0 and inside(n - 3):
                            output(n - 3, 3)
                        if a > 0 and inside(n - 2):
                            output(n - 2, a - 1)
                        if inside(n - 2):
                            turn(n - 2, par, a)
                        if inside(n - 1):
                            mix(n - 1, 1 - par, a)
                over_chunks(pe, body)

            @block.scalar
            def _(act):
                def values(n, par, a):
                    act.wait_ge(v_mm, 4 * n + a + 1)
                    wait(act, mixed, 4 * (n - 2) + 4)
                    act.activation(v[par][:, 2 * a:2 * a + 2], v_bank[a % 2][:], ACT.Copy, scale=1.0 / 64).then_inc(v_ready, 1)

                def open_gates(n, par, a):
                    act.wait_ge(gate_raw, 4 * n + a + 1)
                    g = gate[par][:, 2 * a:2 * a + 2]
                    act.activation(g, g, ACT.Sigmoid).then_inc(gate_ready, 1)

                def move(n, a):
                    act.wait_ge(turned, 4 * n + a + 1)
                    wait(act, out_mm, 4 * n + a - 1)
                    act.activation(gatedT[a % 2][:], t_bank[:], ACT.Copy).then_inc(moved, 1)

                def body(n, par):
                    for a in range(4):
                        if inside(n):
                            values(n, par, a)
                        if inside(n - 2):
                            move(n - 2, a)
                        if inside(n):
                            open_gates(n, par, a)
                over_chunks(act, body)

            @block.vector
            def _(dve):
                def bias_gates(n, par, a):
                    dve.wait_ge(g_mm, 4 * n + a + 1)
                    wait(dve, gated_ready, 4 * (n - 2) + 4)
                    dve.scalar_tensor_tensor(out=gate[par][:, 2 * a:2 * a + 2], in0=g_bank[a % 2][:], scalar=1.0 / 64,
                                             in1=spread(k.bg_row[:], 1, 2), op0=ALU.mult, op1=ALU.add).then_inc(gate_raw, 1)

                def multiply(n, par, a):
                    dve.wait_ge(gate_ready, 4 * n + 4)
                    wait(dve, turned, 4 * (n - 2) + 4)
                    dve.wait_ge(mixed, 4 * n + a + 1)
                    view = "p i (h c) -> p h i c"
                    dve.tensor_tensor(gated[par][:, :, 64 * a:64 * a + 64].rearrange(view, h=2), o_bank[a % 2][:],
                                      gate[par][:, :, 64 * a:64 * a + 64].rearrange(view, h=2), ALU.mult).then_inc(gated_ready, 1)

                def add(n):
                    dve.wait_ge(out_mm, 4 * n + 4)
                    dve.wait_ge(biased, 1)
                    dve.tensor_tensor(h_half[:, bass.ds(n * CH, CH), :], h_half[:, bass.ds(n * CH, CH), :], r_bank[:],
                                      ALU.add).then_inc(added, 1)

                def body(n, par):
                    for a in range(4):
                        if inside(n):
                            bias_gates(n, par, a)
                        if a == 0 and inside(n - 3):
                            add(n - 3)
                        if inside(n - 1):
                            multiply(n - 1, 1 - par, a)
                over_chunks(dve, body)


def feed_forward(nc, zT, h_dram, out, k):
    B, L, RING = 64, 384, 4
    with ExitStack() as stack:
        t = Memory(nc, stack)
        w_sel = [t.sb(f"w_sel{i}", [P, 2, P + 1]) for i in range(RING)]
        hid = [[t.sb(f"hid{n}_{i}", [P, L]) for i in range(2)] for n in range(3)]
        res = [t.sb(f"res{i}", [P, 3, 64]) for i in range(RING)]
        final = [t.sb(f"final{i}", [P, 3, 64]) for i in range(RING)]
        bank = [[t.ps(f"ff_bank{n}_{i}", [P, 512]) for i in range(2)] for n in range(4)]
        selected, res_ready = t.sem("selected"), [t.sem(f"res_ready{i}") for i in range(RING)]
        mm = [t.sem(f"mm{n}") for n in range(4)]
        relu = [t.sem(f"relu{n}") for n in range(3)]
        res_biased, final_ready, stored = t.sem("res_biased"), t.sem("final_ready"), [t.sem(f"stored{i}") for i in range(RING)]

        def count(semaphore_step, b, slot):
            if isinstance(b, int):
                return semaphore_step * (b // RING + 1)
            return (b - slot) * (semaphore_step // RING) + semaphore_step

        def over_rows(eng, body, skew):
            for s in range(2 * RING):
                body(s, s % RING)
            with eng.Fori(2, B // RING) as g:
                for s in range(RING):
                    body(g * RING + s, s)
            for s in range(skew):
                body(B + s, s)

        def inside(b):
            return not isinstance(b, int) or 0 <= b < B

        with nc.Block() as block:
            @block.gpsimd
            def _(pool):
                experts = k.w_exp[:].rearrange("p (l e) c -> p l e c", l=2)

                def body(b, slot):
                    wait(pool, relu[2], b - RING + 1)
                    e = pool.value_load(k.route[0:1, bass.ds(b, 1)], min_val=0, max_val=15)
                    pool.tensor_copy(w_sel[slot][:].unsqueeze(2), experts[:, :, bass.ds(e, 1), :]).then_inc(selected, 1)
                over_rows(pool, body, 0)

            @block.sync
            def _(sp):
                def store(b, slot):
                    wait(sp, final_ready, b + 1)
                    sp.dma_start(out[b].rearrange("(j p) c -> p j c", p=P), final[slot][:]).then_inc(stored[slot], 16)

                def body(b, slot):
                    if inside(b):
                        wait(sp, final_ready, b - RING + 1)
                        sp.dma_start(res[slot][:], h_dram[b].rearrange("(j p) c -> p j c", p=P)).then_inc(res_ready[slot], 16)
                    if inside(b - 3):
                        store(b - 3, (slot - 3) % RING)
                over_rows(sp, body, 3)
                for s in range(RING):
                    sp.wait_ge(stored[s], 16 * (B // RING))

            @block.tensor
            def _(pe):
                def layer(n, b, slot):
                    par = slot % 2
                    dst = bank[n][par]
                    if n < 3:
                        wait(pe, relu[n], b - 1)
                    else:
                        wait(pe, final_ready, b - 1)
                    if n == 0:
                        tokens = zT.rearrange("p l (b a) -> p b a l", a=2)[:, bass.ds(b, 1)]
                        for part, weights in enumerate((k.wi_hi, k.wi_lo)):
                            last = pe.matmul(dst[:, 0:L].rearrange("p (o a l) -> p o a l", o=1, a=2), weights[:], tokens,
                                             start=(part == 0), stop=(part == 1))
                    elif n < 3:
                        pe.wait_ge(relu[n - 1], b + 1)
                        pe.wait_ge(selected, b + 1)
                        last = pe.matmul(dst[:, 0:L], w_sel[slot][:, n - 1, 0:P], hid[n - 1][par][:], start=True, stop=True)
                    else:
                        pe.wait_ge(relu[2], b + 1)
                        for j in range(3):
                            last = pe.matmul(dst[:, 64 * j:64 * j + 64], hid[2][par][:, P * j:P * j + P], k.ffn_wo[:],
                                             start=True, stop=True)
                    last.then_inc(mm[n], 1)

                def body(b, slot):
                    for n in (3, 2, 1, 0):
                        if inside(b - n):
                            layer(n, b - n, (slot - n) % RING)
                over_rows(pe, body, 3)

            @block.scalar
            def _(act):
                def relu_of(n, b, slot):
                    par = slot % 2
                    act.wait_ge(mm[n], b + 1)
                    wait(act, mm[n + 1], b - 1)
                    bias = k.bi[:, 0:1] if n == 0 else w_sel[slot][:, n - 1, P:P + 1]
                    act.activation(hid[n][par][:], bank[n][par][:, 0:L], ACT.Relu, bias=bias,
                                   scale=1.0 / 64 if n == 0 else 1.0).then_inc(relu[n], 1)

                def body(b, slot):
                    for n in (2, 0):
                        if inside(b - n):
                            relu_of(n, b - n, (slot - n) % RING)
                over_rows(act, body, 2)

            @block.vector
            def _(dve):
                def hidden(b, slot):
                    par = slot % 2
                    dve.wait_ge(mm[1], b + 1)
                    wait(dve, mm[2], b - 1)
                    dve.tensor_scalar(hid[1][par][:], bank[1][par][:, 0:L], w_sel[slot][:, 0, P:P + 1], 0.0,
                                      ALU.add, ALU.max).then_inc(relu[1], 1)

                def finish(b, slot):
                    dve.wait_ge(res_ready[slot], count(16, b, slot))
                    dve.tensor_tensor(res[slot][:], res[slot][:], spread(k.ffn_bo_row[:], 1, 3), ALU.add).then_inc(res_biased, 1)
                    dve.wait_ge(res_biased, b + 1)
                    dve.wait_ge(mm[3], b + 1)
                    if inside(b - RING):
                        dve.wait_ge(stored[slot], count(16, b, slot) - 16)
                    dve.tensor_tensor(final[slot][:], bank[3][slot % 2][:, 0:192].rearrange("p (j c) -> p j c", j=3),
                                      res[slot][:], ALU.add).then_inc(final_ready, 1)

                def body(b, slot):
                    for n, step in ((3, finish), (1, hidden)):
                        if inside(b - n):
                            step(b - n, (slot - n) % RING)
                over_rows(dve, body, 3)


class Kept:

    def __init__(self, m):
        sb = m.sb
        self.ident, self.ident16, self.parity = sb("ident", [P, P]), sb("ident16", [P, P], F16), sb("parity", [P, 2])
        self.centre = sb("centre", [P, P])
        self.w_k, self.w_v, self.w_q, self.w_proj = (sb(n, [P, P]) for n in ("w_k", "w_v", "w_q", "w_proj"))
        self.lnq_w, self.lnq_b, self.bi = sb("lnq_w", [P, 1]), sb("lnq_b", [P, 1]), sb("bi", [P, 1])
        self.tok_const = sb("tok_const", [P, P])
        self.gamma_row, self.beta_row = sb("gamma_row", [P, 64]), sb("beta_row", [P, 64])
        self.attn_bo_row, self.ffn_bo_row = sb("attn_bo_row", [P, 64]), sb("ffn_bo_row", [P, 64])
        self.bg_row, self.attn_wo = sb("bg_row", [P, 256]), sb("attn_wo", [P, 2, 64])
        self.w_qk, self.w_vg = sb("w_qk", [P, 2, 512], F16), sb("w_vg", [P, 2, 512], F16)
        self.wi_hi, self.wi_lo, self.ffn_wo = sb("wi_hi", [P, P], F16), sb("wi_lo", [P, P], F16), sb("ffn_wo", [P, 64])
        self.w_exp = sb("w_exp", [P, 32, P + 1])
        self.route = sb("route", [1, 64], I32)


def early_fusion(nc, x, w, out):
    B, L, C = 64, 384, 64
    h_dram = nc.dram_tensor("h_scratch", (B, L, C), F32, kind="Internal").ap()
    h2_dram = nc.dram_tensor("h2_scratch", (B, L, C), F32, kind="Internal").ap()
    halves = "b (a l) c -> (b a) l c"
    with ExitStack() as outer:
        m = Memory(nc, outer)
        k = Kept(m)
        tokens_buffer = m.sb("tokens_buffer", [P, B * L * C // P])
        k.h_tok = tokens_buffer[:].rearrange("p (b j c) -> p b j c", j=3, c=C)
        h_half = tokens_buffer[:].rearrange("p (l c) -> p l c", c=C)
        setup_weights(nc, m, w, k)
        local_attention(nc, x, k)
        zT = m.sb("zT", [P, B, L], F16)
        k.att_blocks = m.sb("att_blocks", [P, 8, P])
        tokens = k.h_tok.rearrange("p b j c -> p (b j) c")
        columns = zT[:].rearrange("p b (j t) -> p (b j) t", j=3)
        stores = [(h_dram[:, P * j:P * j + P, :].rearrange("b t c -> t b c"), k.h_tok[:, :, j, :]) for j in range(3)]
        normalise_and_turn(nc, tokens, lambda n, a: columns[:, bass.ds(n * 24 + 8 * a, 8), :],
                           stores, (1 + EPS) / C, EPS * EPS, k, True)
        tied_scores(nc, zT, h_half, h_dram.rearrange(halves, a=2), k)
        tied_output(nc, zT, h_half, k)
        z2 = zT[:].rearrange("p b l -> p (b l)").rearrange("p (l t) -> p l t", t=P)
        normalise_and_turn(nc, h_half, lambda n, a: z2[:, bass.ds(n * 24 + 8 * a, 8), :],
                           [(h2_dram.rearrange(halves, a=2), h_half)], 1.0 / C, EPS, k, False)
        feed_forward(nc, z2, h2_dram, out, k)


_OUT = (64, 384, 64)


def kernel(**inputs):
    from concourse import bacc
    from concourse.bass_utils import run_bass_kernel_spmd

    nc = bacc.Bacc("TRN2", target_bir_lowering=False, num_devices=1)
    arrays, weights = {}, {}
    for name, value in inputs.items():
        a = np.ascontiguousarray(value)
        arrays[f"in_{name}"] = a
        ap = nc.dram_tensor(f"in_{name}", a.shape, mybir.dt.from_np(a.dtype), kind="ExternalInput").ap()
        weights[name[3:] if name.startswith("L0_") else name] = ap
    out = nc.dram_tensor("out", _OUT, F32, kind="ExternalOutput").ap()
    x = weights.pop("x")
    early_fusion(nc, x, weights, out)
    return run_bass_kernel_spmd(nc, [arrays], core_ids=[0]).results[0]["out"]
```

```python
from contextlib import ExitStack

import numpy as np

import concourse.bass as bass
from concourse import mybir

ALU = mybir.AluOpType
ACT = mybir.ActivationFunctionType
AX = mybir.AxisListType.X
F32 = mybir.dt.float32
F16 = mybir.dt.float16
I32 = mybir.dt.int32
NEWTON = 3
ROOT_STEPS = 3 * NEWTON + 1
PAIRS, RING = 32, 4

P = 128
EPS = 1e-5


def wait(eng, semaphore, value):
    if isinstance(value, int) and value <= 0:
        return
    eng.wait_ge(semaphore, value)


def spread(ap, axis, count):
    ap = ap.unsqueeze(axis)
    shape = list(ap.shape)
    shape[axis] = count
    return ap.to_broadcast(shape)


def guess_root(dve, step, var, root):
    step(dve.tensor_scalar(root.bitcast(I32), var.bitcast(I32), 1, None, ALU.logical_shift_right))
    step(dve.tensor_scalar(root.bitcast(I32), root.bitcast(I32), -1.0, float(0x5F3759DF), ALU.mult, ALU.add))


def newton_root(dve, step, var, root, half_sq, out):
    step(dve.scalar_tensor_tensor(out=half_sq, in0=root, scalar=-0.5, in1=root, op0=ALU.mult, op1=ALU.mult))
    step(dve.tensor_tensor(half_sq, half_sq, var, ALU.mult))
    return dve.scalar_tensor_tensor(out=out, in0=half_sq, scalar=1.5, in1=root, op0=ALU.add, op1=ALU.mult)


class Memory:

    def __init__(self, nc, stack, prefix=""):
        self.nc, self.stack, self.prefix = nc, stack, prefix

    def sb(self, name, shape, dtype=F32):
        return self.stack.enter_context(self.nc.sbuf_tensor(self.prefix + name, shape, dtype))

    def ps(self, name, shape, dtype=F32):
        return self.stack.enter_context(self.nc.psum_tensor(self.prefix + name, shape, dtype))

    def sem(self, name):
        return self.stack.enter_context(self.nc.semaphore(self.prefix + name))


def load_pair(eng, x, k, r, slot):
    pair = x.rearrange("(r b) c (h i) w -> r (b c) i h w", b=2, i=4)[r]
    for i in range(4):
        eng.dma_start(k.x_pair[slot][:, i, :].rearrange("p (h w) -> p h w", h=16), pair[:, i]).then_inc(k.x_loaded[slot], 16)


def setup_weights(nc, x, w, k):
    with ExitStack() as stack:
        t = Memory(nc, stack)
        C = 64
        wkv = t.sb("wkv", [P, C])
        wv = t.sb("wv", [C, C])
        wq2 = t.sb("wq2", [C, 2, C])
        proj2 = t.sb("proj2", [C, 2, C])
        kvw_row = t.sb("kvw_row", [P, C])
        kvb_row = t.sb("kvb_row", [C, C])
        wkv_sum = t.sb("wkv_sum", [P, 1])
        wkv2 = t.sb("wkv2", [P, 2, C])
        wvb = t.sb("wvb", [C, C])
        vbias = t.sb("vbias", [C, 1])
        ones = t.sb("ones", [C, P])
        vbias_cols = t.sb("vbias_cols", [C, P])
        projT = t.sb("projT", [C, C])
        projb_row = t.sb("projb_row", [P, C])
        qkvg = t.sb("qkvg", [P, 4, 256])
        qkvg_s = t.sb("qkvg_s", [P, 1024])
        brs = t.sb("brs", [32, P])
        bss = t.sb("bss", [32, P])
        wi = t.sb("wi", [P, 2, C])
        wi_s = t.sb("wi_s", [P, P])
        wo_nat = t.sb("wo_nat", [C, P])
        bank = [t.ps(f"sbank{i}", [P, 512]) for i in range(2)]
        loaded, zeroed, made = t.sem("loaded"), t.sem("zeroed"), t.sem("made")
        vec, product, moved = t.sem("vec"), t.sem("product"), t.sem("moved")
        n_loads = [0]

        with nc.Block() as block:
            @block.sync
            def _(sp):
                def load(dst, src):
                    sp.dma_start(dst, src).then_inc(loaded, 16)
                    n_loads[0] += 16
                load(wkv[:], w["tok_Wkv"])
                load(wv[:], w["tok_Wkv"][C:2 * C, :])
                load(wq2[:], spread(w["tok_Wq"], 1, 2))
                load(proj2[:], spread(w["tok_proj_w"], 1, 2))
                load(wi[:], spread(w["ffn_Wi"], 1, 2))
                for d in range(2):
                    load(k.lnq_w[d * C:(d + 1) * C, :], w["tok_ln_q_w"].unsqueeze(1))
                    load(k.lnq_b[d * C:(d + 1) * C, :], w["tok_ln_q_b"].unsqueeze(1))
                    for n, name in enumerate(("attn_Wq", "attn_Wk", "attn_Wv", "attn_Wg")):
                        load(qkvg[d * C:(d + 1) * C, n, :], w[name])
                load(kvw_row[:], w["tok_ln_kv_w"].partition_broadcast(P))
                load(kvb_row[:], w["tok_ln_kv_b"].partition_broadcast(C))
                load(projb_row[:], w["tok_proj_b"].partition_broadcast(P))
                load(brs[:], w["ffn_br"].rearrange("l e o -> (l e) o"))
                for n in range(2):
                    load(bss[16 * n:16 * n + 16, :], w["ffn_bs"][n, 0].partition_broadcast(16))
                load(wo_nat[:], w["ffn_Wo"])

            @block.scalar
            def _(act):
                load_pair(act, x, k, 0, 0)
                act.wait_ge(loaded, n_loads[0])
                load_pair(act, x, k, 1, 1)

            @block.gpsimd
            def _(pool):
                clear = [(k.ident, 0.0), (k.parity, 0.0), (k.centre, 0.0), (k.w_k, 0.0), (k.w_v, 0.0),
                         (k.w_q, 0.0), (k.w_proj, 0.0), (ones, 1.0)]
                for tile, value in clear:
                    pool.memset(tile[:], value).then_inc(zeroed, 1)
                pool.wait_ge(zeroed, len(clear))
                pool.affine_select(out=k.ident[:], in_=k.ident[:], compare_op=ALU.not_equal, fill=1.0,
                                   base=0, pattern=[[-1, P]], channel_multiplier=1).then_inc(made, 1)
                pool.wait_ge(made, 1)
                pool.tensor_copy(k.ident16[:], k.ident[:]).then_inc(made, 1)

            steps = [0]

            @block.vector
            def _(dve):
                def step(instruction):
                    steps[0] += 1
                    instruction.then_inc(vec, 1)
                    dve.wait_ge(vec, steps[0])
                dve.wait_ge(made, 2)
                for img in range(2):
                    step(dve.memset(k.centre[64 * img:64 * img + 64, 64 * img:64 * img + 64], -1.0 / C))
                step(dve.tensor_tensor(k.centre[:], k.centre[:], k.ident[:], ALU.add))
                step(dve.tensor_reduce(k.parity[:], k.ident[:].rearrange("p (t a) -> p a t", a=2), AX, ALU.add))
                dve.wait_ge(loaded, n_loads[0])
                step(dve.tensor_tensor(wkv[:], wkv[:], kvw_row[:], ALU.mult))
                step(dve.tensor_reduce(wkv_sum[:], wkv[:], AX, ALU.add))
                step(dve.tensor_scalar(wkv_sum[:], wkv_sum[:], -1.0 / C, None, ALU.mult))
                for d in range(2):
                    step(dve.tensor_scalar(wkv2[:, d, :], wkv[:], wkv_sum[:, 0:1], None, ALU.add))
                step(dve.tensor_tensor(wvb[:], wv[:], kvb_row[:], ALU.mult))
                step(dve.tensor_reduce(vbias[:], wvb[:], AX, ALU.add))
                step(dve.tensor_scalar(vbias_cols[:], ones[:], vbias[:, 0:1], None, ALU.mult))
                step(dve.tensor_scalar(qkvg_s[:], qkvg[:].rearrange("p a b -> p (a b)"), 64.0, None, ALU.mult))
                split = [(k.w_qk[:, 0].rearrange("p (g a h c) -> p a g h c", g=4, a=2, h=2)[:, n],
                          k.w_qk[:, 1].rearrange("p (g a h c) -> p a g h c", g=4, a=2, h=2)[:, n],
                          qkvg_s[:, 256 * n:256 * n + 256].rearrange("p (g h c) -> p g h c", g=4, h=2))
                         for n in range(2)]
                split.append((k.w_vg[:, 0], k.w_vg[:, 1], qkvg_s[:, 512:1024]))
                for hi, lo, whole in split:
                    step(dve.tensor_copy(hi, whole))
                    step(dve.tensor_tensor(lo, whole, hi, ALU.subtract))
                step(dve.tensor_tensor(brs[:], brs[:], bss[:], ALU.add))

                def copy(n, dst, src, scale=1.0):
                    dve.wait_ge(product, n + 1)
                    dve.tensor_scalar(dst, src, scale, None, ALU.mult).then_inc(moved, 1)

                def halves(n, dst, src_of, scale=1.0):
                    dve.wait_ge(product, n + 1)
                    dve.tensor_scalar(dst[0:64, 0:64], src_of(0), scale, None, ALU.mult)
                    dve.tensor_scalar(dst[64:128, 64:128], src_of(1), scale, None, ALU.mult).then_inc(moved, 1)
                dve.wait_ge(product, 1)
                for j, dst in enumerate((k.w_k, k.w_v)):
                    dve.tensor_copy(dst[0:64, 0:64], bank[0][0:64, 64 * j:64 * j + 64])
                    last = dve.tensor_copy(dst[64:128, 64:128], bank[0][64:128, 64 * j:64 * j + 64])
                last.then_inc(moved, 1)
                halves(1, k.w_q, lambda i: bank[1][64 * i:64 * i + 64, 0:64], C ** -0.5)
                halves(2, k.w_proj, lambda i: bank[0][64 * i:64 * i + 64, 0:64])
                dve.wait_ge(product, 4)
                dve.tensor_copy(projT[:], bank[1][0:64, 0:64]).then_inc(moved, 1)
                dve.wait_ge(product, 5)
                for half in range(2):
                    last = dve.tensor_tensor(k.tok_const[:, 64 * half:64 * half + 64], bank[0][:, 0:64],
                                             projb_row[:], ALU.add)
                last.then_inc(moved, 1)
                dve.wait_ge(product, 6)
                dve.tensor_scalar(wi_s[:], bank[1][:, 0:128], 64.0, None, ALU.mult).then_inc(moved, 1)
                dve.wait_ge(moved, 6)
                step(dve.tensor_copy(k.wi_hi[:], wi_s[:]))
                step(dve.tensor_tensor(k.wi_lo[:], wi_s[:], k.wi_hi[:], ALU.subtract))
                copy(6, k.ffn_wo[:], bank[0][:, 0:64])
                copy(7, k.w_exp[:, :, P], bank[1][:, 0:32])

            @block.tensor
            def _(pe):
                pe.wait_ge(made, 2)
                pe.wait_ge(vec, steps[0] - 2)
                n = [0]

                def start():
                    if n[0] >= 2:
                        pe.wait_ge(moved, n[0] - 1)
                    n[0] += 1
                    return bank[(n[0] - 1) % 2]
                pe.transpose(start()[:, 0:128], wkv2[:].rearrange("p a b -> p (a b)"), k.ident[:]).then_inc(product, 1)
                for src in (wq2, proj2, proj2):
                    pe.transpose(start()[:, 0:64], src[:].rearrange("p a b -> p (a b)"),
                                 k.ident[0:64, 0:64]).then_inc(product, 1)
                b = start()
                pe.wait_ge(moved, 4)
                pe.matmul(b[:, 0:64], vbias_cols[:], projT[:], start=True, stop=True).then_inc(product, 1)
                pe.transpose(start()[:, 0:128], wi[:].rearrange("p a b -> p (a b)"), k.ident[:]).then_inc(product, 1)
                pe.transpose(start()[:, 0:64], wo_nat[:], k.ident[0:64, 0:64]).then_inc(product, 1)
                pe.transpose(start()[:, 0:32], brs[:], k.ident[0:32, 0:32]).then_inc(product, 1)


def local_attention(nc, x, w, k):
    ROOTING = ROOT_STEPS + 1
    with ExitStack() as stack:
        t = Memory(nc, stack)
        x_pair, x_loaded = k.x_pair, k.x_loaded
        f1, f2 = t.sb("f1", [P, 512]), t.sb("f2", [P, P, 2])
        feat_ch = [t.sb(f"feat_ch{i}", [P, 2, P]) for i in range(2)]
        squares, var = [t.sb(f"squares{i}", [P, 34, 2]) for i in range(2)], t.sb("var", [P, 68])
        mean_sq = t.sb("mean_sq", [P, 4, 64])
        root, half_sq = t.sb("root", [P, 68]), t.sb("half_sq", [P, 68])
        rstd = [t.sb(f"rstd{i}", [P, 34, 2]) for i in range(2)]
        feat = [t.sb(f"feat{i}", [P, 256]) for i in range(2)]
        feat_c = [t.sb(f"feat_c{i}", [P, 256]) for i in range(2)]
        q_hat, q_hatT = t.sb("q_hat", [P, 256]), t.sb("q_hatT", [P, 256])
        q = [t.sb(f"q{i}", [P, 2, P]) for i in range(2)]
        kq = t.sb("kq", [P, 16, P])
        logit = [t.sb(f"logit{i}", [P, 256]) for i in range(2)]
        expo = [t.sb(f"expo{i}", [P, 256]) for i in range(2)]
        top = t.sb("top", [P, 16])
        weight = t.sb("weight", [P, 256])
        denom = t.sb("denom", [P, 16])
        inv = [t.sb(f"inv{i}", [P, 16]) for i in range(2)]
        wv = [t.sb(f"wv{i}", [P, 16, P]) for i in range(2)]
        agg = [t.sb(f"agg{i}", [P, P]) for i in range(2)]
        agg_n, aggT = t.sb("agg_n", [P, P]), t.sb("aggT", [P, P])
        k_bank = [t.ps(f"k_bank{i}", [P, 4, P]) for i in range(2)]
        v_bank = [t.ps(f"v_bank{i}", [P, 4, P]) for i in range(2)]
        x_bank = [t.ps(f"x_bank{i}", [P, 4, 2, 64]) for i in range(2)]
        q_bank, a_bank = t.ps("q_bank", [P, 512]), t.ps("a_bank", [P, 512])

        text_loaded, rest_loaded, measured = t.sem("text_loaded"), t.sem("rest_loaded"), t.sem("measured")
        feat_part, feat_done, x_turned, squared = t.sem("feat_part"), t.sem("feat_done"), t.sem("x_turned"), t.sem("squared")
        feat_turned, feat_ready, feat_squared = t.sem("feat_turned"), t.sem("feat_ready"), t.sem("feat_squared")
        rooting, rstd_ready = t.sem("rooting"), t.sem("rstd_ready")
        q_hat_ready, q_turned, q_hatT_ready = t.sem("q_hat_ready"), t.sem("q_turned"), t.sem("q_hatT_ready")
        q_mm, q_ready, feat_c_ready = t.sem("q_mm"), t.sem("q_ready"), t.sem("feat_c_ready")
        k_mm, kq_done, logits_raw, logits_ready = t.sem("k_mm"), t.sem("kq_done"), t.sem("logits_raw"), t.sem("logits_ready")
        top_ready, shifted, exp_ready = t.sem("top_ready"), t.sem("shifted"), t.sem("exp_ready")
        weight_ready, denom_ready, inv_ready = t.sem("weight_ready"), t.sem("denom_ready"), t.sem("inv_ready")
        v_mm, wv_done, agg_part, agg_ready = t.sem("v_mm"), t.sem("wv_done"), t.sem("agg_part"), t.sem("agg_ready")
        agg_n_ready, agg_turned, aggT_ready = t.sem("agg_n_ready"), t.sem("agg_turned"), t.sem("aggT_ready")
        proj_mm, h_ready = t.sem("proj_mm"), t.sem("h_ready")

        def over_pairs(eng, first, body, tail):
            first()
            for slot in range(RING):
                body(slot, slot)
            with eng.Fori(1, PAIRS // RING - 1) as g:
                for slot in range(RING):
                    body(g * RING + slot, slot)
            for slot in range(RING):
                body(PAIRS - RING + slot, slot)
            tail()

        def known(r, least, most):
            return not isinstance(r, int) or least <= r <= most

        with nc.Block() as block:
            @block.sync
            def _(sp):
                def load(r, slot):
                    if known(r, RING, PAIRS):
                        sp.wait_ge(feat_turned, r - 1)
                    if known(r, 2, PAIRS):
                        load_pair(sp, x, k, r, slot)

                def rest():
                    sp.dma_start(k.h_tok[:, :, 2, :], w["txt"].rearrange("b t c -> t b c")).then_inc(text_loaded, 16)
                    sp.dma_start(k.w_exp[:, :, 0:P], w["ffn_Wr"].rearrange("l e o i -> o (l e) i")).then_inc(k.experts_loaded, 16)
                    as_they_are = [(k.gamma_row[:], w["attn_gamma"].partition_broadcast(P)),
                                   (k.beta_row[:], w["attn_beta"].partition_broadcast(P)),
                                   (k.bg_row[:], w["attn_bg"].partition_broadcast(P)),
                                   (k.attn_bo_row[:], w["attn_bo"].partition_broadcast(P)),
                                   (k.ffn_bo_row[:], w["ffn_bo"].partition_broadcast(P)),
                                   (k.attn_wo[:], w["attn_Wo"].rearrange("(k p) c -> p k c", k=2)),
                                   (k.w_shared[:], w["ffn_Ws"].rearrange("l s o i -> o (l s) i")),
                                   (k.bi[:], w["ffn_bi"].unsqueeze(1)),
                                   (k.route[:], w["ffn_route_id"].unsqueeze(0))]
                    for dst, src in as_they_are:
                        sp.dma_start(dst, src).then_inc(rest_loaded, 16)
                    sp.wait_ge(rest_loaded, 16 * len(as_they_are))
                over_pairs(sp, lambda: None, load, rest)

            def loaded(eng, r, slot):
                if isinstance(r, int):
                    eng.wait_ge(x_loaded[slot], 64 * (r // RING + 1))
                else:
                    eng.wait_ge(x_loaded[slot], (r - slot) * (64 // RING) + 64)

            @block.gpsimd
            def _(pool):
                def features(r, slot, half):
                    u = 2 * r + half
                    loaded(pool, r, slot)
                    xp = x_pair[slot][:, :, 512 * half:512 * half + 512]
                    wait(pool, feat_done, u)
                    pool.tensor_tensor(f1[:], xp[:, 0, :], xp[:, 1, :], ALU.add).then_inc(feat_part, 1)
                    for i in (2, 3):
                        pool.wait_ge(feat_part, 4 * u + i - 1)
                        pool.tensor_tensor(f1[:], f1[:], xp[:, i, :], ALU.add).then_inc(feat_part, 1)
                    pool.wait_ge(feat_part, 4 * u + 3)
                    f = f1[:].rearrange("p (t j) -> p t j", j=4)
                    pool.tensor_tensor(f2[:], f[:, :, 0:2], f[:, :, 2:4], ALU.add).then_inc(feat_part, 1)
                    pool.wait_ge(feat_part, 4 * u + 4)
                    wait(pool, feat_turned, r - 1)
                    pool.tensor_tensor(feat_ch[slot % 2][:, half, :], f2[:, :, 0], f2[:, :, 1], ALU.add).then_inc(feat_done, 1)

                def sum_pixels(u, par):
                    wait(pool, wv_done, 4 * u + 4)
                    w = wv[par]
                    for n, half in enumerate((8, 4, 2)):
                        pool.tensor_tensor(w[:, 0:half], w[:, 0:half], w[:, half:2 * half], ALU.add).then_inc(agg_part, 1)
                        pool.wait_ge(agg_part, 3 * u + n + 1)
                    wait(pool, agg_n_ready, u - 1)
                    pool.tensor_tensor(agg[par][:], w[:, 0], w[:, 1], ALU.add).then_inc(agg_ready, 1)

                def first():
                    for r in range(2):
                        for half in range(2):
                            features(r, r, half)

                def body(r, slot):
                    more = known(r, 0, PAIRS - 3)
                    if more:
                        features(r + 2, (slot + 2) % RING, 0)
                    if known(r, 1, PAIRS):
                        sum_pixels(2 * r - 1, 1)
                    if more:
                        features(r + 2, (slot + 2) % RING, 1)
                    sum_pixels(2 * r, 0)
                over_pairs(pool, first, body, lambda: sum_pixels(2 * PAIRS - 1, 1))

            @block.scalar
            def _(act):
                def copy(dst, src, after, count, done, scale=1.0):
                    act.wait_ge(after, count)
                    act.activation(dst, src, ACT.Copy, scale=scale).then_inc(done, 1)

                def square_pixels(r, slot, half, i):
                    step = 8 * r + 4 * half + i
                    act.wait_ge(x_turned, step + 1)
                    if half == 0 and i == 0:
                        wait(act, rooting, ROOTING * (r - 2) + 1)
                    for j in range(4):
                        for img in range(2):
                            group = 16 * half + 4 * i + j
                            act.activation(x_bank[i % 2][:, j, img], x_bank[i % 2][:, j, img], ACT.Square,
                                           accum_out=squares[slot % 2][:, group, img:img + 1]).then_inc(squared, 1)

                def patch_means(r, slot):
                    wait(act, feat_c_ready, r - 1)
                    copy(feat[slot % 2][:], q_bank[:, 0:256], feat_turned, r + 1, feat_ready, 1.0 / 16)
                    wait(act, feat_squared, 4 * r)
                    for n in range(4):
                        act.activation(mean_sq[:, n], q_bank[:, 256 + 64 * n:320 + 64 * n], ACT.Square, scale=1.0 / 16,
                                       accum_out=squares[slot % 2][:, 32 + n // 2, n % 2:n % 2 + 1]).then_inc(feat_squared, 1)

                def affine_means(r):
                    act.wait_ge(q_turned, r + 1)
                    act.activation(q_hatT[:], q_bank[:, 0:256], ACT.Identity, bias=k.lnq_b[:, 0:1],
                                   scale=k.lnq_w[:, 0:1]).then_inc(q_hatT_ready, 1)

                def move_queries(r, slot):
                    wait(act, kq_done, 8 * (r - 2) + 8)
                    copy(q[slot % 2][:].rearrange("p a b -> p (a b)"), q_bank[:, 256:512], q_mm, r + 1, q_ready)

                def exponential(u, par):
                    act.wait_ge(shifted, u + 1)
                    act.activation(expo[par][:], logit[par][:], ACT.Exp).then_inc(exp_ready, 1)

                def turned(u):
                    copy(aggT[:], a_bank[:, 0:128], agg_turned, u + 1, aggT_ready)

                def first():
                    for half in range(2):
                        for i in range(4):
                            square_pixels(0, 0, half, i)
                    patch_means(0, 0)
                    for i in range(4):
                        square_pixels(1, 1, 0, i)

                def body(r, slot):
                    more = known(r, 0, PAIRS - 2)
                    before = known(r, 1, PAIRS)
                    for half in range(2):
                        u = 2 * r + half
                        for i in range(4):
                            if half == 0 and i == 1:
                                affine_means(r)
                                move_queries(r, slot)
                            if i == 1 and (half or before):
                                exponential(u - 1, 1 - half)
                            if half and known(r, 0, PAIRS - 3):
                                square_pixels(r + 2, slot, 0, i)
                            if half == 0 and more:
                                square_pixels(r + 1, (slot + 1) % RING, 1, i)
                        if before:
                            turned(u - 2)
                        if more and half == 0:
                            patch_means(r + 1, (slot + 1) % RING)

                def tail():
                    exponential(2 * PAIRS - 1, 1)
                    turned(2 * PAIRS - 2)
                    turned(2 * PAIRS - 1)
                over_pairs(act, first, body, tail)

            @block.tensor
            def _(pe):
                def turn_pixels(r, slot, half, i):
                    step = 8 * r + 4 * half + i
                    if half == 0 and i == 0:
                        loaded(pe, r, slot)
                    wait(pe, squared, 8 * step - 8)
                    pixels = x_pair[slot][:, i, 512 * half:512 * half + 512].rearrange("p (t j) -> p j t", j=4)
                    for j in range(4):
                        last = pe.matmul(x_bank[i % 2][:, j].rearrange("p m c -> p (m c)"), pixels[:, j, :], k.centre[:],
                                         start=True, stop=True)
                    last.then_inc(x_turned, 1)

                def prepare_a(r, slot):
                    pe.wait_ge(feat_done, 2 * r + 2)
                    wait(pe, q_ready, r)
                    for half in range(2):
                        pe.transpose(q_bank[:, P * half:P * half + P], feat_ch[slot % 2][:, half, :], k.ident[:])
                    for half in range(2):
                        last = pe.matmul(q_bank[:, 256 + P * half:256 + P * half + P], feat_ch[slot % 2][:, half, :],
                                         k.centre[:], start=True, stop=True)
                    last.then_inc(feat_turned, 1)

                def prepare_b(r, slot):
                    pe.wait_ge(q_hat_ready, r + 1)
                    for half in range(2):
                        last = pe.transpose(q_bank[:, P * half:P * half + P],
                                            q_hat[:, P * half:P * half + P], k.ident[:])
                    last.then_inc(q_turned, 1)

                def queries(r, slot):
                    pe.wait_ge(q_hatT_ready, r + 1)
                    for half in range(2):
                        last = pe.matmul(q_bank[:, 256 + P * half:256 + P * half + P], q_hatT[:, P * half:P * half + P],
                                         k.w_q[:], start=True, stop=True)
                    last.then_inc(q_mm, 1)

                def project_pixels(u, slot, half, i, banks, weights, done, used):
                    wait(pe, used, 4 * u + i - 1)
                    pixels = x_pair[slot][:, i, 512 * half:512 * half + 512].rearrange("p (t j) -> p j t", j=4)
                    for j in range(4):
                        last = pe.matmul(banks[i % 2][:, j, :], pixels[:, j, :], weights[:], start=True, stop=True)
                    last.then_inc(done, 1)

                def keys(u, slot, half, i):
                    project_pixels(u, slot, half, i, k_bank, k.w_k, k_mm, kq_done)

                def values(u, slot, half, i):
                    project_pixels(u, slot, half, i, v_bank, k.w_v, v_mm, wv_done)

                def turn(u):
                    pe.wait_ge(agg_n_ready, u + 1)
                    wait(pe, h_ready, u)
                    pe.transpose(a_bank[:, 0:P], agg_n[:], k.ident[:]).then_inc(agg_turned, 1)

                def project(u):
                    pe.wait_ge(aggT_ready, u + 1)
                    pe.matmul(a_bank[:, P:2 * P], aggT[:], k.w_proj[:], start=True, stop=True).then_inc(proj_mm, 1)

                def first():
                    for half in range(2):
                        for i in range(4):
                            turn_pixels(0, 0, half, i)
                    prepare_a(0, 0)
                    for i in range(4):
                        turn_pixels(1, 1, 0, i)

                def body(r, slot):
                    more, nxt, prev = known(r, 0, PAIRS - 2), (slot + 1) % RING, (slot - 1) % RING
                    before = known(r, 1, PAIRS)
                    for half in range(2):
                        u = 2 * r + half
                        place = (u - 1, slot, 0) if half else (u - 1, prev, 1)
                        for i in range(4):
                            if half == 0 and i == 1:
                                prepare_b(r, slot)
                            if half and known(r, 0, PAIRS - 3):
                                turn_pixels(r + 2, (slot + 2) % RING, 0, i)
                            if half == 0 and more:
                                turn_pixels(r + 1, nxt, 1, i)
                            if half == 0 and i == 1:
                                queries(r, slot)
                            keys(u, slot, half, i)
                            if half or before:
                                values(*place, i)
                        if before:
                            turn(u - 2)
                        if more and half == 0:
                            prepare_a(r + 1, nxt)
                        if before:
                            project(u - 2)

                def tail():
                    for i in range(4):
                        values(2 * PAIRS - 1, RING - 1, 1, i)
                    for u in (2 * PAIRS - 2, 2 * PAIRS - 1):
                        turn(u)
                        project(u)
                over_pairs(pe, first, body, tail)

            @block.vector
            def _(dve):
                def root_part(r, slot, i):
                    n = [ROOTING * r + (0, 3, 6, 9)[i]]

                    def step(instruction):
                        instruction.then_inc(rooting, 1)
                        n[0] = n[0] + 1
                        dve.wait_ge(rooting, n[0])
                    if i == 0:
                        dve.wait_ge(feat_squared, 4 * r + 4)
                        dve.wait_ge(squared, 64 * r + 64)
                        step(dve.tensor_scalar(var[:], squares[slot % 2][:].rearrange("p g m -> p (g m)"), 1.0 / 64, EPS,
                                               ALU.mult, ALU.add))
                        guess_root(dve, step, var[:], root[:])
                    elif i < NEWTON:
                        step(newton_root(dve, step, var[:], root[:], half_sq[:], root[:]))
                    else:
                        wait(dve, wv_done, 8 * (r - 1))
                        newton_root(dve, step, var[:], root[:], half_sq[:],
                                    rstd[slot % 2][:].rearrange("p g m -> p (g m)")).then_inc(rstd_ready, 1)

                def normalise_means(r, slot):
                    view = "p (g c) -> p g c"
                    dve.wait_ge(rstd_ready, r + 1)
                    wait(dve, q_turned, r)
                    dve.scalar_tensor_tensor(out=q_hat[:].rearrange(view, g=4), in0=q_bank[:, 256:512].rearrange(view, g=4),
                                             scalar=1.0 / 16, in1=spread(rstd[slot % 2][:, 32:34].rearrange("p g m -> p (g m)"), 2, 64),
                                             op0=ALU.mult, op1=ALU.mult).then_inc(q_hat_ready, 1)

                def residual(r, slot):
                    wait(dve, h_ready, 2 * (r - 2) + 2)
                    dve.wait_ge(feat_ready, r + 1)
                    dve.tensor_tensor(feat_c[slot % 2][:].rearrange("p (f m) -> p f m", f=2),
                                      feat[slot % 2][:].rearrange("p (f m) -> p f m", f=2),
                                      spread(k.tok_const[:], 1, 2), ALU.add).then_inc(feat_c_ready, 1)

                def score(u, r, slot, half, i):
                    dve.wait_ge(k_mm, 4 * u + i + 1)
                    dve.tensor_tensor(kq[:, 4 * i:4 * i + 4, :], k_bank[i % 2][:],
                                      spread(q[slot % 2][:, half, :], 1, 4), ALU.mult).then_inc(kq_done, 1)

                def sum_scores(u, half, part):
                    dve.wait_ge(kq_done, 4 * u + 2 * part + 2)
                    if part == 0:
                        wait(dve, exp_ready, u - 1)
                    dve.tensor_reduce(logit[half][:, 128 * part:128 * part + 128],
                                      kq[:, 8 * part:8 * part + 8].rearrange("p n (h d) -> p (n h) d", d=8), AX, ALU.add).then_inc(logits_raw, 1)

                def shift(u, r, slot, par):
                    half = par
                    dve.wait_ge(logits_raw, 2 * u + 2)
                    dve.wait_ge(rstd_ready, r + 1)
                    rs = rstd[slot % 2][:, 16 * half:16 * half + 16].rearrange("p g m -> p (g m)")
                    dve.tensor_tensor(logit[par][:].rearrange("p (a h) -> p a h", h=8),
                                      logit[par][:].rearrange("p (a h) -> p a h", h=8),
                                      spread(rs, 2, 8), ALU.mult).then_inc(logits_ready, 1)
                    dve.wait_ge(logits_ready, u + 1)
                    dve.tensor_reduce(top[:], logit[par][:].rearrange("p (n g) -> p g n", g=16), AX, ALU.max).then_inc(top_ready, 1)
                    dve.wait_ge(top_ready, u + 1)
                    dve.tensor_tensor(logit[par][:].rearrange("p (n g) -> p n g", g=16),
                                      logit[par][:].rearrange("p (n g) -> p n g", g=16),
                                      spread(top[:], 1, 16), ALU.subtract).then_inc(shifted, 1)

                def weights(u, slot, half):
                    dve.wait_ge(exp_ready, u + 1)
                    wait(dve, wv_done, 4 * u)
                    rs = rstd[slot % 2][:, 16 * half:16 * half + 16].rearrange("p g m -> p (g m)")
                    dve.tensor_tensor(weight[:].rearrange("p (a h) -> p a h", h=8),
                                      expo[half][:].rearrange("p (a h) -> p a h", h=8),
                                      spread(rs, 2, 8), ALU.mult).then_inc(weight_ready, 1)
                    dve.tensor_reduce(denom[:], expo[half][:].rearrange("p (n g) -> p g n", g=16), AX, ALU.add).then_inc(denom_ready, 1)
                    dve.wait_ge(denom_ready, u + 1)
                    dve.reciprocal(inv[half][:], denom[:]).then_inc(inv_ready, 1)
                    dve.wait_ge(weight_ready, u + 1)
                    wait(dve, agg_ready, u - 1)

                def weigh(u, half, i):
                    dve.wait_ge(v_mm, 4 * u + i + 1)
                    dve.tensor_tensor(wv[half][:, 4 * i:4 * i + 4, :].rearrange("p n (h d) -> p (n h) d", d=8),
                                      v_bank[i % 2][:].rearrange("p n (h d) -> p (n h) d", d=8),
                                      spread(weight[:, 64 * i:64 * i + 64], 2, 8), ALU.mult).then_inc(wv_done, 1)

                def normalise(u, half):
                    dve.wait_ge(agg_ready, u + 1)
                    dve.wait_ge(inv_ready, u + 1)
                    wait(dve, agg_turned, u)
                    dve.tensor_tensor(agg_n[:].rearrange("p (g d) -> p g d", d=8),
                                      agg[half][:].rearrange("p (g d) -> p g d", d=8),
                                      spread(inv[half][:], 2, 8), ALU.mult).then_inc(agg_n_ready, 1)

                def finish(u, r, slot, half):
                    dve.wait_ge(proj_mm, u + 1)
                    dve.wait_ge(feat_c_ready, r + 1)
                    tokens = k.h_tok[:, bass.ds(2 * r, 2), half, :]
                    dve.tensor_tensor(tokens, a_bank[:, P:2 * P].rearrange("p (m c) -> p m c", m=2),
                                      feat_c[slot % 2][:, P * half:P * half + P].rearrange("p (m c) -> p m c", m=2),
                                      ALU.add).then_inc(h_ready, 1)
                    dve.wait_ge(h_ready, u + 1)
                    dve.bn_stats(k.stats[:, bass.ds(3 * r + half, 1)].rearrange("p g m s -> p (g m s)"),
                                 tokens.rearrange("p m c -> p c m")).then_inc(measured, 1)

                def measure_text(r):
                    dve.bn_stats(k.stats[:, 3 * r + 2].rearrange("p m s -> p (m s)"),
                                 k.h_tok[:, 2 * r:2 * r + 2, 2, :].rearrange("p m c -> p c m")).then_inc(measured, 1)

                def first():
                    for i in range(4):
                        root_part(0, 0, i)
                    normalise_means(0, 0)
                    residual(0, 0)

                def body(r, slot):
                    more, nxt, prev = known(r, 0, PAIRS - 2), (slot + 1) % RING, (slot - 1) % RING
                    before = known(r, 1, PAIRS)
                    for half in range(2):
                        u = 2 * r + half
                        if half or before:
                            weights(u - 1, slot if half else prev, 1 - half)
                        dve.wait_ge(q_ready, r + 1)
                        for i in range(4):
                            score(u, r, slot, half, i)
                            if half or before:
                                weigh(u - 1, 1 - half, i)
                            if before and i == 2:
                                normalise(u - 2, half)
                            if i == 2:
                                sum_scores(u, half, 0)
                            if more and half and i:
                                root_part(r + 1, nxt, i)
                        if more and half:
                            normalise_means(r + 1, nxt)
                        sum_scores(u, half, 1)
                        if more and half == 0:
                            root_part(r + 1, nxt, 0)
                        shift(u, r, slot, half)
                        if before:
                            finish(u - 2, r - 1, prev, half)
                        if more and half:
                            residual(r + 1, nxt)

                def tail():
                    last = PAIRS - 1
                    weights(2 * last + 1, RING - 1, 1)
                    for i in range(4):
                        weigh(2 * last + 1, 1, i)
                    dve.wait_ge(text_loaded, 16)
                    for half in range(2):
                        for r in range(16 * half, 16 * half + 16):
                            measure_text(r)
                        normalise(2 * last + half, half)
                        finish(2 * last + half, last, RING - 1, half)
                over_pairs(dve, first, body, tail)


def normalise_and_turn(nc, tokens, target_of, stores, var_scale, var_add, k, affine):
    ALL, GROUPS, NORMED = 192, 24, 4
    apart = 3 if affine else 1
    chunks, banks = ALL // GROUPS, GROUPS // 8
    with ExitStack() as stack:
        t = Memory(nc, stack, "attn_" if affine else "ffn_")
        var, root, half_sq, rstd, mean = (t.sb(n, [P, ALL]) for n in ("var", "root", "half_sq", "rstd", "mean"))
        normed = [t.sb(f"normed{i}", [P, GROUPS, 64]) for i in range(NORMED)]
        split = [t.sb(f"split{i}", [P, GROUPS, 2, 64], F16) for i in range(2)]
        bank = [t.ps(f"turn{i}", [P, 8, P], F16) for i in range(2 * banks)]
        expert_bank = [t.ps(f"expert_bank{i}", [P, 4, P]) for i in range(2)]
        expert_turned, expert_moved = t.sem("expert_turned"), t.sem("expert_moved")
        stored, rooting, rstd_ready = t.sem("stored"), t.sem("rooting"), t.sem("rstd_ready")
        centred, centred_even = t.sem("centred"), t.sem("centred_even")
        scaled, weighted, norm_ready = t.sem("scaled"), t.sem("weighted"), t.sem("norm_ready")
        hi_ready, split_ready, turned, moved = t.sem("hi_ready"), t.sem("split_ready"), t.sem("turned"), t.sem("moved")

        def over_chunks(eng, body, tail=None):
            for c in range(NORMED):
                body(c, c)
            with eng.Fori(1, chunks // NORMED) as g:
                for c in range(NORMED):
                    body(NORMED * g + c, c)
            if tail:
                tail()

        def started(n):
            return not isinstance(n, int) or n >= 0

        def centre(eng, n, slot, semaphore, step):
            wait(eng, split_ready, n - NORMED + 1)
            eng.tensor_tensor(normed[slot][:], tokens[:, bass.ds(n * GROUPS, GROUPS), :],
                              mean[:, bass.ds(n * GROUPS, GROUPS)].unsqueeze(2).to_broadcast([P, GROUPS, 64]),
                              ALU.subtract).then_inc(semaphore, step)

        with nc.Block() as block:
            @block.sync
            def _(sp):
                for dst, src in stores:
                    sp.dma_start(dst, src).then_inc(stored, 16)
                sp.wait_ge(stored, 16 * len(stores))

            @block.vector
            def _(dve):
                count = [0]

                def step(instruction):
                    instruction.then_inc(rooting, 1)
                    count[0] += 1
                    dve.wait_ge(rooting, count[0])
                by_group = "p (g j) m s -> p g m j s"
                measured = k.stats[:].rearrange(by_group, j=apart)
                order = "p (g m j) -> p g m j"
                for j in range(apart):
                    step(dve.tensor_copy(mean[:].rearrange(order, m=2, j=apart)[:, :, :, j], measured[:, :, :, j, 1]))
                for j in range(apart):
                    step(dve.tensor_scalar(var[:].rearrange(order, m=2, j=apart)[:, :, :, j], measured[:, :, :, j, 2],
                                           var_scale, var_add, ALU.mult, ALU.add))
                guess_root(dve, step, var[:], root[:])
                for _ in range(NEWTON - 1):
                    step(newton_root(dve, step, var[:], root[:], half_sq[:], root[:]))
                newton_root(dve, step, var[:], root[:], half_sq[:], rstd[:]).then_inc(rstd_ready, 1)
                dve.wait_ge(rstd_ready, 1)
                def normalise(n, slot):
                    z = normed[slot]
                    if affine and slot % 2 == 0:
                        centre(dve, n, slot, centred_even, 2)
                        dve.wait_ge(centred_even, n + 2)
                    else:
                        dve.wait_ge(centred, n + 1)
                    dve.tensor_tensor(z[:], z[:], rstd[:, bass.ds(n * GROUPS, GROUPS)].unsqueeze(2).to_broadcast([P, GROUPS, 64]),
                                      ALU.mult).then_inc(scaled if affine else norm_ready, 1)
                    if affine:
                        dve.wait_ge(scaled, n + 1)
                        dve.tensor_tensor(z[:], z[:], spread(k.gamma_row[:], 1, GROUPS), ALU.mult).then_inc(weighted, 1)

                def second_part(n, slot):
                    dve.wait_ge(hi_ready, n + 1)
                    dve.tensor_tensor(split[slot % 2][:, :, 1, :], normed[slot][:], split[slot % 2][:, :, 0, :],
                                      ALU.subtract).then_inc(split_ready, 1)

                def body(n, slot):
                    normalise(n, slot)
                    if started(n - 1):
                        second_part(n - 1, (slot - 1) % NORMED)
                over_chunks(dve, body, lambda: second_part(chunks - 1, NORMED - 1))

            @block.gpsimd
            def _(pool):
                def body(n, slot):
                    if not affine:
                        centre(pool, n, slot, centred, 1)
                        return
                    if slot % 2 == 0:
                        centre(pool, n + 1, slot + 1, centred, 2)
                    pool.wait_ge(weighted, n + 1)
                    pool.tensor_tensor(normed[slot][:], normed[slot][:], spread(k.beta_row[:], 1, GROUPS),
                                       ALU.add).then_inc(norm_ready, 1)
                pool.wait_ge(rooting, apart)
                over_chunks(pool, body)

            @block.tensor
            def _(pe):
                def body(n, slot):
                    pe.wait_ge(split_ready, n + 1)
                    for a in range(banks):
                        wait(pe, moved, banks * (n - 2) + a + 1)
                        for i in range(8):
                            last = pe.transpose(bank[slot % 2 * banks + a][:, i, :],
                                                split[slot % 2][:, 8 * a + i].rearrange("p s c -> p (s c)"), k.ident16[:])
                        last.then_inc(turned, 1)
                if not affine:
                    for a in range(8):
                        wait(pe, expert_moved, a - 1)
                        for i in range(4):
                            last = pe.transpose(expert_bank[a % 2][:, i], k.w_exp[:, 4 * a + i, 0:P], k.ident[:])
                        last.then_inc(expert_turned, 1)
                over_chunks(pe, body)

            @block.scalar
            def _(act):
                if not affine:
                    for a in range(8):
                        act.wait_ge(expert_turned, a + 1)
                        act.activation(k.w_exp[:, 4 * a:4 * a + 4, 0:P], expert_bank[a % 2][:], ACT.Copy).then_inc(expert_moved, 1)

                def first_part(n, slot):
                    act.wait_ge(norm_ready, n + 1)
                    wait(act, turned, banks * (n - 1))
                    act.activation(split[slot % 2][:, :, 0, :], normed[slot][:], ACT.Copy).then_inc(hi_ready, 1)

                def move(n, slot):
                    for a in range(banks):
                        act.wait_ge(turned, banks * n + a + 1)
                        act.activation(target_of(n, a), bank[slot % 2 * banks + a][:], ACT.Copy).then_inc(moved, 1)

                def body(n, slot):
                    first_part(n, slot)
                    if started(n - 1):
                        move(n - 1, (slot - 1) % NORMED)
                over_chunks(act, body, lambda: move(chunks - 1, NORMED - 1))


def tied_scores(nc, zT, h_half, h_source, k):
    with ExitStack() as stack:
        t = Memory(nc, stack)
        qk = [t.sb(f"qk{i}", [P, 2, 2, 64, 32]) for i in range(2)]
        score, top, denom, inv = t.sb("score", [P, 4, 64]), t.sb("stop", [P, 4]), t.sb("sdenom", [P, 4]), t.sb("sinv", [P, 4])
        att2 = t.sb("att2", [P, 4, 64, 2])
        bank = [t.ps(f"qk_bank{i}", [P, 4, 2, 2, 32]) for i in range(4)]
        s_bank = t.ps("score_bank", [P, 4, 2, 64])
        t_bank = [t.ps(f"att_bank{i}", [P, 512]) for i in range(2)]
        projected, moved_a, moved_v, summed = t.sem("projected"), t.sem("moved_a"), t.sem("moved_v"), t.sem("summed")
        vec, exp_ready, att_turned, att_used = t.sem("vec"), t.sem("exp_ready"), t.sem("att_turned"), t.sem("att_used")
        h_loaded, joined = t.sem("h_loaded"), t.sem("joined")
        UNITS = [(g, j) for g in range(4) for j in range(3)]

        def move(eng, u, a, done, op):
            eng.wait_ge(projected, 16 * u + a + 1)
            wait(eng, summed, u - 1)
            for kind in range(2):
                last = op(qk[u % 2][:, kind, :, 4 * a:4 * a + 4, :],
                          bank[a % 4][:, :, kind].rearrange("p s h c -> p h s c"))
            last.then_inc(done, 1)

        with nc.Block() as block:
            @block.sync
            def _(sp):
                sp.dma_start(h_half, h_source).then_inc(h_loaded, 16)
                sp.wait_ge(h_loaded, 16)

            @block.gpsimd
            def _(pool):
                for n in range(2):
                    pool.tensor_tensor(k.w_shared[:, n, :], k.w_shared[:, n, :], k.ident[:], ALU.add).then_inc(joined, 1)
                pool.wait_ge(joined, 2)
                pool.wait_ge(k.experts_loaded, 16)
                for n in range(2):
                    experts = k.w_exp[:, 16 * n:16 * n + 16, 0:P]
                    pool.tensor_tensor(experts, experts, spread(k.w_shared[:, n, :], 1, 16), ALU.add).then_inc(joined, 1)

            @block.tensor
            def _(pe):
                def project(u, g, j):
                    for s in range(64):
                        a = s // 4
                        if s % 4 == 0:
                            n = 16 * u + a - 4
                            wait(pe, moved_a if a % 2 == 0 else moved_v, n // 2 + 1 if n >= 0 else 0)
                        for part in range(2):
                            last = pe.matmul(bank[a % 4][:, s % 4].rearrange("p k h c -> p (k h c)"),
                                             zT[:, s, P * j:P * j + P], k.w_qk[:, part, P * g:P * g + P],
                                             start=(part == 0), stop=(part == 1))
                        if s % 4 == 3:
                            last.then_inc(projected, 1)

                def score_sums(u, g, j):
                    pe.wait_ge(moved_a, 8 * u + 8)
                    pe.wait_ge(moved_v, 8 * u + 8)
                    q = qk[u % 2][:].rearrange("p k h s c -> p k (h s) c")
                    for c in range(32):
                        last = pe.matmul(s_bank[:, g].rearrange("p h t -> p (h t)"), q[:, 0, :, c], q[:, 1, :, c],
                                         start=(j == 0 and c == 0), stop=(j == 2 and c == 31))
                    last.then_inc(summed, 1)
                for u, (g, j) in enumerate(UNITS):
                    project(u, g, j)
                    if u:
                        score_sums(u - 1, *UNITS[u - 1])
                score_sums(len(UNITS) - 1, *UNITS[-1])
                pe.wait_ge(vec, 6)
                for g in range(4):
                    wait(pe, att_used, g - 1)
                    pe.transpose(t_bank[g % 2][:, 0:P], att2[:, g].rearrange("p t a -> p (t a)"), k.ident[:]).then_inc(att_turned, 1)

            @block.scalar
            def _(act):
                for u in range(len(UNITS)):
                    for a in range(0, 16, 2):
                        move(act, u, a, moved_a, lambda o, i: act.activation(o, i, ACT.Copy, scale=1.0 / 64))
                act.wait_ge(vec, 3)
                act.activation(score[:], score[:], ACT.Exp).then_inc(exp_ready, 1)

            @block.vector
            def _(dve):
                for u in range(len(UNITS)):
                    for a in range(1, 16, 2):
                        move(dve, u, a, moved_v, lambda o, i: dve.tensor_scalar(o, i, 1.0 / 64, None, ALU.mult))
                dve.wait_ge(summed, len(UNITS))
                scale = 32 ** -0.5 * 384 ** -0.5
                for h in range(2):
                    last = dve.tensor_scalar(score[64 * h:64 * h + 64], s_bank[64 * h:64 * h + 64, :, h, :], scale, None, ALU.mult)
                last.then_inc(vec, 1)
                dve.wait_ge(vec, 1)
                dve.tensor_reduce(top[:], score[:], AX, ALU.max).then_inc(vec, 1)
                dve.wait_ge(vec, 2)
                dve.tensor_tensor(score[:], score[:], spread(top[:], 2, 64), ALU.subtract).then_inc(vec, 1)
                dve.wait_ge(exp_ready, 1)
                dve.tensor_reduce(denom[:], score[:], AX, ALU.add).then_inc(vec, 1)
                dve.wait_ge(vec, 4)
                dve.reciprocal(inv[:], denom[:]).then_inc(vec, 1)
                dve.wait_ge(vec, 5)
                for a in range(2):
                    last = dve.tensor_tensor(att2[:, :, :, a], score[:], spread(inv[:], 2, 64), ALU.mult)
                last.then_inc(vec, 1)
                for g in range(4):
                    dve.wait_ge(att_turned, g + 1)
                    for h in range(2):
                        last = dve.tensor_tensor(k.att_blocks[:, 2 * g + h].rearrange("p (s a) -> p s a", a=2),
                                                 spread(t_bank[g % 2][:, 64 * h:64 * h + 64], 2, 2),
                                                 spread(k.parity[:], 1, 64), ALU.mult)
                    last.then_inc(att_used, 1)


def tied_output(nc, zT, h_half, k):
    CH, CHUNKS, PEEL, LAG = 8, 24, 4, 3
    with ExitStack() as stack:
        t = Memory(nc, stack)
        v = [t.sb(f"v{i}", [P, CH, 256]) for i in range(2)]
        gate = [t.sb(f"gate{i}", [P, CH, 256]) for i in range(2)]
        gated = [t.sb(f"gated{i}", [P, CH, 256]) for i in range(2)]
        gatedT = [t.sb(f"gatedT{i}", [P, 4, P]) for i in range(2)]
        v_bank = [t.ps(f"value_bank{i}", [P, 2, 256]) for i in range(2)]
        g_bank = [t.ps(f"gate_bank{i}", [P, 2, 256]) for i in range(2)]
        o_bank = [t.ps(f"o_bank{i}", [P, 2, CH, 32]) for i in range(2)]
        t_bank, r_bank = t.ps("gt_bank", [P, 4, P]), t.ps("r_bank", [P, CH, 64])
        v_mm, g_mm, v_ready = t.sem("v_mm"), t.sem("g_mm"), t.sem("v_ready")
        gate_raw, gate_ready = t.sem("gate_raw"), t.sem("gate_ready")
        mixed, gated_ready, turned, moved = t.sem("mixed"), t.sem("gated_ready"), t.sem("turned"), t.sem("moved")
        out_mm, added, biased, measured = t.sem("out_mm"), t.sem("added"), t.sem("biased"), t.sem("measured")

        def over_chunks(eng, body):
            for n in range(PEEL):
                body(n, n % 2)
            with eng.Fori(PEEL // 2, CHUNKS // 2) as g:
                for n in range(2):
                    body(2 * g + n, n)
            for n in range(CHUNKS, CHUNKS + LAG):
                body(n, n % 2)

        def inside(n):
            return not isinstance(n, int) or 0 <= n < CHUNKS

        zcols = zT[:].rearrange("p b l -> p (b l)").rearrange("p (t l) -> p l t", l=192)
        with nc.Block() as block:
            @block.gpsimd
            def _(pool):
                pool.tensor_tensor(h_half, h_half, spread(k.attn_bo_row[:], 1, 192), ALU.add).then_inc(biased, 1)

            @block.tensor
            def _(pe):
                def project(n, a):
                    for kind, (banks, used, done) in enumerate(((v_bank, v_ready, v_mm), (g_bank, gate_raw, g_mm))):
                        wait(pe, used, 4 * n + a - 1)
                        for i in range(2):
                            for part in range(2):
                                last = pe.matmul(banks[a % 2][:, i], zcols[:, n * CH + 2 * a + i, :],
                                                 k.w_vg[:, part, 256 * kind:256 * kind + 256],
                                                 start=(part == 0), stop=(part == 1))
                        last.then_inc(done, 1)

                def mix(n, par, a):
                    pe.wait_ge(v_ready, 4 * n + 4)
                    wait(pe, gated_ready, 4 * n + a - 1)
                    for h in range(2):
                        head = 2 * a + h
                        last = pe.matmul(o_bank[a % 2][:, h], k.att_blocks[:, head],
                                         v[par][:, :, 32 * head:32 * head + 32], start=True, stop=True)
                    last.then_inc(mixed, 1)

                def turn(n, par, a):
                    pe.wait_ge(gated_ready, 4 * n + 4)
                    wait(pe, moved, 4 * n + a)
                    for i in range(2):
                        for half in range(2):
                            last = pe.transpose(t_bank[:, 2 * i + half],
                                                gated[par][:, 2 * a + i, P * half:P * half + P], k.ident[:])
                    last.then_inc(turned, 1)

                def output(n, a):
                    pe.wait_ge(moved, 4 * n + a + 1)
                    if a == 0:
                        wait(pe, added, n)
                    for i in range(2):
                        for half in range(2):
                            last = pe.matmul(r_bank[:, 2 * a + i], gatedT[a % 2][:, 2 * i + half], k.attn_wo[:, half],
                                             start=(half == 0), stop=(half == 1))
                    last.then_inc(out_mm, 1)

                def body(n, par):
                    for a in range(4):
                        if inside(n):
                            project(n, a)
                        if a == 0 and inside(n - 3):
                            output(n - 3, 3)
                        if a > 0 and inside(n - 2):
                            output(n - 2, a - 1)
                        if inside(n - 2):
                            turn(n - 2, par, a)
                        if inside(n - 1):
                            mix(n - 1, 1 - par, a)
                over_chunks(pe, body)

            @block.scalar
            def _(act):
                def values(n, par, a):
                    act.wait_ge(v_mm, 4 * n + a + 1)
                    wait(act, mixed, 4 * (n - 2) + 4)
                    act.activation(v[par][:, 2 * a:2 * a + 2], v_bank[a % 2][:], ACT.Copy, scale=1.0 / 64).then_inc(v_ready, 1)

                def open_gates(n, par, a):
                    act.wait_ge(gate_raw, 4 * n + a + 1)
                    g = gate[par][:, 2 * a:2 * a + 2]
                    act.activation(g, g, ACT.Sigmoid).then_inc(gate_ready, 1)

                def move(n, a):
                    act.wait_ge(turned, 4 * n + a + 1)
                    wait(act, out_mm, 4 * n + a - 1)
                    act.activation(gatedT[a % 2][:], t_bank[:], ACT.Copy).then_inc(moved, 1)

                def body(n, par):
                    for a in range(4):
                        if inside(n):
                            values(n, par, a)
                        if inside(n - 2):
                            move(n - 2, a)
                        if inside(n):
                            open_gates(n, par, a)
                over_chunks(act, body)

            @block.vector
            def _(dve):
                def bias_gates(n, par, a):
                    dve.wait_ge(g_mm, 4 * n + a + 1)
                    wait(dve, gated_ready, 4 * (n - 2) + 4)
                    dve.scalar_tensor_tensor(out=gate[par][:, 2 * a:2 * a + 2], in0=g_bank[a % 2][:], scalar=1.0 / 64,
                                             in1=spread(k.bg_row[:], 1, 2), op0=ALU.mult, op1=ALU.add).then_inc(gate_raw, 1)

                def multiply(n, par, a):
                    dve.wait_ge(gate_ready, 4 * n + 4)
                    wait(dve, turned, 4 * (n - 2) + 4)
                    dve.wait_ge(mixed, 4 * n + a + 1)
                    view = "p i (h c) -> p h i c"
                    dve.tensor_tensor(gated[par][:, :, 64 * a:64 * a + 64].rearrange(view, h=2), o_bank[a % 2][:],
                                      gate[par][:, :, 64 * a:64 * a + 64].rearrange(view, h=2), ALU.mult).then_inc(gated_ready, 1)

                def add(n):
                    dve.wait_ge(out_mm, 4 * n + 4)
                    dve.wait_ge(biased, 1)
                    dve.tensor_tensor(h_half[:, bass.ds(n * CH, CH), :], h_half[:, bass.ds(n * CH, CH), :], r_bank[:],
                                      ALU.add).then_inc(added, 1)

                def measure(n, i):
                    dve.wait_ge(added, n + 1)
                    dve.bn_stats(k.stats[:, bass.ds(n * (CH // 2) + i, 1)].rearrange("p g m s -> p (g m s)"),
                                 h_half[:, bass.ds(n * CH + 2 * i, 2), :].rearrange("p m c -> p c m")).then_inc(measured, 1)

                def body(n, par):
                    for a in range(4):
                        if inside(n):
                            bias_gates(n, par, a)
                        if a == 0 and inside(n - 3):
                            add(n - 3)
                        if inside(n - 1):
                            multiply(n - 1, 1 - par, a)
                        if inside(n - 3):
                            measure(n - 3, a)
                over_chunks(dve, body)


def feed_forward(nc, zT, h_dram, out, k):
    B, L, RING = 64, 384, 4
    with ExitStack() as stack:
        t = Memory(nc, stack)
        w_sel = [t.sb(f"w_sel{i}", [P, 2, P + 1]) for i in range(RING)]
        hid = [[t.sb(f"hid{n}_{i}", [P, L]) for i in range(2)] for n in range(3)]
        res = [t.sb(f"res{i}", [P, 3, 64]) for i in range(RING)]
        final = [t.sb(f"final{i}", [P, 3, 64]) for i in range(RING)]
        bank = [[t.ps(f"ff_bank{n}_{i}", [P, 512]) for i in range(2)] for n in range(4)]
        selected, res_ready = t.sem("selected"), [t.sem(f"res_ready{i}") for i in range(RING)]
        mm = [t.sem(f"mm{n}") for n in range(4)]
        relu = [t.sem(f"relu{n}") for n in range(3)]
        res_biased, final_ready, stored = t.sem("res_biased"), t.sem("final_ready"), [t.sem(f"stored{i}") for i in range(RING)]

        def count(semaphore_step, b, slot):
            if isinstance(b, int):
                return semaphore_step * (b // RING + 1)
            return (b - slot) * (semaphore_step // RING) + semaphore_step

        def over_rows(eng, body, skew):
            for s in range(2 * RING):
                body(s, s % RING)
            with eng.Fori(2, B // RING) as g:
                for s in range(RING):
                    body(g * RING + s, s)
            for s in range(skew):
                body(B + s, s)

        def inside(b):
            return not isinstance(b, int) or 0 <= b < B

        with nc.Block() as block:
            @block.gpsimd
            def _(pool):
                experts = k.w_exp[:].rearrange("p (l e) c -> p l e c", l=2)

                def body(b, slot):
                    wait(pool, relu[2], b - RING + 1)
                    e = pool.value_load(k.route[0:1, bass.ds(b, 1)], min_val=0, max_val=15)
                    pool.tensor_copy(w_sel[slot][:].unsqueeze(2), experts[:, :, bass.ds(e, 1), :]).then_inc(selected, 1)
                over_rows(pool, body, 0)

            @block.sync
            def _(sp):
                def store(b, slot):
                    wait(sp, final_ready, b + 1)
                    sp.dma_start(out[b].rearrange("(j p) c -> p j c", p=P), final[slot][:]).then_inc(stored[slot], 16)

                def body(b, slot):
                    if inside(b):
                        wait(sp, final_ready, b - RING + 1)
                        sp.dma_start(res[slot][:], h_dram[b].rearrange("(j p) c -> p j c", p=P)).then_inc(res_ready[slot], 16)
                    if inside(b - 3):
                        store(b - 3, (slot - 3) % RING)
                over_rows(sp, body, 3)
                for s in range(RING):
                    sp.wait_ge(stored[s], 16 * (B // RING))

            @block.tensor
            def _(pe):
                def layer(n, b, slot):
                    par = slot % 2
                    dst = bank[n][par]
                    if n < 3:
                        wait(pe, relu[n], b - 1)
                    else:
                        wait(pe, final_ready, b - 1)
                    if n == 0:
                        tokens = zT.rearrange("p l (b a) -> p b a l", a=2)[:, bass.ds(b, 1)]
                        for part, weights in enumerate((k.wi_hi, k.wi_lo)):
                            last = pe.matmul(dst[:, 0:L].rearrange("p (o a l) -> p o a l", o=1, a=2), weights[:], tokens,
                                             start=(part == 0), stop=(part == 1))
                    elif n < 3:
                        pe.wait_ge(relu[n - 1], b + 1)
                        pe.wait_ge(selected, b + 1)
                        last = pe.matmul(dst[:, 0:L], w_sel[slot][:, n - 1, 0:P], hid[n - 1][par][:], start=True, stop=True)
                    else:
                        pe.wait_ge(relu[2], b + 1)
                        for j in range(3):
                            last = pe.matmul(dst[:, 64 * j:64 * j + 64], hid[2][par][:, P * j:P * j + P], k.ffn_wo[:],
                                             start=True, stop=True)
                    last.then_inc(mm[n], 1)

                def body(b, slot):
                    for n in (3, 2, 1, 0):
                        if inside(b - n):
                            layer(n, b - n, (slot - n) % RING)
                over_rows(pe, body, 3)

            @block.scalar
            def _(act):
                def relu_of(n, b, slot):
                    par = slot % 2
                    act.wait_ge(mm[n], b + 1)
                    wait(act, mm[n + 1], b - 1)
                    bias = k.bi[:, 0:1] if n == 0 else w_sel[slot][:, n - 1, P:P + 1]
                    act.activation(hid[n][par][:], bank[n][par][:, 0:L], ACT.Relu, bias=bias,
                                   scale=1.0 / 64 if n == 0 else 1.0).then_inc(relu[n], 1)

                def body(b, slot):
                    for n in (2, 0):
                        if inside(b - n):
                            relu_of(n, b - n, (slot - n) % RING)
                over_rows(act, body, 2)

            @block.vector
            def _(dve):
                def hidden(b, slot):
                    par = slot % 2
                    dve.wait_ge(mm[1], b + 1)
                    wait(dve, mm[2], b - 1)
                    dve.tensor_scalar(hid[1][par][:], bank[1][par][:, 0:L], w_sel[slot][:, 0, P:P + 1], 0.0,
                                      ALU.add, ALU.max).then_inc(relu[1], 1)

                def finish(b, slot):
                    dve.wait_ge(res_ready[slot], count(16, b, slot))
                    dve.tensor_tensor(res[slot][:], res[slot][:], spread(k.ffn_bo_row[:], 1, 3), ALU.add).then_inc(res_biased, 1)
                    dve.wait_ge(res_biased, b + 1)
                    dve.wait_ge(mm[3], b + 1)
                    if inside(b - RING):
                        dve.wait_ge(stored[slot], count(16, b, slot) - 16)
                    dve.tensor_tensor(final[slot][:], bank[3][slot % 2][:, 0:192].rearrange("p (j c) -> p j c", j=3),
                                      res[slot][:], ALU.add).then_inc(final_ready, 1)

                def body(b, slot):
                    for n, step in ((3, finish), (1, hidden)):
                        if inside(b - n):
                            step(b - n, (slot - n) % RING)
                over_rows(dve, body, 3)


class Kept:

    def __init__(self, m):
        sb = m.sb
        self.ident, self.ident16, self.parity = sb("ident", [P, P]), sb("ident16", [P, P], F16), sb("parity", [P, 2])
        self.centre = sb("centre", [P, P])
        self.w_k, self.w_v, self.w_q, self.w_proj = (sb(n, [P, P]) for n in ("w_k", "w_v", "w_q", "w_proj"))
        self.lnq_w, self.lnq_b, self.bi = sb("lnq_w", [P, 1]), sb("lnq_b", [P, 1]), sb("bi", [P, 1])
        self.tok_const = sb("tok_const", [P, P])
        self.gamma_row, self.beta_row = sb("gamma_row", [P, 64]), sb("beta_row", [P, 64])
        self.attn_bo_row, self.ffn_bo_row = sb("attn_bo_row", [P, 64]), sb("ffn_bo_row", [P, 64])
        self.bg_row, self.attn_wo = sb("bg_row", [P, 256]), sb("attn_wo", [P, 2, 64])
        self.w_qk, self.w_vg = sb("w_qk", [P, 2, 512], F16), sb("w_vg", [P, 2, 512], F16)
        self.wi_hi, self.wi_lo, self.ffn_wo = sb("wi_hi", [P, P], F16), sb("wi_lo", [P, P], F16), sb("ffn_wo", [P, 64])
        self.w_exp = sb("w_exp", [P, 32, P + 1])
        self.stats = sb("stats", [P, 96, 2, 3])
        self.w_shared, self.experts_loaded = sb("w_shared", [P, 2, P]), m.sem("experts_loaded")
        self.route = sb("route", [1, 64], I32)


def early_fusion(nc, x, w, out):
    B, L, C = 64, 384, 64
    h_dram = nc.dram_tensor("h_scratch", (B, L, C), F32, kind="Internal").ap()
    h2_dram = nc.dram_tensor("h2_scratch", (B, L, C), F32, kind="Internal").ap()
    halves = "b (a l) c -> (b a) l c"
    with ExitStack() as outer:
        m = Memory(nc, outer)
        k = Kept(m)
        tokens_buffer = m.sb("tokens_buffer", [P, B * L * C // P])
        k.h_tok = tokens_buffer[:].rearrange("p (b j c) -> p b j c", j=3, c=C)
        h_half = tokens_buffer[:].rearrange("p (l c) -> p l c", c=C)
        with ExitStack() as early:
            t = Memory(nc, early)
            k.x_pair = [t.sb(f"x_pair{i}", [P, 4, 1024]) for i in range(RING)]
            k.x_loaded = [t.sem(f"x_loaded{i}") for i in range(RING)]
            setup_weights(nc, x, w, k)
            local_attention(nc, x, w, k)
        zT = m.sb("zT", [P, B, L], F16)
        k.att_blocks = m.sb("att_blocks", [P, 8, P])
        tokens = k.h_tok.rearrange("p b j c -> p (b j) c")
        columns = zT[:].rearrange("p b (j t) -> p (b j) t", j=3)
        stores = [(h_dram[:, P * j:P * j + P, :].rearrange("b t c -> t b c"), k.h_tok[:, :, j, :]) for j in range(3)]
        normalise_and_turn(nc, tokens, lambda n, a: columns[:, bass.ds(n * 24 + 8 * a, 8), :],
                           stores, (1 + EPS) / C, EPS * EPS, k, True)
        tied_scores(nc, zT, h_half, h_dram.rearrange(halves, a=2), k)
        tied_output(nc, zT, h_half, k)
        z2 = zT[:].rearrange("p b l -> p (b l)").rearrange("p (l t) -> p l t", t=P)
        normalise_and_turn(nc, h_half, lambda n, a: z2[:, bass.ds(n * 24 + 8 * a, 8), :],
                           [(h2_dram.rearrange(halves, a=2), h_half)], 1.0 / C, EPS, k, False)
        feed_forward(nc, z2, h2_dram, out, k)


_OUT = (64, 384, 64)


def kernel(**inputs):
    from concourse import bacc
    from concourse.bass_utils import run_bass_kernel_spmd

    nc = bacc.Bacc("TRN2", target_bir_lowering=False, num_devices=1)
    arrays, weights = {}, {}
    for name, value in inputs.items():
        a = np.ascontiguousarray(value)
        arrays[f"in_{name}"] = a
        ap = nc.dram_tensor(f"in_{name}", a.shape, mybir.dt.from_np(a.dtype), kind="ExternalInput").ap()
        weights[name[3:] if name.startswith("L0_") else name] = ap
    out = nc.dram_tensor("out", _OUT, F32, kind="ExternalOutput").ap()
    x = weights.pop("x")
    early_fusion(nc, x, weights, out)
    return run_bass_kernel_spmd(nc, [arrays], core_ids=[0]).results[0]["out"]
```
